# Optimizing a Trainium2 kernel written in Bass

```python
import numpy as np
import jax
import jax.numpy as jnp

def _softmax(x, axis=-1):
    return jax.nn.softmax(x, axis=axis)

def _gelu(x):
    return jax.nn.gelu(x, approximate=True)

def _silu(x):
    return jax.nn.silu(x)

def _sigmoid(x):
    return jax.nn.sigmoid(x)

def _layernorm(x, axis=-1, eps=1e-05):
    m = jnp.mean(x, axis=axis, keepdims=True)
    v = jnp.var(x, axis=axis, keepdims=True)
    return (x - m) / jnp.sqrt(v + eps)

def _scatter_add(tgt, idx, src, axis=0):
    return tgt.at[idx].add(src)

def _segment_sum(src, seg, n):
    return jax.ops.segment_sum(src, seg, n)
kernel_name = 'mk_seq_postln_d2_jaxref_r4_021953'

def setup_inputs(seed: int=0):
    np.random.seed(seed)
    _w = jnp.asarray

    def _L0_attn_setup():
        import jax, jax.numpy as jnp
        import numpy as np
        EPS = 1e-05
        CHUNK = 128

        def lightning_attn(q, k, v, ld, chunk=CHUNK):
            b, n, h, d = q.shape
            nc = n // chunk
            idx = jnp.arange(chunk)
            diff = idx[:, None] - idx[None, :]
            mask = diff >= 0
            D = jnp.exp(ld[:, None, None] * jnp.where(mask, diff, 0)) * mask
            q_decay = jnp.exp(ld[None, :] * (idx + 1)[:, None])
            k_decay = jnp.exp(ld[None, :] * (chunk - 1 - idx)[:, None])
            chunk_decay = jnp.exp(ld * chunk)
            qc = jnp.moveaxis(q.reshape(b, nc, chunk, h, d), 1, 0)
            kc = jnp.moveaxis(k.reshape(b, nc, chunk, h, d), 1, 0)
            vc = jnp.moveaxis(v.reshape(b, nc, chunk, h, d), 1, 0)

            def step(S, inp):
                qb, kb, vb = inp
                scores = jnp.einsum('bchd,bshd->bhcs', qb, kb) * D[None]
                o_intra = jnp.einsum('bhcs,bshd->bchd', scores, vb)
                o_inter = jnp.einsum('bchd,bhde->bche', qb, S) * q_decay[None, :, :, None]
                S_new = chunk_decay[None, :, None, None] * S + jnp.einsum('bshd,bshe->bhde', kb * k_decay[None, :, :, None], vb)
                return (S_new, o_intra + o_inter)
            S0 = jnp.zeros((b, h, d, d), dtype=q.dtype)
            S_final, oc = jax.lax.scan(step, S0, (qc, kc, vc))
            out = jnp.moveaxis(oc, 0, 1).reshape(b, n, h, d)
            return (out, S_final)

        def group_rmsnorm_fused_gate(o, gate, w, num_heads):
            b, n, d = o.shape
            hd = d // num_heads
            o = o * jax.nn.sigmoid(gate)
            og = o.reshape(b, n, num_heads, hd)
            og = og * jax.lax.rsqrt(jnp.mean(og * og, axis=-1, keepdims=True) + EPS)
            return og.reshape(b, n, d) * w
        key = jax.random.key(seed)
        ks = jax.random.split(key, 10)
        B, N, D, H = (2, 1024, 512, 16)
        HD = D // H
        s = 1.0 / np.sqrt(D)
        x = jax.random.normal(ks[0], (B, N, D), dtype=jnp.float32)
        log_decay = -jax.random.uniform(ks[1], (H,), dtype=jnp.float32, minval=0.01, maxval=1.0)
        Wq = jax.random.normal(ks[2], (D, D), dtype=jnp.float32) * s
        Wk = jax.random.normal(ks[3], (D, D), dtype=jnp.float32) * s
        Wv = jax.random.normal(ks[4], (D, D), dtype=jnp.float32) * s
        Wo = jax.random.normal(ks[5], (D, D), dtype=jnp.float32) * s
        Wg1 = jax.random.normal(ks[6], (D, HD), dtype=jnp.float32) * s
        Wg2 = jax.random.normal(ks[7], (HD, D), dtype=jnp.float32) / np.sqrt(HD)
        norm_w = jnp.ones((D,), dtype=jnp.float32)
        return {'x': x, 'log_decay': log_decay, 'Wq': Wq, 'Wk': Wk, 'Wv': Wv, 'Wo': Wo, 'Wg1': Wg1, 'Wg2': Wg2, 'norm_w': norm_w}
    _L0_attn_in = _L0_attn_setup()

    def _L0_ffn_setup():
        import jax, jax.numpy as jnp
        import numpy as np
        B, S, D, H = (4, 512, 512, 2048)

        def fwht(x):
            orig_shape = x.shape
            n = orig_shape[-1]
            x = x.reshape(-1, n)
            h = 1
            while h < n:
                xb = x.reshape(-1, n // (2 * h), 2, h)
                a = xb[:, :, 0, :]
                b = xb[:, :, 1, :]
                x = jnp.stack([a + b, a - b], axis=2).reshape(-1, n)
                h *= 2
            scale = jnp.asarray(1.0 / np.sqrt(n), dtype=x.dtype)
            return (x * scale).reshape(orig_shape)
        key = jax.random.key(seed)
        kx, k1, k2, k3 = jax.random.split(key, 4)
        x = jax.random.normal(kx, (B, S, D), dtype=jnp.float32)
        W1 = jax.random.normal(k1, (H, D), dtype=jnp.float32) * (1.0 / np.sqrt(D))
        W2 = jax.random.normal(k2, (D, H), dtype=jnp.float32) * (1.0 / np.sqrt(H))
        W3 = jax.random.normal(k3, (H, D), dtype=jnp.float32) * (1.0 / np.sqrt(D))
        return {'x': x, 'W1': W1, 'W2': W2, 'W3': W3}
    _L0_ffn_in = _L0_ffn_setup()

    def _L1_attn_setup():
        import jax, jax.numpy as jnp
        import numpy as np
        DIM = 512
        DT_RANK = 64
        DIM_INNER = 512
        D_STATE = 32
        B_SZ = 4
        L = 512

        def _selective_scan(u, delta, A, Bm, Cm, D_param):

            def step(h, inp):
                delta_t, B_t, C_t, u_t = inp
                dA = jnp.exp(delta_t[:, :, None] * A[None])
                dBu = (delta_t * u_t)[:, :, None] * B_t[:, None, :]
                h = dA * h + dBu
                y_t = jnp.einsum('bdn,bn->bd', h, C_t)
                return (h, y_t)
            b = u.shape[0]
            h0 = jnp.zeros((b, A.shape[0], A.shape[1]), dtype=u.dtype)
            xs = (jnp.moveaxis(delta, 1, 0), jnp.moveaxis(Bm, 1, 0), jnp.moveaxis(Cm, 1, 0), jnp.moveaxis(u, 1, 0))
            _, ys = jax.lax.scan(step, h0, xs)
            y = jnp.moveaxis(ys, 0, 1)
            return y + u * D_param[None, None, :]
        key = jax.random.key(seed)
        ks = jax.random.split(key, 6)
        x = jax.random.normal(ks[0], (B_SZ, L, DIM), dtype=jnp.float32)
        z = jax.random.normal(ks[1], (B_SZ, L, DIM_INNER), dtype=jnp.float32)
        W_bc = jax.random.normal(ks[2], (DT_RANK + 2 * D_STATE, DIM), dtype=jnp.float32) * DIM ** (-0.5)
        W_dt = jax.random.normal(ks[3], (DIM_INNER, DT_RANK), dtype=jnp.float32) * DT_RANK ** (-0.5)
        b_dt = jax.random.normal(ks[4], (DIM_INNER,), dtype=jnp.float32) * 0.1
        A_log = jnp.log(jnp.tile(jnp.arange(1, D_STATE + 1, dtype=jnp.float32), (DIM_INNER, 1)))
        D_param = jnp.ones((DIM_INNER,), dtype=jnp.float32)
        return {'x': x, 'z': z, 'W_bc': W_bc, 'W_dt': W_dt, 'b_dt': b_dt, 'A_log': A_log, 'D_param': D_param}
    _L1_attn_in = _L1_attn_setup()

    def _L1_ffn_setup():
        import jax, jax.numpy as jnp
        import numpy as np
        HIDDEN = 512
        INTER = 2048
        BATCH, LOCAL_SEQ = (2, 1024)
        key = jax.random.key(seed)
        k1, k2, k3 = jax.random.split(key, 3)
        h_shard = jax.random.normal(k1, (BATCH, LOCAL_SEQ, HIDDEN), dtype=jnp.float32)
        w_gate_up = jax.random.normal(k2, (2 * INTER, HIDDEN), dtype=jnp.float32) * 0.02
        w_down = jax.random.normal(k3, (HIDDEN, INTER), dtype=jnp.float32) * 0.02
        return {'h_shard': h_shard, 'w_gate_up': w_gate_up, 'w_down': w_down}
    _L1_ffn_in = _L1_ffn_setup()
    _d = {'L0_attn_x': _L0_attn_in['x'], 'L0_attn_log_decay': _L0_attn_in['log_decay'], 'L0_attn_Wq': _L0_attn_in['Wq'], 'L0_attn_Wk': _L0_attn_in['Wk'], 'L0_attn_Wv': _L0_attn_in['Wv'], 'L0_attn_Wo': _L0_attn_in['Wo'], 'L0_attn_Wg1': _L0_attn_in['Wg1'], 'L0_attn_Wg2': _L0_attn_in['Wg2'], 'L0_attn_norm_w': _L0_attn_in['norm_w'], 'L0_ffn_W1': _L0_ffn_in['W1'], 'L0_ffn_W2': _L0_ffn_in['W2'], 'L0_ffn_W3': _L0_ffn_in['W3'], 'L1_attn_z': _L1_attn_in['z'], 'L1_attn_W_bc': _L1_attn_in['W_bc'], 'L1_attn_W_dt': _L1_attn_in['W_dt'], 'L1_attn_b_dt': _L1_attn_in['b_dt'], 'L1_attn_A_log': _L1_attn_in['A_log'], 'L1_attn_D_param': _L1_attn_in['D_param'], 'L1_ffn_w_gate_up': _L1_ffn_in['w_gate_up'], 'L1_ffn_w_down': _L1_ffn_in['w_down']}
    _x0 = _d['L0_attn_x']
    _d['L0_attn_x'] = jax.random.normal(jax.random.fold_in(jax.random.key(seed), 1), (2, 1024, 512), dtype=_x0.dtype)
    del _x0
    return _d

def reference(L0_attn_x, L0_attn_log_decay, L0_attn_Wq, L0_attn_Wk, L0_attn_Wv, L0_attn_Wo, L0_attn_Wg1, L0_attn_Wg2, L0_attn_norm_w, L0_ffn_W1, L0_ffn_W2, L0_ffn_W3, L1_attn_z, L1_attn_W_bc, L1_attn_W_dt, L1_attn_b_dt, L1_attn_A_log, L1_attn_D_param, L1_ffn_w_gate_up, L1_ffn_w_down):

    def _L0_attn_ref(x, log_decay, Wq, Wk, Wv, Wo, Wg1, Wg2, norm_w):
        import jax, jax.numpy as jnp
        import numpy as np
        EPS = 1e-05
        CHUNK = 128

        def lightning_attn(q, k, v, ld, chunk=CHUNK):
            b, n, h, d = q.shape
            nc = n // chunk
            idx = jnp.arange(chunk)
            diff = idx[:, None] - idx[None, :]
            mask = diff >= 0
            D = jnp.exp(ld[:, None, None] * jnp.where(mask, diff, 0)) * mask
            q_decay = jnp.exp(ld[None, :] * (idx + 1)[:, None])
            k_decay = jnp.exp(ld[None, :] * (chunk - 1 - idx)[:, None])
            chunk_decay = jnp.exp(ld * chunk)
            qc = jnp.moveaxis(q.reshape(b, nc, chunk, h, d), 1, 0)
            kc = jnp.moveaxis(k.reshape(b, nc, chunk, h, d), 1, 0)
            vc = jnp.moveaxis(v.reshape(b, nc, chunk, h, d), 1, 0)

            def step(S, inp):
                qb, kb, vb = inp
                scores = jnp.einsum('bchd,bshd->bhcs', qb, kb) * D[None]
                o_intra = jnp.einsum('bhcs,bshd->bchd', scores, vb)
                o_inter = jnp.einsum('bchd,bhde->bche', qb, S) * q_decay[None, :, :, None]
                S_new = chunk_decay[None, :, None, None] * S + jnp.einsum('bshd,bshe->bhde', kb * k_decay[None, :, :, None], vb)
                return (S_new, o_intra + o_inter)
            S0 = jnp.zeros((b, h, d, d), dtype=q.dtype)
            S_final, oc = jax.lax.scan(step, S0, (qc, kc, vc))
            out = jnp.moveaxis(oc, 0, 1).reshape(b, n, h, d)
            return (out, S_final)

        def group_rmsnorm_fused_gate(o, gate, w, num_heads):
            b, n, d = o.shape
            hd = d // num_heads
            o = o * jax.nn.sigmoid(gate)
            og = o.reshape(b, n, num_heads, hd)
            og = og * jax.lax.rsqrt(jnp.mean(og * og, axis=-1, keepdims=True) + EPS)
            return og.reshape(b, n, d) * w
        b, n, d = x.shape
        H = log_decay.shape[0]
        hd = d // H
        q = jax.nn.silu(jnp.einsum('bnd,de->bne', x, Wq).reshape(b, n, H, hd))
        k = jax.nn.silu(jnp.einsum('bnd,de->bne', x, Wk).reshape(b, n, H, hd))
        v = jax.nn.silu(jnp.einsum('bnd,de->bne', x, Wv).reshape(b, n, H, hd))
        o, _ = lightning_attn(q, k, v, log_decay)
        o = o.reshape(b, n, d)
        gate = jnp.einsum('bnk,kd->bnd', jnp.einsum('bnd,dk->bnk', x, Wg1), Wg2)
        o = group_rmsnorm_fused_gate(o, gate, norm_w, H)
        return jnp.einsum('bnd,de->bne', o, Wo)

    def _L0_ffn_ref(x, W1, W2, W3):
        import jax, jax.numpy as jnp
        import numpy as np
        B, S, D, H = (4, 512, 512, 2048)

        def fwht(x):
            orig_shape = x.shape
            n = orig_shape[-1]
            x = x.reshape(-1, n)
            h = 1
            while h < n:
                xb = x.reshape(-1, n // (2 * h), 2, h)
                a = xb[:, :, 0, :]
                b = xb[:, :, 1, :]
                x = jnp.stack([a + b, a - b], axis=2).reshape(-1, n)
                h *= 2
            scale = jnp.asarray(1.0 / np.sqrt(n), dtype=x.dtype)
            return (x * scale).reshape(orig_shape)
        up_gate = jnp.einsum('bsd,hd->bsh', x, W1)
        up_lin = jnp.einsum('bsd,hd->bsh', x, W3)
        hidden = jax.nn.silu(up_gate) * up_lin
        hidden = fwht(hidden)
        out = jnp.einsum('bsh,dh->bsd', hidden, W2)
        return out

    def _L1_attn_ref(x, z, W_bc, W_dt, b_dt, A_log, D_param):
        import jax, jax.numpy as jnp
        import numpy as np
        DIM = 512
        DT_RANK = 64
        DIM_INNER = 512
        D_STATE = 32
        B_SZ = 4
        L = 512

        def _selective_scan(u, delta, A, Bm, Cm, D_param):

            def step(h, inp):
                delta_t, B_t, C_t, u_t = inp
                dA = jnp.exp(delta_t[:, :, None] * A[None])
                dBu = (delta_t * u_t)[:, :, None] * B_t[:, None, :]
                h = dA * h + dBu
                y_t = jnp.einsum('bdn,bn->bd', h, C_t)
                return (h, y_t)
            b = u.shape[0]
            h0 = jnp.zeros((b, A.shape[0], A.shape[1]), dtype=u.dtype)
            xs = (jnp.moveaxis(delta, 1, 0), jnp.moveaxis(Bm, 1, 0), jnp.moveaxis(Cm, 1, 0), jnp.moveaxis(u, 1, 0))
            _, ys = jax.lax.scan(step, h0, xs)
            y = jnp.moveaxis(ys, 0, 1)
            return y + u * D_param[None, None, :]
        A = -jnp.exp(A_log)
        deltaBC = jnp.einsum('bld,od->blo', x, W_bc)
        dt_r = deltaBC[..., :DT_RANK]
        Bm = deltaBC[..., DT_RANK:DT_RANK + D_STATE]
        Cm = deltaBC[..., DT_RANK + D_STATE:]
        dt = jnp.einsum('blr,dr->bld', dt_r, W_dt)
        delta = jax.nn.softplus(dt + b_dt[None, None, :])
        y = _selective_scan(x, delta, A, Bm, Cm, D_param)
        return y

    def _L1_ffn_ref(h_shard, w_gate_up, w_down):
        import jax, jax.numpy as jnp
        import numpy as np
        HIDDEN = 512
        INTER = 2048
        BATCH, LOCAL_SEQ = (2, 1024)
        batch, local_seq, hidden = h_shard.shape
        gate_up = jnp.einsum('bsh,oh->bso', h_shard, w_gate_up)
        gate, up = jnp.split(gate_up, 2, axis=-1)
        h = jax.nn.silu(gate) * up
        out = jnp.einsum('bsi,hi->bsh', h, w_down)
        return out
    x = L0_attn_x
    x = _layernorm(x + _L0_attn_ref(x, L0_attn_log_decay, L0_attn_Wq, L0_attn_Wk, L0_attn_Wv, L0_attn_Wo, L0_attn_Wg1, L0_attn_Wg2, L0_attn_norm_w), axis=-1)
    x = _layernorm(x + _L0_ffn_ref(x, L0_ffn_W1, L0_ffn_W2, L0_ffn_W3), axis=-1)
    x = _layernorm(x + _L1_attn_ref(x, L1_attn_z, L1_attn_W_bc, L1_attn_W_dt, L1_attn_b_dt, L1_attn_A_log, L1_attn_D_param), axis=-1)
    x = _layernorm(x + _L1_ffn_ref(x, L1_ffn_w_gate_up, L1_ffn_w_down), axis=-1)
    return x

_drawn_inputs = setup_inputs


def setup_inputs(seed=0):
    import zlib

    import numpy as np

    out = dict(_drawn_inputs(seed))
    spreads = {'L0_attn_norm_w': (1.0, 0.2), 'L1_attn_D_param': (1.0, 0.2)}
    factors = {}
    for name, (base, spread) in spreads.items():
        noise = np.random.default_rng([zlib.crc32(name.encode()), seed]).standard_normal(out[name].shape)
        drawn = base * np.exp(spread * noise) if base else spread * noise
        out[name] = jnp.asarray(drawn.astype(out[name].dtype))
    for name, factor in factors.items():
        out[name] = (out[name] * factor).astype(out[name].dtype)
    return out
```

```python
from contextlib import ExitStack

import concourse.bass as bass
from concourse import mybir

F32 = mybir.dt.float32
F32R = mybir.dt.float32r
BF16 = mybir.dt.bfloat16
ALU = mybir.AluOpType
ACT = mybir.ActivationFunctionType

P = 128
D = 512
KD = D // P
BATCH, SEQ = 2, 1024
TOK = BATCH * SEQ
TT = 512
NT = TOK // TT
TILES_PER_SEQ = SEQ // TT
HID = 2048
NH, HD = 16, 32
HPT = P // HD
CH = 128
CPT = TT // CH
NS = 32
RK = 64
EPS = 1e-5
GW = 256
NG = HID // GW
HC = GW // P

C_ID, C_MEAN, C_HEAD, C_HAD, C_DIFF, C_MASK, C_POS, C_BD = (i * P for i in range(8))
C_REV = 8 * P
C_M1, C_M2, C_EPS = C_REV + 1, C_REV + 2, C_REV + 3
CW = C_EPS + 1


def bcast(ap, shape):
    return ap.to_broadcast(shape)


class Prog:

    def __init__(self, nc, ctx):
        self.nc, self.ctx = nc, ctx

    def sb(self, name, shape, dt=F32):
        return self.ctx.enter_context(self.nc.sbuf_tensor(name, shape, dt))

    def ps(self, name, shape, dt=F32):
        return self.ctx.enter_context(self.nc.psum_tensor(name, shape, dt))

    def sem(self, name):
        return self.nc.alloc_semaphore(name)


def three_passes(pe, out, w_hi, w_lo, x_hi, x_lo, first, last):
    pe.matmul(out, w_hi, x_hi, start=first, stop=False)
    pe.matmul(out, w_hi, x_lo, start=False, stop=False)
    return pe.matmul(out, w_lo, x_hi, start=False, stop=last)


def hadamard_phase(nc, const, w2n, aw_hi, aw_lo, w2h, cn, aw, x_dram, x, s_x):
    NC = HID // P
    STAGES = NC.bit_length() - 1
    with ExitStack() as ctx:
        p = Prog(nc, ctx)
        a = p.sb("had_a", [P, NC, D])
        b = p.sb("had_b", [P, NC, D])
        aw_raw = p.sb("attn_w_raw", [P, 1, KD, D])
        acc = p.ps("had_acc", [P, 4, D])
        bufs = [a, b]
        s_const, s_w2, s_aw = p.sem("const_in"), p.sem("w2_in"), p.sem("attn_w_in")
        s_stage = p.sem("had_stage_done")
        s_mm = p.sem("had_product_done")
        s_ev = p.sem("had_scaled")
        s_hi, s_lo = p.sem("attn_w_hi"), p.sem("attn_w_lo")
        s_out = p.sem("w2h_stored")
        last = bufs[STAGES % 2]
        other = bufs[(STAGES + 1) % 2]
        with nc.Block() as block:
            @block.sync
            def _(sp):
                sp.dma_start(a[:, :, :], w2n).then_inc(s_w2, 16)
                sp.dma_start(const[:, :], cn).then_inc(s_const, 16)
                for t in range(NT):
                    sp.dma_start(x[:, :, t * TT:(t + 1) * TT], x_dram[:, :, t * TT:(t + 1) * TT]).then_inc(s_x[t], 16)
                for i in range(4):
                    sp.wait_ge(s_lo, i)
                    sp.dma_start(aw_raw[:, 0], aw[i]).then_inc(s_aw, 16)
                for c in range(0, NC, 4):
                    sp.wait_ge(s_ev, c + 4)
                    sp.dma_start(w2h[:, c:c + 4, :], other[:, c:c + 4, :]).then_inc(s_out, 16)
                sp.wait_ge(s_out, 16 * (NC // 4))

            @block.vector
            def _(dve):
                dve.wait_ge(s_w2, 16)
                for s in range(STAGES):
                    h = 1 << s
                    src = bufs[s % 2][:, :, :].rearrange("p (g two h) d -> p g two (h d)", two=2, h=h)
                    dst = bufs[(s + 1) % 2][:, :, :].rearrange("p (g two h) d -> p g two (h d)", two=2, h=h)
                    if s:
                        dve.wait_ge(s_stage, 2 * s)
                    dve.tensor_tensor(dst[:, :, 0], src[:, :, 0], src[:, :, 1], ALU.add).then_inc(s_stage, 1)
                    dve.tensor_tensor(dst[:, :, 1], src[:, :, 0], src[:, :, 1], ALU.subtract).then_inc(s_stage, 1)

            @block.tensor
            def _(pe):
                pe.wait_ge(s_stage, 2 * STAGES)
                pe.wait_ge(s_const, 16)
                for c in range(NC):
                    if c >= 4:
                        pe.wait_ge(s_ev, c - 3)
                    pe.matmul(acc[:, c % 4], const[:, C_HAD:C_HAD + P], last[:, c, :]).then_inc(s_mm, 1)

            @block.scalar
            def _(act):
                for i in range(4):
                    act.wait_ge(s_aw, 16 * (i + 1))
                    act.copy(aw_hi[:, i], aw_raw[:, 0]).then_inc(s_hi, 1)
                for c in range(NC):
                    act.wait_ge(s_mm, c + 1)
                    act.mul(other[:, c, :], acc[:, c % 4], float(HID) ** -0.5).then_inc(s_ev, 1)

            @block.gpsimd
            def _(pool):
                for i in range(4):
                    pool.wait_ge(s_hi, i + 1)
                    pool.tensor_tensor(aw_lo[:, i], aw_raw[:, 0], aw_hi[:, i].bitcast(F32), ALU.subtract)\
                        .then_inc(s_lo, 1)


def attention_phase(nc, const, x, s_x, aw_hi, aw_lo, ld_tok, ld_feat, ld_cols, wg1_d, wg2_d, nw_d):
    with ExitStack() as ctx:
        p = Prog(nc, ctx)
        small = p.sb("attn_small", [P, NH + KD + KD + 1])
        ldt, ldf, nw = small[:, 0:NH], small[:, NH:NH + KD], small[:, NH + KD:NH + 2 * KD]
        wg1 = p.sb("wg1", [P, KD, HD])
        wg2 = p.sb("wg2", [HD, D])
        dmask = p.sb("decay_st", [P, HPT, KD, CH])
        qdec = p.sb("q_decay", [P, KD, CH])
        kdec = p.sb("k_decay", [P, D])
        cdec = p.sb("chunk_decay", [P, KD])
        xh = p.sb("attn_x_hi", [P, KD, TT], F32R)
        xl = p.sb("attn_x_lo", [P, KD, TT], F32R)
        qT = p.sb("qT", [P, KD, TT])
        kT = p.sb("kT", [P, KD, TT])
        v = p.sb("v", [P, CPT, D])
        kd = p.sb("k_decayed", [P, CPT, D])
        qd = p.sb("q_decayed", [P, KD, TT])
        sig = p.sb("gate_sigmoid", [P, KD, TT])
        pr = p.sb("probs", [P, HPT, KD, CH])
        og = p.sb("o_gated", [P, KD, TT])
        g1 = p.sb("g1", [HD, TT])
        st = p.sb("state", [P, KD, CH])
        um = p.sb("state_update", [P, KD, CH])
        sd = p.sb("head_rms", [P, 2, TT])
        sq = pr[:, :, :, :].rearrange("p a b c -> p a (b c)")
        on = qd

        scores = p.ps("scores", [P, HPT, KD, CH])
        o_ps = p.ps("o_ps", [P, KD, CH])
        u_ps = p.ps("u_ps", [P, KD, CH])
        proj = p.ps("proj", [P, 2, TT])
        g1_ps = o_ps[0:HD, :, :].rearrange("p m c -> p (m c)")

        s_sm = p.sem("attn_small_in")
        s_dexp, s_dm = p.sem("decay_exp"), p.sem("decay_masked")
        s_xh, s_xl = p.sem("attn_xh"), p.sem("attn_xl")
        s_pj = p.sem("proj_done")
        s_at, s_dt = p.sem("proj_taken_by_act"), p.sem("proj_taken_by_dve")
        s_g1p, s_g1 = p.sem("g1_product"), p.sem("g1_ready")
        s_qd = p.sem("qd_ready")
        s_sc, s_pr = p.sem("scores_done"), p.sem("probs_ready")
        s_o, s_og = p.sem("o_done"), p.sem("og_ready")
        s_u, s_um, s_us, s_st = (p.sem(n) for n in ("update_done", "update_masked", "state_scaled", "state_ready"))
        s_sq, s_sd, s_rs, s_on = (p.sem(n) for n in ("squares", "head_sd", "head_rstd", "on_ready"))
        s_oh, s_ol = p.sem("on_hi"), p.sem("on_lo")

        items = ["q"] * KD + ["k"] * KD + ["v"] * CPT + ["gate"] * KD + ["kT"] * CPT + ["norm"] * KD + ["wo"] * KD
        by_dve = [n in ("kT", "wo") for n in items]
        PJ, PJ_D = len(items), sum(by_dve)
        PJ_A = PJ - PJ_D
        assert PJ % 2 == 0
        at = {n: items.index(n) for n in items}
        TPS = TILES_PER_SEQ

        def taken(i, t):
            if by_dve[i]:
                return s_dt, PJ_D * t + sum(by_dve[:i + 1]) + 2
            return s_at, PJ_A * t + i + 1 - sum(by_dve[:i + 1])

        with nc.Block() as block:
            @block.sync
            def _(sp):
                sp.dma_start(ldt, ld_tok).then_inc(s_sm, 16)
                sp.dma_start(ldf, ld_feat).then_inc(s_sm, 16)
                sp.dma_start(nw, nw_d).then_inc(s_sm, 16)
                sp.dma_start(kdec[:, :], ld_cols).then_inc(s_sm, 16)
                sp.dma_start(wg1[:, :, :], wg1_d).then_inc(s_sm, 16)
                sp.dma_start(wg2[:, :], wg2_d).then_inc(s_sm, 16)

            @block.tensor
            def _(pe):
                pe.wait_ge(s_sm, 96)

                def tile(b, u):
                    t = b * TPS + u

                    def bank(i):
                        if i < 2:
                            pe.wait_ge(s_dt, PJ_D * t + i + 1)
                        else:
                            pe.wait_ge(*taken(i - 2, t))
                        return proj[:, i % 2]

                    def project(name, w, m):
                        out = bank(at[name] + m)
                        for k in range(KD):
                            mm = three_passes(pe, out, aw_hi[:, w, k, m * P:(m + 1) * P],
                                              aw_lo[:, w, k, m * P:(m + 1) * P],
                                              xh[:, k, :], xl[:, k, :], k == 0, k == KD - 1)
                        mm.then_inc(s_pj, 1)

                    pe.wait_ge(s_xl, t + 1)
                    for m in range(KD):
                        project("q", 0, m)
                    for m in range(KD):
                        project("k", 1, m)
                    for c in range(CPT):
                        out = bank(at["v"] + c)
                        cs = slice(c * CH, (c + 1) * CH)
                        for k in range(KD):
                            mm = three_passes(pe, out, xh[:, k, cs], xl[:, k, cs],
                                              aw_hi[:, 2, k, :], aw_lo[:, 2, k, :], k == 0, k == KD - 1)
                        mm.then_inc(s_pj, 1)
                    pe.wait_ge(s_og, CPT * t)
                    for k in range(KD):
                        mm = pe.matmul(g1_ps, wg1[:, k, :], x[:, k, bass.ts(t, TT)],
                                       start=(k == 0), stop=(k == KD - 1))
                    mm.then_inc(s_g1p, 1)
                    pe.wait_ge(s_g1, t + 1)
                    for m in range(KD):
                        out = bank(at["gate"] + m)
                        pe.matmul(out, wg2[:, m * P:(m + 1) * P], g1[:, :]).then_inc(s_pj, 1)
                    pe.wait_ge(*taken(at["v"] + CPT - 1, t))
                    for c in range(CPT):
                        out = bank(at["kT"] + c)
                        for m in range(KD):
                            mm = pe.transpose(out[:, m * P:(m + 1) * P], kT[:, m, c * CH:(c + 1) * CH],
                                              const[:, C_ID:C_ID + P])
                        mm.then_inc(s_pj, 1)
                    for c in range(CPT):
                        n = CPT * t + c
                        cs = slice(c * CH, (c + 1) * CH)
                        for j in range(HPT):
                            r = slice(j * HD, (j + 1) * HD)
                            pe.wait_ge(s_pr, HPT * n)
                            for m in range(KD):
                                mm = pe.matmul(scores[:, j, m, :], kT[r, m, cs], qT[r, m, cs])
                            mm.then_inc(s_sc, 1)
                        pe.wait_ge(s_st, n + b + 1)
                        pe.wait_ge(s_qd, t + 1)
                        pe.wait_ge(s_og, n)
                        for m in range(KD):
                            pe.matmul(o_ps[:, m, :], st[:, m, :], qd[:, m, cs],
                                      start=(m == 0), stop=(m == KD - 1), skip_group_check=True)
                        pe.wait_ge(*taken(at["kT"] + c, t))
                        pe.wait_ge(s_um, n)
                        for m in range(KD):
                            mm = pe.matmul(u_ps[:, m, :], kd[:, c, m * P:(m + 1) * P], v[:, c, m * P:(m + 1) * P])
                        mm.then_inc(s_u, 1)
                        for j in range(HPT):
                            pe.wait_ge(s_pr, HPT * n + j + 1)
                            for m in range(KD):
                                h = m * HPT + j
                                mm = pe.matmul(o_ps[j * HD:(j + 1) * HD, m, :], v[:, c, h * HD:(h + 1) * HD],
                                               pr[:, j, m, :], start=False, stop=True, skip_group_check=True,
                                               tile_position=(0, j * HD))
                        mm.then_inc(s_o, 1)
                    pe.wait_ge(s_sq, t + 1)
                    for m in range(KD):
                        out = bank(at["norm"] + m)
                        pe.matmul(out, const[:, C_HEAD:C_HEAD + P], sq[:, m, :]).then_inc(s_pj, 1)
                    pe.wait_ge(s_ol, t + 1)
                    for m in range(KD):
                        project("wo", 3, m)

                with pe.Fori(0, BATCH) as b:
                    with pe.Fori(0, TPS) as u:
                        tile(b, u)

            @block.scalar
            def _(act):
                act.wait_ge(s_sm, 96)
                for j in range(HPT):
                    for m in range(KD):
                        h = m * HPT + j
                        act.activation(dmask[:, j, m, :], const[:, C_DIFF:C_DIFF + P], ACT.Exp,
                                       scale=ldt[:, h:h + 1]).then_inc(s_dexp, 1)
                for m in range(KD):
                    act.activation(qdec[:, m, :], const[:, C_POS:C_POS + P], ACT.Exp,
                                   scale=ldf[:, m:m + 1]).then_inc(s_dexp, 1)
                act.activation(kdec[:, :], kdec[:, :], ACT.Exp,
                               scale=const[:, C_REV:C_REV + 1]).then_inc(s_dexp, 1)
                act.activation(cdec[:, :], ldf, ACT.Exp, scale=float(CH)).then_inc(s_dexp, 1)
                for t in range(NT):
                    act.wait_ge(s_x[t], 16)
                with act.Fori(0, NT) as t:
                    act.wait_ge(s_dt, PJ_D * t + 2)
                    act.copy(xh[:, :, :], x[:, :, bass.ts(t, TT)]).then_inc(s_xh, 1)

                    def take(name, out, f):
                        i = at[name]
                        for m in range(KD):
                            act.wait_ge(s_pj, PJ * t + i + m + 1)
                            act.activation(out[:, m, :], proj[:, (i + m) % 2], f).then_inc(s_at, 1)

                    take("q", qT, ACT.Silu)
                    take("k", kT, ACT.Silu)
                    take("v", v, ACT.Silu)
                    act.wait_ge(s_g1p, t + 1)
                    act.copy(g1[:, :], g1_ps).then_inc(s_g1, 1)
                    take("gate", sig, ACT.Sigmoid)
                    act.wait_ge(s_og, CPT * t + CPT)
                    act.activation(sq[:, :, :], og[:, :, :], ACT.Square).then_inc(s_sq, 1)
                    for m in range(KD):
                        act.wait_ge(s_pj, PJ * t + at["norm"] + m + 1)
                        if m >= 2:
                            act.wait_ge(s_on, KD * t + m - 1)
                        act.activation(sd[:, m % 2], proj[:, (at["norm"] + m) % 2], ACT.Sqrt,
                                       bias=const[:, C_EPS:C_EPS + 1]).then_inc(s_at, 1)
                    act.wait_ge(s_on, KD * t + KD)
                    act.copy(xh[:, :, :], on[:, :, :]).then_inc(s_oh, 1)

            @block.vector
            def _(dve):
                dve.sem_inc(s_dt, 2)
                dve.wait_ge(s_dexp, HPT * KD + KD + 2)
                dve.tensor_tensor(dmask[:, :, :, :].rearrange("p a b c -> p (a b) c"),
                                  dmask[:, :, :, :].rearrange("p a b c -> p (a b) c"),
                                  const[:, C_MASK:C_MASK + P].unsqueeze(1).to_broadcast([P, NH, CH]),
                                  ALU.mult).then_inc(s_dm, 1)
                dve.wait_ge(s_dm, 1)

                def tile(b, u):
                    t = b * TPS + u
                    dve.wait_ge(s_st, CPT * t + b + 1)
                    dve.wait_ge(s_xh, t + 1)
                    dve.tensor_tensor(xl[:, :, :], x[:, :, bass.ts(t, TT)], xh[:, :, :].bitcast(F32),
                                      ALU.subtract).then_inc(s_xl, 1)
                    dve.wait_ge(*taken(at["q"] + KD - 1, t))
                    dve.tensor_tensor(qd[:, :, :].rearrange("p m (c i) -> p m c i", c=CPT),
                                      qT[:, :, :].rearrange("p m (c i) -> p m c i", c=CPT),
                                      qdec[:, :, :].unsqueeze(2).to_broadcast([P, KD, CPT, CH]),
                                      ALU.mult).then_inc(s_qd, 1)
                    for c in range(CPT):
                        dve.wait_ge(s_pj, PJ * t + at["kT"] + c + 1)
                        dve.tensor_tensor(kd[:, c, :], proj[:, (at["kT"] + c) % 2], kdec[:, :], ALU.mult)\
                           .then_inc(s_dt, 1)
                    for c in range(CPT):
                        n = CPT * t + c
                        for j in range(HPT):
                            dve.wait_ge(s_sc, HPT * n + j + 1)
                            dve.tensor_tensor(pr[:, j], scores[:, j], dmask[:, j], ALU.mult).then_inc(s_pr, 1)
                        dve.wait_ge(s_u, n + 1)
                        dve.tensor_tensor(um[:, :, :], u_ps[:, :, :],
                                          const[:, C_BD:C_BD + P].unsqueeze(1).to_broadcast([P, KD, CH]),
                                          ALU.mult).then_inc(s_um, 1)
                        dve.tensor_tensor(st[:, :, :], st[:, :, :],
                                          cdec[:, :].unsqueeze(2).to_broadcast([P, KD, CH]),
                                          ALU.mult).then_inc(s_us, 1)
                        dve.wait_ge(s_um, n + 1)
                        dve.wait_ge(s_us, n + 1)
                        dve.tensor_tensor(st[:, :, :], st[:, :, :], um[:, :, :], ALU.add).then_inc(s_st, 1)
                        dve.wait_ge(s_o, n + 1)
                        dve.wait_ge(*taken(at["gate"] + KD - 1, t))
                        dve.tensor_tensor(og[:, :, c * CH:(c + 1) * CH], o_ps[:, :, :],
                                          sig[:, :, c * CH:(c + 1) * CH], ALU.mult).then_inc(s_og, 1)
                        dve.wait_ge(s_st, n + b + 2)
                    for m in range(KD):
                        dve.wait_ge(*taken(at["norm"] + m, t))
                        dve.reciprocal(sd[:, m % 2], sd[:, m % 2]).then_inc(s_rs, 1)
                        dve.wait_ge(s_rs, KD * t + m + 1)
                        dve.wait_ge(s_og, CPT * t + CPT)
                        dve.scalar_tensor_tensor(out=on[:, m, :], in0=og[:, m, :], scalar=nw[:, m:m + 1],
                                                 in1=sd[:, m % 2], op0=ALU.mult, op1=ALU.mult).then_inc(s_on, 1)
                    dve.wait_ge(s_oh, t + 1)
                    dve.tensor_tensor(xl[:, :, :], on[:, :, :], xh[:, :, :].bitcast(F32),
                                      ALU.subtract).then_inc(s_ol, 1)
                    for m in range(KD):
                        i = at["wo"] + m
                        dve.wait_ge(s_pj, PJ * t + i + 1)
                        dve.tensor_tensor(x[:, m, bass.ts(t, TT)], x[:, m, bass.ts(t, TT)], proj[:, i % 2],
                                          ALU.add).then_inc(s_dt, 1)

                with dve.Fori(0, BATCH) as b:
                    dve.wait_ge(s_st, (SEQ // CH + 1) * b)
                    dve.memset(st[:, :, :], 0.0).then_inc(s_st, 1)
                    with dve.Fori(0, TPS) as u:
                        tile(b, u)


def layernorm_phase(nc, const, tag, x, xh=None, xl=None, out=None):
    with ExitStack() as ctx:
        p = Prog(nc, ctx)
        xc = p.sb(f"{tag}_centred", [P, 2, KD, TT])
        sq = p.sb(f"{tag}_squares", [P, 2, KD, TT])
        sd = p.sb(f"{tag}_sd", [P, 2, TT])
        mean = p.ps(f"{tag}_mean", [P, 2, TT])
        var = p.ps(f"{tag}_var", [P, 2, TT])
        s_m, s_c, s_q, s_v, s_s, s_r, s_x, s_h, s_l, s_o = (p.sem(f"{tag}_{n}") for n in (
            "mean", "centred", "squares", "var", "sd", "rstd", "x", "hi", "lo", "stored"))
        with nc.Block() as block:
            def tiles(eng, stages):
                with eng.Fori(0, NT // 2) as i:
                    for stage in stages:
                        for s in range(2):
                            stage(2 * i + s, s, 2 * i)

            @block.tensor
            def _(pe):
                def means(t, s, done):
                    pe.wait_ge(s_c, done)
                    for k in range(KD):
                        mm = pe.matmul(mean[:, s], const[:, C_MEAN:C_MEAN + P], x[:, k, bass.ts(t, TT)],
                                       start=(k == 0), stop=(k == KD - 1))
                    mm.then_inc(s_m, 1)

                def variances(t, s, done):
                    pe.wait_ge(s_q, t + 1)
                    pe.wait_ge(s_s, done)
                    for k in range(KD):
                        mm = pe.matmul(var[:, s], const[:, C_MEAN:C_MEAN + P], sq[:, s, k, :],
                                       start=(k == 0), stop=(k == KD - 1))
                    mm.then_inc(s_v, 1)
                tiles(pe, [means, variances])

            @block.vector
            def _(dve):
                def centre(t, s, done):
                    dve.wait_ge(s_m, t + 1)
                    dve.wait_ge(s_x, done)
                    dve.wait_ge(s_q, done)
                    dve.tensor_tensor(xc[:, s], x[:, :, bass.ts(t, TT)],
                                      mean[:, s].unsqueeze(1).to_broadcast([P, KD, TT]),
                                      ALU.subtract).then_inc(s_c, 1)

                def scale(t, s, done):
                    dve.wait_ge(s_s, t + 1)
                    dve.reciprocal(sd[:, s], sd[:, s]).then_inc(s_r, 1)
                    dve.wait_ge(s_r, t + 1)
                    dve.tensor_tensor(x[:, :, bass.ts(t, TT)], xc[:, s],
                                      sd[:, s].unsqueeze(1).to_broadcast([P, KD, TT]), ALU.mult).then_inc(s_x, 1)
                tiles(dve, [centre, scale])

            @block.scalar
            def _(act):
                def square(t, s, done):
                    act.wait_ge(s_c, t + 1)
                    act.wait_ge(s_v, done)
                    act.activation(sq[:, s], xc[:, s], ACT.Square).then_inc(s_q, 1)

                def root(t, s, done):
                    act.wait_ge(s_v, t + 1)
                    act.wait_ge(s_x, done)
                    act.activation(sd[:, s], var[:, s], ACT.Sqrt, bias=const[:, C_EPS:C_EPS + 1]).then_inc(s_s, 1)

                def high(t, s, done):
                    act.wait_ge(s_x, t + 1)
                    act.copy(xh[:, :, bass.ts(t, TT)], x[:, :, bass.ts(t, TT)]).then_inc(s_h, 1)
                tiles(act, [square, root] + ([high] if xh is not None else []))

            if xh is not None:
                @block.gpsimd
                def _(pool):
                    with pool.Fori(0, NT) as t:
                        pool.wait_ge(s_h, t + 1)
                        pool.tensor_tensor(xl[:, :, bass.ts(t, TT)], x[:, :, bass.ts(t, TT)],
                                           xh[:, :, bass.ts(t, TT)].bitcast(F32), ALU.subtract).then_inc(s_l, 1)

            if out is not None:
                @block.sync
                def _(sp):
                    with sp.Fori(0, NT) as t:
                        sp.wait_ge(s_x, t + 1)
                        sp.dma_start(out[:, :, bass.ts(t, TT)], x[:, :, bass.ts(t, TT)]).then_inc(s_o, 16)
                    sp.wait_ge(s_o, 16 * NT)


def ffn_phase(nc, tag, x, xh, xl, w13_d, w2_d):
    with ExitStack() as ctx:
        p = Prog(nc, ctx)
        raw13 = p.sb(f"{tag}_w13_raw", [P, 2, KD, GW])
        raw2 = p.sb(f"{tag}_w2_raw", [P, HC, D])
        w13h = p.sb(f"{tag}_w13_hi", [P, 2, 2, KD, GW], F32R)
        w13l = p.sb(f"{tag}_w13_lo", [P, 2, 2, KD, GW], F32R)
        w2h = p.sb(f"{tag}_w2_hi", [P, 2, HC, D], F32R)
        w2l = p.sb(f"{tag}_w2_lo", [P, 2, HC, D], F32R)
        sg = p.sb(f"{tag}_silu", [P, HC, TT])
        h = p.sb(f"{tag}_h", [P, HC, TT])
        hh = p.sb(f"{tag}_h_hi", [P, HC, TT], F32R)
        hl = p.sb(f"{tag}_h_lo", [P, HC, TT], F32R)
        gate = p.ps(f"{tag}_gate", [P, HC, TT])
        up = p.ps(f"{tag}_up", [P, HC, TT])
        y = p.ps(f"{tag}_y", [P, KD, TT])
        s_raw, s_wh, s_wl = (p.sem(f"{tag}_{n}") for n in ("w_in", "w_hi", "w_lo"))
        s_gu, s_s, s_h, s_hh, s_hl, s_y, s_add = (p.sem(f"{tag}_{n}") for n in (
            "gate_up_done", "silu_done", "h_done", "h_hi", "h_lo", "y_done", "y_added"))
        NQ = NT * HC

        with nc.Block() as block:
            @block.sync
            def _(sp):
                with sp.Fori(0, NG) as g:
                    sp.wait_ge(s_wl, 2 * g)
                    sp.dma_start(raw13[:, :, :, :].rearrange("p a k n -> p (a k n)"), w13_d[:, g, :]).then_inc(s_raw, 16)
                    sp.dma_start(raw2[:, :, :].rearrange("p c d -> p (c d)"), w2_d[:, g, :]).then_inc(s_raw, 16)

            @block.gpsimd
            def _(pool):
                with pool.Fori(0, NG // 2) as gp:
                    for slot in range(2):
                        g = gp * 2 + slot
                        pool.wait_ge(s_wh, 2 * g + 2)
                        pool.tensor_tensor(w13l[:, slot], raw13[:, :, :, :], w13h[:, slot].bitcast(F32),
                                           ALU.subtract).then_inc(s_wl, 1)
                        pool.tensor_tensor(w2l[:, slot], raw2[:, :, :], w2h[:, slot].bitcast(F32),
                                           ALU.subtract).then_inc(s_wl, 1)

            @block.tensor
            def _(pe):
                def gate_up(g, t, c, slot):
                    q = (g * NT + t) * HC + c
                    pe.wait_ge(s_h, q + 1)
                    for a, out in ((0, gate), (1, up)):
                        for k in range(KD):
                            cs = slice(c * P, (c + 1) * P)
                            mm = three_passes(pe, out[:, c], w13h[:, slot, a, k, cs], w13l[:, slot, a, k, cs],
                                              xh[:, k, bass.ts(t, TT)], xl[:, k, bass.ts(t, TT)],
                                              k == 0, k == KD - 1)
                    mm.then_inc(s_gu, 1)

                def down(g, t, c, slot):
                    q = (g * NT + t) * HC + c
                    pe.wait_ge(s_hl, q + 1)
                    if c == 0:
                        pe.wait_ge(s_add, g * NT + t)
                    for m in range(KD):
                        ms = slice(m * P, (m + 1) * P)
                        mm = three_passes(pe, y[:, m], w2h[:, slot, c, ms], w2l[:, slot, c, ms],
                                          hh[:, c], hl[:, c], c == 0, c == HC - 1)
                    mm.then_inc(s_y, 1)

                def tile(g, t, slot, before):
                    gate_up(g, t, 0, slot)
                    if before is not None:
                        down(*before)
                    gate_up(g, t, 1, slot)
                    down(g, t, 0, slot)

                def groups(gp, first):
                    for slot in range(2):
                        g = gp * 2 + slot
                        pe.wait_ge(s_wl, 2 * g + 2)
                        before = None if first and slot == 0 else (g - 1, NT - 1, HC - 1, 1 - slot)
                        tile(g, 0, slot, before)
                        with pe.Fori(1, NT) as t:
                            tile(g, t, slot, (g, t - 1, HC - 1, slot))

                groups(0, True)
                with pe.Fori(1, NG // 2) as gp:
                    groups(gp, False)
                down(NG - 1, NT - 1, HC - 1, 1)

            @block.scalar
            def _(act):
                def split(g, slot):
                    act.wait_ge(s_raw, 32 * g + 32)
                    act.wait_ge(s_y, HC + NQ * (g - 1) if not isinstance(g, int) or g else 0)
                    act.copy(w13h[:, slot], raw13[:, :, :, :]).then_inc(s_wh, 1)
                    act.copy(w2h[:, slot], raw2[:, :, :]).then_inc(s_wh, 1)

                def tile(g, t):
                    for c in range(HC):
                        q = (g * NT + t) * HC + c
                        act.wait_ge(s_gu, q + 1)
                        act.wait_ge(s_h, q + 1)
                        act.activation(sg[:, c], gate[:, c], ACT.Silu).then_inc(s_s, 1)
                        act.wait_ge(s_h, q + HC + 1)
                        act.wait_ge(s_y, q + 1)
                        act.copy(hh[:, c], h[:, c]).then_inc(s_hh, 1)

                def groups(gp, last):
                    for slot in range(2):
                        g = gp * 2 + slot
                        tile(g, 0)
                        if not (last and slot):
                            split(g + 1, 1 - slot)
                        with act.Fori(1, NT) as t:
                            tile(g, t)

                split(0, 0)
                with act.Fori(0, NG // 2 - 1) as gp:
                    groups(gp, False)
                groups(NG // 2 - 1, True)

            @block.vector
            def _(dve):
                dve.sem_inc(s_h, HC)
                dve.sem_inc(s_y, HC)

                def hidden(g, t, c):
                    q = (g * NT + t) * HC + c
                    dve.wait_ge(s_s, q + 1)
                    dve.tensor_tensor(h[:, c], sg[:, c], up[:, c], ALU.mult).then_inc(s_h, 1)
                    dve.wait_ge(s_h, q + HC + 1)
                    dve.wait_ge(s_hh, q + 1)
                    dve.wait_ge(s_y, q + 1)
                    dve.tensor_tensor(hl[:, c], h[:, c], hh[:, c].bitcast(F32), ALU.subtract).then_inc(s_hl, 1)

                def add(g, t):
                    dve.wait_ge(s_y, HC + (g * NT + t + 1) * HC)
                    dve.tensor_tensor(x[:, :, bass.ts(t, TT)], x[:, :, bass.ts(t, TT)], y[:, :, :],
                                      ALU.add).then_inc(s_add, 1)

                def tile(g, t, before):
                    hidden(g, t, 0)
                    if before is not None:
                        dve.wait_ge(s_add, before[0] * NT + before[1])
                        add(*before)
                    hidden(g, t, 1)

                def groups(gp, first):
                    for slot in range(2):
                        g = gp * 2 + slot
                        tile(g, 0, None if first and slot == 0 else (g - 1, NT - 1))
                        with dve.Fori(1, NT) as t:
                            tile(g, t, (g, t - 1))

                groups(0, True)
                with dve.Fori(1, NG // 2) as gp:
                    groups(gp, False)
                add(NG - 1, NT - 1)


def scan_phase(nc, const, x, sel_d, wbc_d, wdt_d, fp_d):
    HALVES, HF = 2, KD // 2
    with ExitStack() as ctx:
        p = Prog(nc, ctx)
        sel = p.sb("selectors", [3 * NS, NS, P], BF16)
        wbc = p.sb("w_bc", [P, KD, RK + 6 * NS])
        wdt = p.sb("w_dt", [RK, D])
        feat = p.sb("scan_feat", [P, 2 * KD])
        bdt, dpar = feat[:, 0:KD], feat[:, KD:2 * KD]
        a = p.sb("a_neg", [P, KD, NS])
        rank = p.sb("rank", [RK, TT])
        soft = p.sb("soft", [P, KD, TT])
        delta = p.sb("delta", [P, KD, TT])
        du = p.sb("du", [P, KD, TT])
        bc_hi = p.sb("bc_hi", [3 * NS, 2, TT], BF16)
        bc_r = p.sb("bc_rest", [3 * NS, 2, TT])
        parts = p.sb("bc_parts", [3 * NS, 2, TT], BF16)
        bs = p.sb("b_spread", [P, 2, TT])
        db = p.sb("d_b", [P, 2, HF, TT])
        hs = p.sb("h_states", [P, 2, HF, TT])
        hc = p.sb("h_times_c", [P, 2, HF, TT])
        hlast = p.sb("h_last", [P, KD, NS])
        tmp = p.sb("y_tmp", [P, TT])
        b_ps = p.ps("b_ps", [P, 2, TT])
        c_ps = p.ps("c_ps", [P, 2, TT])
        da = p.ps("decay", [P, HF, TT])
        y = p.ps("scan_y", [P, HF, TT])
        names = ("in", "a", "rank_mm", "rank", "bc_mm", "split", "dt_mm", "abs", "relu", "soft", "delta", "du",
                 "b_mm", "c_mm", "b_spread", "decay", "db", "h", "hlast", "hc", "ysum", "ytmp", "yout", "zero")
        (s_in, s_a, s_rm, s_r, s_bm, s_sp, s_dm, s_ab, s_re, s_so, s_de, s_du, s_b, s_c, s_bs, s_da, s_db,
         s_h, s_hl, s_hc, s_y, s_yt, s_yo, s_z) = (p.sem(f"scan_{n}") for n in names)
        STEPS = HALVES * NS
        TPS = TILES_PER_SEQ
        SPLIT = 5

        PAIRS = NS // 2

        def steps(eng, t, body, after_half=None, after_first_pair=None):
            for half in range(HALVES):
                def pair(i):
                    for u in range(2):
                        body(STEPS * t + NS * half + 2 * i + u, u, half, 2 * i + u)
                pair(0)
                if after_first_pair:
                    after_first_pair(half)
                with eng.Fori(1, PAIRS - 2) as i:
                    pair(i)
                pair(PAIRS - 2)
                pair(PAIRS - 1)
                if after_half:
                    after_half(half)

        def is_first(n, half=0):
            return half == 0 and isinstance(n, int) and n == 0

        def left(n, half):
            return NS - 1 - n if half == HALVES - 1 and isinstance(n, int) else NS

        def ahead(n, k):
            return (n + k) % NS if isinstance(n, int) else n + k

        with nc.Block() as block:
            @block.sync
            def _(sp):
                sp.dma_start(sel[:, :, :], sel_d).then_inc(s_in, 16)
                sp.dma_start(wbc[:, :, :], wbc_d).then_inc(s_in, 16)
                sp.dma_start(wdt[:, :], wdt_d).then_inc(s_in, 16)
                sp.dma_start(feat[:, :], fp_d[:, 0:2 * KD]).then_inc(s_in, 16)
                sp.dma_start(a[:, :, :], fp_d[:, 2 * KD:].rearrange("p (k n) -> p k n", k=KD)).then_inc(s_in, 16)

            @block.tensor
            def _(pe):
                pe.wait_ge(s_in, 80)
                with pe.Fori(0, NT) as t:
                    pe.wait_ge(s_yo, HF * HALVES * t)
                    for k in range(KD):
                        mm = pe.matmul(y[0:RK, 0], wbc[:, k, 0:RK], x[:, k, bass.ts(t, TT)],
                                       start=(k == 0), stop=(k == KD - 1))
                    mm.then_inc(s_rm, 1)
                    pe.wait_ge(s_h, HF * STEPS * t + HF)
                    for i in range(2):
                        for k in range(KD):
                            cs = slice(RK + 3 * NS * i, RK + 3 * NS * (i + 1))
                            mm = pe.matmul(da[0:3 * NS, i], wbc[:, k, cs], x[:, k, bass.ts(t, TT)],
                                           start=(k == 0), stop=(k == KD - 1))
                        mm.then_inc(s_bm, 1)
                    pe.wait_ge(s_r, t + 1)
                    for m in range(KD):
                        if m < 2:
                            pe.wait_ge(s_r, t + 1)
                        else:
                            pe.wait_ge(s_re, KD * t + m - 1)
                        pe.matmul(y[:, m % 2], wdt[:, m * P:(m + 1) * P], rank[:, :]).then_inc(s_dm, 1)

                    def spread_b(s, slot, n):
                        pe.wait_ge(s_bs, s + 1)
                        pe.matmul(b_ps[:, slot], sel[:, n, :], parts[:, 0, :]).then_inc(s_b, 1)

                    def spread_c(s, slot, n):
                        pe.wait_ge(s_hc, s + 1)
                        pe.matmul(c_ps[:, slot], sel[:, n, :], parts[:, 1, :]).then_inc(s_c, 1)

                    def sum_states(s, slot, start):
                        pe.wait_ge(s_hc, s + 3)
                        for f in range(HF):
                            mm = pe.matmul(y[:, f], const[:, C_ID:C_ID + P], hc[:, slot, f, :],
                                           start=start, stop=True, skip_group_check=True)
                        mm.then_inc(s_y, 1)

                    def body(s, slot, half, n):
                        if left(n, half) >= 3:
                            spread_b(s + 3, 1 - slot, ahead(n, 3))
                        if not (isinstance(n, int) and n == 0):
                            start = isinstance(n, int) and n == 1
                            if start:
                                if half == 0:
                                    pe.wait_ge(s_re, KD * t + KD)
                                pe.wait_ge(s_yo, HF * (HALVES * t + half))
                            sum_states(s - 1, 1 - slot, start)
                        if left(n, half) >= 1:
                            spread_c(s + 1, 1 - slot, ahead(n, 1))

                    def tail(half):
                        sum_states(STEPS * t + NS * (half + 1) - 1, 1, False)

                    pe.wait_ge(s_sp, SPLIT * t + SPLIT)
                    spread_b(STEPS * t, 0, 0)
                    spread_b(STEPS * t + 1, 1, 1)
                    spread_b(STEPS * t + 2, 0, 2)
                    spread_c(STEPS * t, 0, 0)
                    steps(pe, t, body, tail)

            @block.scalar
            def _(act):
                act.wait_ge(s_in, 80)
                act.activation(a[:, :, :], a[:, :, :], ACT.Exp).then_inc(s_a, 1)
                act.wait_ge(s_a, 1)
                act.mul(a[:, :, :], a[:, :, :], -1.0).then_inc(s_a, 1)
                act.wait_ge(s_a, 2)
                with act.Fori(0, NT) as t:
                    act.wait_ge(s_rm, t + 1)
                    act.copy(rank[:, :], y[0:RK, 0]).then_inc(s_r, 1)
                    act.wait_ge(s_de, t)
                    for m in range(KD):
                        act.wait_ge(s_dm, KD * t + m + 1)
                        act.activation(soft[:, m, :], y[:, m % 2], ACT.Abs, bias=bdt[:, m:m + 1]).then_inc(s_ab, 1)
                    act.wait_ge(s_ab, KD * t + KD)
                    act.activation(soft[:, :, :], soft[:, :, :], ACT.Exp, scale=-1.0).then_inc(s_so, 1)
                    act.wait_ge(s_so, 2 * t + 1)
                    act.activation(soft[:, :, :], soft[:, :, :], ACT.Ln, bias=1.0).then_inc(s_so, 1)
                    act.wait_ge(s_du, t + 1)
                    act.wait_ge(s_sp, SPLIT * t + SPLIT)

                    def take_b(s, slot):
                        act.wait_ge(s_b, s + 1)
                        act.wait_ge(s_db, s + 1)
                        act.copy(bs[:, slot], b_ps[:, slot]).then_inc(s_bs, 1)

                    def decays(s, half, n, f):
                        act.wait_ge(s_h, HF * s + f + 1)
                        act.activation(da[:, f], delta[:, HF * half + f, :], ACT.Exp,
                                       scale=a[:, HF * half + f, bass.ds(n, 1)]).then_inc(s_da, 1)

                    def keep(s, slot, half, n):
                        act.wait_ge(s_h, HF * s + 2 * HF)
                        act.copy(hlast[:, HF * half:HF * (half + 1), bass.ds(n, 1)],
                                 hs[:, slot, :, TT - 1:TT]).then_inc(s_hl, 1)

                    def body(s, slot, half, n):
                        if left(n, half) >= 1:
                            take_b(s + 1, 1 - slot)
                        decays(s, half, n, 0)
                        decays(s, half, n, 1)
                        if is_first(n, half):
                            return
                        new_half = isinstance(n, int) and n == 0
                        keep(s - 1, 1 - slot, half - new_half, ahead(n, -1))

                    take_b(STEPS * t, 0)
                    steps(act, t, body)
                    keep(STEPS * (t + 1) - 1, 1, HALVES - 1, NS - 1)

            @block.gpsimd
            def _(pool):
                pool.sem_inc(s_bs, 2)
                pool.sem_inc(s_db, 2)
                with pool.Fori(0, NT) as t:
                    pool.wait_ge(s_du, t + 1)

                    def body(s, slot, half, n):
                        pool.wait_ge(s_bs, s + 3)
                        pool.wait_ge(s_h, HF * s)
                        pool.tensor_tensor(db[:, slot], du[:, HF * half:HF * (half + 1), :],
                                           bs[:, slot].unsqueeze(1).to_broadcast([P, HF, TT]),
                                           ALU.mult).then_inc(s_db, 1)
                    steps(pool, t, body)

            @block.vector
            def _(dve):
                dve.sem_inc(s_hl, 2)
                dve.sem_inc(s_hc, 2)
                dve.sem_inc(s_h, HF)

                def tile(b, u):
                    t = b * TPS + u
                    dve.wait_ge(s_bm, 2 * t + 2)
                    dve.wait_ge(s_y, STEPS * t)
                    src = da[0:3 * NS, :, :]
                    dve.tensor_copy(bc_hi[:, :, :], src).then_inc(s_sp, 1)
                    dve.wait_ge(s_sp, SPLIT * t + 1)
                    dve.scalar_tensor_tensor(out=bc_r[:, :, :], in0=bc_hi[:, :, :], scalar=const[0:3 * NS, C_M1:C_M1 + 1],
                                             in1=src, op0=ALU.mult, op1=ALU.add).then_inc(s_sp, 1)
                    dve.wait_ge(s_sp, SPLIT * t + 2)
                    dve.tensor_copy(bc_hi[:, :, :], bc_r[:, :, :]).then_inc(s_sp, 1)
                    dve.wait_ge(s_sp, SPLIT * t + 3)
                    dve.scalar_tensor_tensor(out=bc_r[:, :, :], in0=bc_hi[:, :, :], scalar=const[0:3 * NS, C_M2:C_M2 + 1],
                                             in1=bc_r[:, :, :], op0=ALU.mult, op1=ALU.add).then_inc(s_sp, 1)
                    dve.wait_ge(s_sp, SPLIT * t + 4)
                    dve.tensor_copy(parts[:, :, :], bc_r[:, :, :]).then_inc(s_sp, 1)
                    dve.wait_ge(s_da, HF * STEPS * t)
                    for m in range(KD):
                        dve.wait_ge(s_ab, KD * t + m + 1)
                        dve.tensor_scalar(delta[:, m, :], y[:, m % 2], bdt[:, m:m + 1], 0.0, ALU.add, ALU.max)\
                           .then_inc(s_re, 1)
                    dve.wait_ge(s_re, KD * t + KD)
                    dve.wait_ge(s_so, 2 * t + 2)
                    dve.tensor_tensor(delta[:, :, :], delta[:, :, :], soft[:, :, :], ALU.add).then_inc(s_de, 1)
                    dve.wait_ge(s_de, t + 1)
                    dve.wait_ge(s_db, STEPS * t)
                    dve.tensor_tensor(du[:, :, :], delta[:, :, :], x[:, :, bass.ts(t, TT)], ALU.mult).then_inc(s_du, 1)
                    dve.wait_ge(s_z, b + 1)
                    dve.wait_ge(s_hl, STEPS * t + 2)

                    def scan(s, slot, half, n, f):
                        m = HF * half + f
                        dve.wait_ge(s_da, HF * s + f + 1)
                        dve.tensor_tensor_scan(hs[:, slot, f, :], da[:, f], db[:, slot, f, :],
                                               hlast[:, m, bass.ds(n, 1)], ALU.mult, ALU.add).then_inc(s_h, 1)

                    def times_c(s, slot, summed):
                        dve.wait_ge(s_h, HF * s + 2 * HF)
                        dve.wait_ge(s_c, s + 1)
                        dve.wait_ge(s_y, summed)
                        dve.tensor_tensor(hc[:, slot], hs[:, slot],
                                          c_ps[:, slot].unsqueeze(1).to_broadcast([P, HF, TT]),
                                          ALU.mult).then_inc(s_hc, 1)

                    def body(s, slot, half, n):
                        dve.wait_ge(s_db, s + 3)
                        dve.wait_ge(s_hl, s + 1)
                        dve.wait_ge(s_hc, s + 1)
                        scan(s, slot, half, n, 0)
                        if not is_first(n, half):
                            times_c(s - 1, 1 - slot, STEPS * t if half == 0 and isinstance(n, int) and n == 1 else s - 2)
                        scan(s, slot, half, n, 1)

                    def leave(half):
                        dve.wait_ge(s_y, STEPS * t + NS * (half + 1))
                        for f in range(HF):
                            m = HF * half + f
                            i = (HALVES * t + half) * HF + f
                            xt = x[:, m, bass.ts(t, TT)]
                            dve.wait_ge(s_yo, i)
                            dve.scalar_tensor_tensor(out=tmp[:, :], in0=xt, scalar=dpar[:, m:m + 1], in1=y[:, f],
                                                     op0=ALU.mult, op1=ALU.add).then_inc(s_yt, 1)
                            dve.wait_ge(s_yt, i + 1)
                            dve.tensor_tensor(xt, xt, tmp[:, :], ALU.add).then_inc(s_yo, 1)
                    def first_half_out(half):
                        if half == 1:
                            leave(0)

                    steps(dve, t, body, after_first_pair=first_half_out)
                    times_c(STEPS * (t + 1) - 1, 1, STEPS * (t + 1) - 2)
                    leave(1)

                with dve.Fori(0, BATCH) as b:
                    dve.wait_ge(s_hl, STEPS * TPS * b + 2)
                    dve.memset(hlast[:, :, :], 0.0).then_inc(s_z, 1)
                    with dve.Fori(0, TPS) as u:
                        tile(b, u)


def program(nc, x_d, cn, w2n, aw, ld_tok, ld_feat, ld_cols, wg1_d, wg2_d, nw_d, w13a, sel_d, wbc_d, wdt_d,
            fp_d, w13b, w2b, out):
    w2h = nc.dram_tensor("w2_hadamard", (P, HID // P, D), F32, kind="Internal").ap()
    s_x = [nc.alloc_semaphore(f"x_in{t}") for t in range(NT)]
    with ExitStack() as ctx:
        p = Prog(nc, ctx)
        const = p.sb("const", [P, CW])
        x = p.sb("x", [P, KD, TOK])
        with ExitStack() as attn:
            q = Prog(nc, attn)
            aw_hi = q.sb("attn_w_hi_sb", [P, 4, KD, D], F32R)
            aw_lo = q.sb("attn_w_lo_sb", [P, 4, KD, D], F32R)
            hadamard_phase(nc, const, w2n, aw_hi, aw_lo, w2h, cn, aw, x_d, x, s_x)
            attention_phase(nc, const, x, s_x, aw_hi, aw_lo, ld_tok, ld_feat, ld_cols, wg1_d, wg2_d, nw_d)
        with ExitStack() as parts:
            q = Prog(nc, parts)
            xh, xl = q.sb("x_hi0", [P, KD, TOK], F32R), q.sb("x_lo0", [P, KD, TOK], F32R)
            layernorm_phase(nc, const, "ln0", x, xh, xl)
            ffn_phase(nc, "ffn0", x, xh, xl, w13a, w2h.rearrange("p (g c) d -> p g (c d)", g=NG))
        layernorm_phase(nc, const, "ln1", x)
        scan_phase(nc, const, x, sel_d, wbc_d, wdt_d, fp_d)
        with ExitStack() as parts:
            q = Prog(nc, parts)
            xh, xl = q.sb("x_hi1", [P, KD, TOK], F32R), q.sb("x_lo1", [P, KD, TOK], F32R)
            layernorm_phase(nc, const, "ln2", x, xh, xl)
            ffn_phase(nc, "ffn1", x, xh, xl, w13b, w2b)
        layernorm_phase(nc, const, "ln3", x, out=out)


def kernel(**inputs):
    import ml_dtypes
    import numpy as np

    import concourse.bacc as bacc
    from concourse.bass_utils import run_bass_kernel_spmd

    def rows(w):
        return np.ascontiguousarray(w.reshape(w.shape[0] // P, P, w.shape[1]).transpose(1, 0, 2))

    def grouped(w1t, w3t):
        both = np.stack([rows(w1t), rows(w3t)], axis=1).reshape(P, 2, KD, NG, GW)
        return np.ascontiguousarray(both.transpose(0, 3, 1, 2, 4)).reshape(P, NG, 2 * KD * GW)

    n = {k: np.asarray(v) for k, v in inputs.items()}
    f = np.float32
    i = np.arange(P)
    const = np.zeros((P, CW), f)
    const[:, C_ID:C_ID + P] = np.eye(P)
    const[:, C_MEAN:C_MEAN + P] = 1.0 / D
    const[:, C_HEAD:C_HEAD + P] = (i[:, None] // HD == i[None] // HD) / HD
    had = np.ones((1, 1))
    while len(had) < P:
        had = np.block([[had, had], [had, -had]])
    const[:, C_HAD:C_HAD + P] = had
    const[:, C_DIFF:C_DIFF + P] = np.maximum(i[None] - i[:, None], 0)
    const[:, C_MASK:C_MASK + P] = i[None] >= i[:, None]
    const[:, C_POS:C_POS + P] = i[None] + 1
    const[:, C_BD:C_BD + P] = i[:, None] // HD == i[None] // HD
    const[:, C_REV] = CH - 1 - i
    const[:, C_M1] = -(i >= NS).astype(f)
    const[:, C_M2] = -(i >= 2 * NS).astype(f)
    const[:, C_EPS] = EPS
    sel = np.zeros((3 * NS, NS, P), ml_dtypes.bfloat16)
    for s in range(NS):
        sel[s::NS, s] = 1
    ld = n["L0_attn_log_decay"]
    wbc = n["L1_attn_W_bc"].T
    wb, wc = wbc[:, RK:RK + NS], wbc[:, RK + NS:]
    arrays = {
        "x_t": rows(n["L0_attn_x"].reshape(TOK, D).T),
        "const": const,
        "w2a_t": rows(n["L0_ffn_W2"].T),
        "attn_w": np.stack([rows(n[f"L0_attn_{w}"]) for w in ("Wq", "Wk", "Wv", "Wo")]),
        "ld_tok": np.ascontiguousarray(np.broadcast_to(ld, (P, NH))),
        "ld_feat": np.ascontiguousarray(np.repeat(ld, HD).reshape(KD, P).T),
        "ld_cols": np.ascontiguousarray(np.broadcast_to(np.repeat(ld, HD), (P, D))),
        "wg1": rows(n["L0_attn_Wg1"]),
        "wg2": np.ascontiguousarray(n["L0_attn_Wg2"]),
        "norm_w": np.ascontiguousarray(n["L0_attn_norm_w"].reshape(KD, P).T),
        "w13a": grouped(n["L0_ffn_W1"].T, n["L0_ffn_W3"].T),
        "selectors": sel,
        "wbc": rows(np.concatenate([wbc[:, :RK], wb, wb, wb, wc, wc, wc], axis=1)),
        "wdt": np.ascontiguousarray(n["L1_attn_W_dt"].T),
        "scan_feat": np.concatenate([n["L1_attn_b_dt"].reshape(KD, P).T, n["L1_attn_D_param"].reshape(KD, P).T,
                                     rows(n["L1_attn_A_log"]).reshape(P, KD * NS)], axis=1),
        "w13b": grouped(n["L1_ffn_w_gate_up"][:HID].T, n["L1_ffn_w_gate_up"][HID:].T),
        "w2b": rows(n["L1_ffn_w_down"].T).reshape(P, NG, HC * D),
    }
    nc = bacc.Bacc("TRN2", target_bir_lowering=False, num_devices=1)
    args = [nc.dram_tensor(f"in_{k}", a.shape, mybir.dt.from_np(a.dtype), kind="ExternalInput").ap()
            for k, a in arrays.items()]
    out = nc.dram_tensor("out_t", (P, KD, TOK), F32, kind="ExternalOutput").ap()
    program(nc, *args, out)
    r = run_bass_kernel_spmd(nc, [{f"in_{k}": a for k, a in arrays.items()}], core_ids=[0])
    got = r.results[0]["out_t"]
    return np.ascontiguousarray(got.transpose(2, 1, 0)).reshape(BATCH, SEQ, D)
```

```python
from contextlib import ExitStack

import concourse.bass as bass
from concourse import mybir

F32 = mybir.dt.float32
F32R = mybir.dt.float32r
BF16 = mybir.dt.bfloat16
I32 = mybir.dt.int32
ALU = mybir.AluOpType
ACT = mybir.ActivationFunctionType

P = 128
D = 512
KD = D // P
BATCH, SEQ = 2, 1024
TOK = BATCH * SEQ
TT = 512
NT = TOK // TT
TILES_PER_SEQ = SEQ // TT
HID = 2048
NH, HD = 16, 32
HPT = P // HD
CH = 128
CPT = TT // CH
NS = 32
RK = 64
EPS = 1e-5
GW = 256
NG = HID // GW
HC = GW // P
NC = HID // P
SW = 64
NSL = D // SW

C_ID, C_MEAN, C_HEAD, C_HAD, C_DIFF, C_MASK, C_POS, C_BD = (i * P for i in range(8))
C_REV = 8 * P
C_M1, C_M2, C_EPS = C_REV + 1, C_REV + 2, C_REV + 3
CW = C_EPS + 1


def bcast(ap, shape):
    return ap.to_broadcast(shape)


class Prog:

    def __init__(self, nc, ctx):
        self.nc, self.ctx = nc, ctx

    def sb(self, name, shape, dt=F32):
        return self.ctx.enter_context(self.nc.sbuf_tensor(name, shape, dt))

    def ps(self, name, shape, dt=F32):
        return self.ctx.enter_context(self.nc.psum_tensor(name, shape, dt))

    def sem(self, name):
        return self.nc.alloc_semaphore(name)


def three_passes(pe, out, w_hi, w_lo, x_hi, x_lo, first, last):
    pe.matmul(out, w_hi, x_hi, start=first, stop=False)
    pe.matmul(out, w_hi, x_lo, start=False, stop=False)
    return pe.matmul(out, w_lo, x_hi, start=False, stop=last)


def attention_phase(nc, const, x, cn, x_dram, aw_d, ld_tok, ld_feat, ld_cols, wg1_d, wg2_d, nw_d, w2n, w2h):
    with ExitStack() as ctx:
        p = Prog(nc, ctx)
        aw_hi = p.sb("attn_w_hi", [P, 4, KD, D], F32R)
        aw_lo = p.sb("attn_w_lo", [P, 4, KD, D], F32R)
        had = [p.sb("had_a", [P, NC, SW]), p.sb("had_b", [P, NC, SW])]
        small = p.sb("attn_small", [P, NH + KD + KD + 1])
        ldt, ldf, nw = small[:, 0:NH], small[:, NH:NH + KD], small[:, NH + KD:NH + 2 * KD]
        wg1 = p.sb("wg1", [P, KD, HD])
        wg2 = p.sb("wg2", [HD, D])
        dmask = p.sb("decay_st", [P, HPT, KD, CH])
        qdec = p.sb("q_decay", [P, KD, CH])
        kdec = p.sb("k_decay", [P, D])
        cdec = p.sb("chunk_decay", [P, KD])
        xh = p.sb("attn_x_hi", [P, KD, TT], F32R)
        xl = p.sb("attn_x_lo", [P, KD, TT], F32R)
        qT = p.sb("qT", [P, KD, TT])
        kT = p.sb("kT", [P, KD, TT])
        v = p.sb("v", [P, CPT, D])
        kd = p.sb("k_decayed", [P, CPT, D])
        qd = p.sb("q_decayed", [P, KD, TT])
        live = p.sb("state_live", [P, NT], I32)
        sig = p.sb("gate_sigmoid_or_og", [P, KD, TT])
        pr = p.sb("probs", [P, HPT, KD, CH])
        g1 = p.sb("g1", [HD, TT])
        st = p.sb("state", [P, KD, CH])
        um = p.sb("state_update", [P, KD, CH])
        sd = p.sb("head_rstd", [P, 2, TT])
        sq = pr[:, :, :, :].rearrange("p a b c -> p a (b c)")
        on = og = sig
        raws = [kd[:, :, :], pr[:, :, :, :].rearrange("p a b c -> p a (b c)")]
        onh, onl = xh, xl

        scores = p.ps("scores", [P, HPT, KD, CH])
        o_ps = p.ps("o_ps", [P, KD, CH])
        u_ps = p.ps("u_ps", [P, KD, CH])
        proj = p.ps("proj", [P, 2, TT])
        g1_ps = o_ps[0:HD, :, :].rearrange("p m c -> p (m c)")

        s_sm, s_const, s_aw = p.sem("attn_small_in"), p.sem("const_in"), [p.sem(f"attn_w{i}_in") for i in range(4)]
        s_x = [p.sem(f"x_in{t}") for t in range(NT)]
        s_wh, s_wl = p.sem("attn_w_hi_ready"), p.sem("attn_w_lo_ready")
        s_w2, s_bf, s_had, s_w2h = (p.sem(n) for n in ("w2_in", "butterflies", "w2_transformed", "w2h_stored"))
        s_dexp, s_dm = p.sem("decay_exp"), p.sem("decay_masked")
        s_xh, s_xl = p.sem("attn_xh"), p.sem("attn_xl")
        s_pj = p.sem("proj_done")
        s_at, s_dt = p.sem("proj_taken_by_act"), p.sem("proj_taken_by_dve")
        s_g1p, s_g1 = p.sem("g1_product"), p.sem("g1_ready")
        s_qd = p.sem("qd_ready")
        s_sc, s_pr = p.sem("scores_done"), p.sem("probs_ready")
        s_o, s_og = p.sem("o_done"), p.sem("og_ready")
        s_u, s_um, s_us, s_st = (p.sem(n) for n in ("update_done", "update_masked", "state_scaled", "state_ready"))
        s_sq, s_sd, s_on = (p.sem(n) for n in ("squares", "head_rstd_ready", "on_ready"))
        s_zero, s_go = p.sem("attn_cleared"), p.sem("attn_go_pool")
        s_oh, s_ol = p.sem("on_hi"), p.sem("on_lo")

        FIRST = (["q"] * KD + ["k"] * KD + ["had0"] * 2 + ["v"] * CPT + ["gate"] * KD + ["had1"] * 2
                 + ["kT"] * CPT)
        NEXT = (["q"] * KD + ["norm"] * KD + ["k"] * KD + ["had0"] * 2 + ["v"] * CPT + ["gate"] * KD
                + ["wo"] * KD + ["had1"] * 2 + ["kT"] * CPT)
        TAIL = ["norm"] * KD + ["wo"] * KD
        STAGES = NC.bit_length() - 1
        BF = 2 * STAGES
        assert STAGES % 2 == 0 and NSL == 2 * NT

        def by_dve(items):
            return sum(n in ("kT", "wo") for n in items)
        CREDITS = 2

        class Round:

            def __init__(self, prev, items):
                self.prev, self.t, self.items = prev, prev + 1, items
                first = items is FIRST
                self.base = 0 if first else len(NEXT) * prev + len(FIRST)
                self.base_d = 0 if first else by_dve(NEXT) * prev + by_dve(FIRST)
                self.base_a = 0 if first else (len(NEXT) - by_dve(NEXT)) * prev + len(FIRST) - by_dve(FIRST)

            def at(self, name):
                return self.items.index(name)

            def done(self, name, m):
                return self.base + self.at(name) + m + 1

            def taken(self, i):
                n = by_dve(self.items[:i + 1])
                if by_dve(self.items[i:i + 1]):
                    return s_dt, self.base_d + n + CREDITS
                return s_at, self.base_a + i + 1 - n

            def out(self, name, m):
                return self.taken(self.at(name) + m)

        def rounds(eng, body):
            body(Round(-1, FIRST))
            with eng.Fori(0, NT - 1) as prev:
                body(Round(prev, NEXT))
            body(Round(NT - 1, TAIL))

        with nc.Block() as block:
            @block.sync
            def _(sp):
                def load_x(t):
                    sp.dma_start(x[:, :, t * TT:(t + 1) * TT], x_dram[:, :, t * TT:(t + 1) * TT]).then_inc(s_x[t], 16)

                def load_w(i):
                    if i >= 2:
                        sp.wait_ge(s_wl, i - 1)
                    sp.dma_start(raws[i % 2], aw_d[i]).then_inc(s_aw[i], 16)

                load_w(0)
                load_x(0)
                load_w(1)
                sp.dma_start(ldt, ld_tok).then_inc(s_sm, 16)
                sp.dma_start(ldf, ld_feat).then_inc(s_sm, 16)
                sp.dma_start(nw, nw_d).then_inc(s_sm, 16)
                sp.dma_start(kdec[:, :], ld_cols).then_inc(s_sm, 16)
                sp.dma_start(wg1[:, :, :], wg1_d).then_inc(s_sm, 16)
                sp.dma_start(wg2[:, :], wg2_d).then_inc(s_sm, 16)
                sp.dma_start(const[:, :], cn).then_inc(s_const, 16)
                load_w(2)
                load_w(3)
                for t in range(1, NT):
                    load_x(t)

                def body(rd):
                    if rd.items is TAIL:
                        return
                    for i in range(2):
                        j = 2 * rd.t + i
                        if i:
                            sp.wait_ge(s_pj, rd.done("had0", 1))
                        elif rd.items is NEXT:
                            sp.wait_ge(s_pj, rd.base - CPT)
                        sp.dma_start(had[0][:, :, :].rearrange("p c d -> p (c d)"), w2n[:, j, :]).then_inc(s_w2, 16)
                        sp.wait_ge(s_had, 2 * j + 2)
                        sp.dma_start(w2h[:, :, bass.ts(j, SW)], had[1][:, :, :]).then_inc(s_w2h, 16)
                rounds(sp, body)
                sp.wait_ge(s_w2h, 16 * NSL)

            @block.tensor
            def _(pe):
                def body(rd):
                    t, items = rd.t, rd.items

                    def bank(i):
                        if i < 2:
                            pe.wait_ge(s_dt, rd.base_d + i - 1 + CREDITS)
                        else:
                            pe.wait_ge(*rd.taken(i - 2))
                        return proj[:, i % 2]

                    def project(name, w, m, hi, lo):
                        out = bank(rd.at(name) + m)
                        for k in range(KD):
                            mm = three_passes(pe, out, aw_hi[:, w, k, m * P:(m + 1) * P],
                                              aw_lo[:, w, k, m * P:(m + 1) * P],
                                              hi[:, k, :], lo[:, k, :], k == 0, k == KD - 1)
                        mm.then_inc(s_pj, 1)

                    def norms():
                        pe.wait_ge(s_sq, t)
                        for m in range(KD):
                            out = bank(rd.at("norm") + m)
                            pe.matmul(out, const[:, C_HEAD:C_HEAD + P], sq[:, m, :]).then_inc(s_pj, 1)

                    def outputs():
                        pe.wait_ge(s_ol, t)
                        for m in range(KD):
                            project("wo", 3, m, onh, onl)

                    def transform(i):
                        pe.wait_ge(s_bf, BF * (2 * t + i) + BF)
                        for half in range(2):
                            out = bank(rd.at(f"had{i}") + half)
                            for c in range(NC // 2):
                                mm = pe.matmul(out[:, c * SW:(c + 1) * SW], const[:, C_HAD:C_HAD + P],
                                               had[0][:, half * (NC // 2) + c, :])
                            mm.then_inc(s_pj, 1)

                    if items is TAIL:
                        norms()
                        outputs()
                        return
                    if items is FIRST:
                        pe.wait_ge(s_wl, 1)
                    pe.wait_ge(s_xl, t + 1)
                    for m in range(KD):
                        project("q", 0, m, xh, xl)
                    if items is NEXT:
                        norms()
                    if items is FIRST:
                        pe.wait_ge(s_wl, 2)
                    for m in range(KD):
                        project("k", 1, m, xh, xl)
                    if items is FIRST:
                        pe.wait_ge(s_const, 16)
                        pe.wait_ge(s_wl, 3)
                    transform(0)
                    for c in range(CPT):
                        out = bank(rd.at("v") + c)
                        cs = slice(c * CH, (c + 1) * CH)
                        for k in range(KD):
                            mm = three_passes(pe, out, xh[:, k, cs], xl[:, k, cs],
                                              aw_hi[:, 2, k, :], aw_lo[:, 2, k, :], k == 0, k == KD - 1)
                        mm.then_inc(s_pj, 1)
                    if items is NEXT:
                        pe.wait_ge(s_og, CPT * t)
                    else:
                        pe.wait_ge(s_sm, 96)
                    for k in range(KD):
                        mm = pe.matmul(g1_ps, wg1[:, k, :], x[:, k, bass.ts(t, TT)],
                                       start=(k == 0), stop=(k == KD - 1))
                    mm.then_inc(s_g1p, 1)
                    pe.wait_ge(s_g1, t + 1)
                    for m in range(KD):
                        out = bank(rd.at("gate") + m)
                        pe.matmul(out, wg2[:, m * P:(m + 1) * P], g1[:, :]).then_inc(s_pj, 1)
                    if items is NEXT:
                        outputs()
                    transform(1)
                    pe.wait_ge(*rd.out("v", CPT - 1))
                    for c in range(CPT):
                        out = bank(rd.at("kT") + c)
                        for m in range(KD):
                            mm = pe.transpose(out[:, m * P:(m + 1) * P], kT[:, m, c * CH:(c + 1) * CH],
                                              const[:, C_ID:C_ID + P])
                        mm.then_inc(s_pj, 1)
                    for c in range(CPT):
                        n = CPT * t + c
                        cs = slice(c * CH, (c + 1) * CH)
                        for j in range(HPT):
                            r = slice(j * HD, (j + 1) * HD)
                            if not (items is FIRST and c == 0):
                                pe.wait_ge(s_pr, HPT * n)
                            for m in range(KD):
                                mm = pe.matmul(scores[:, j, m, :], kT[r, m, cs], qT[r, m, cs])
                            mm.then_inc(s_sc, 1)
                        pe.wait_ge(s_st, n + t + 1)
                        pe.wait_ge(s_qd, t + 1)
                        if not (items is FIRST and c == 0):
                            pe.wait_ge(s_og, n)
                        for m in range(KD):
                            pe.matmul(o_ps[:, m, :], st[:, m, :], qd[:, m, cs],
                                      start=(m == 0), stop=(m == KD - 1), skip_group_check=True)
                        pe.wait_ge(*rd.out("kT", c))
                        if not (items is FIRST and c == 0):
                            pe.wait_ge(s_um, n)
                        for m in range(KD):
                            mm = pe.matmul(u_ps[:, m, :], kd[:, c, m * P:(m + 1) * P], v[:, c, m * P:(m + 1) * P])
                        mm.then_inc(s_u, 1)
                        for j in range(HPT):
                            pe.wait_ge(s_pr, HPT * n + j + 1)
                            for m in range(KD):
                                h = m * HPT + j
                                mm = pe.matmul(o_ps[j * HD:(j + 1) * HD, m, :], v[:, c, h * HD:(h + 1) * HD],
                                               pr[:, j, m, :], start=False, stop=True, skip_group_check=True,
                                               tile_position=(0, j * HD))
                        mm.then_inc(s_o, 1)

                rounds(pe, body)

            @block.scalar
            def _(act):
                def weight_high(i):
                    act.wait_ge(s_aw[i], 16)
                    act.copy(aw_hi[:, i], raws[i % 2]).then_inc(s_wh, 1)

                def decays():
                    act.wait_ge(s_sm, 96)
                    act.wait_ge(s_const, 16)
                    for j in range(HPT):
                        for m in range(KD):
                            h = m * HPT + j
                            act.activation(dmask[:, j, m, :], const[:, C_DIFF:C_DIFF + P], ACT.Exp,
                                           scale=ldt[:, h:h + 1]).then_inc(s_dexp, 1)
                    for m in range(KD):
                        act.activation(qdec[:, m, :], const[:, C_POS:C_POS + P], ACT.Exp,
                                       scale=ldf[:, m:m + 1]).then_inc(s_dexp, 1)
                    act.activation(kdec[:, :], kdec[:, :], ACT.Exp,
                                   scale=const[:, C_REV:C_REV + 1]).then_inc(s_dexp, 1)
                    act.activation(cdec[:, :], ldf, ACT.Exp, scale=float(CH)).then_inc(s_dexp, 1)

                def body(rd):
                    t, items = rd.t, rd.items

                    def take(name, out, f):
                        for m in range(KD):
                            act.wait_ge(s_pj, rd.done(name, m))
                            act.activation(out[:, m, :], proj[:, (rd.at(name) + m) % 2], f).then_inc(s_at, 1)

                    def head_rstd():
                        for pair in range(0, KD, 2):
                            for m in range(pair, pair + 2):
                                act.wait_ge(s_pj, rd.done("norm", m))
                                act.wait_ge(s_on, KD * rd.prev + max(m - 1, 0))
                                act.activation(sd[:, m % 2], proj[:, (rd.at("norm") + m) % 2], ACT.Ln,
                                               bias=const[:, C_EPS:C_EPS + 1]).then_inc(s_at, 1)
                            for m in range(pair, pair + 2):
                                act.wait_ge(*rd.out("norm", m))
                                act.activation(sd[:, m % 2], sd[:, m % 2], ACT.Exp, scale=-0.5).then_inc(s_sd, 1)

                    def high_of_normed():
                        act.wait_ge(s_on, KD * t)
                        act.wait_ge(s_pj, rd.base if items is TAIL else rd.done("v", CPT - 1))
                        act.copy(onh[:, :, :], on[:, :, :]).then_inc(s_oh, 1)

                    def take_transformed(i):
                        for half in range(2):
                            act.wait_ge(s_pj, rd.done(f"had{i}", half))
                            act.mul(had[1][:, half * (NC // 2):(half + 1) * (NC // 2), :],
                                    proj[:, (rd.at(f"had{i}") + half) % 2].rearrange("p (c d) -> p c d", c=NC // 2),
                                    float(HID) ** -0.5).then_inc(s_at, 1)
                            act.wait_ge(*rd.out(f"had{i}", half))
                            act.sem_inc(s_had, 1)

                    if items is FIRST:
                        weight_high(0)
                        act.wait_ge(s_x[0], 16)
                    if items is not TAIL:
                        if items is NEXT:
                            act.wait_ge(s_pj, rd.base - CPT)
                        act.copy(xh[:, :, :], x[:, :, bass.ts(t, TT)]).then_inc(s_xh, 1)
                    if items is not FIRST:
                        act.wait_ge(s_og, CPT * t)
                        act.activation(sq[:, :, :], og[:, :, :], ACT.Square).then_inc(s_sq, 1)
                    if items is TAIL:
                        head_rstd()
                        high_of_normed()
                        return
                    if items is FIRST:
                        weight_high(1)
                    take("q", qT, ACT.Silu)
                    if items is FIRST:
                        weight_high(2)
                    if items is NEXT:
                        head_rstd()
                    take("k", kT, ACT.Silu)
                    if items is FIRST:
                        weight_high(3)
                    take_transformed(0)
                    take("v", v, ACT.Silu)
                    if items is NEXT:
                        high_of_normed()
                    act.wait_ge(s_g1p, t + 1)
                    act.copy(g1[:, :], g1_ps).then_inc(s_g1, 1)
                    if items is NEXT:
                        act.wait_ge(s_ol, t)
                    take("gate", sig, ACT.Sigmoid)
                    if items is FIRST:
                        decays()
                        for i in range(1, NT):
                            act.wait_ge(s_x[i], 16)
                    take_transformed(1)

                rounds(act, body)

            @block.gpsimd
            def _(pool):
                def butterflies(j):
                    pool.wait_ge(s_w2, 16 * j + 16)
                    pool.wait_ge(s_w2h, 16 * j)
                    for s in range(STAGES):
                        h = 1 << s
                        src = had[s % 2][:, :, :].rearrange("p (g two h) d -> p g two (h d)", two=2, h=h)
                        dst = had[(s + 1) % 2][:, :, :].rearrange("p (g two h) d -> p g two (h d)", two=2, h=h)
                        if s:
                            pool.wait_ge(s_bf, BF * j + 2 * s)
                        pool.tensor_tensor(dst[:, :, 0], src[:, :, 0], src[:, :, 1], ALU.add).then_inc(s_bf, 1)
                        pool.tensor_tensor(dst[:, :, 1], src[:, :, 0], src[:, :, 1], ALU.subtract).then_inc(s_bf, 1)

                with pool.Fori(0, NT) as t:
                    pool.wait_ge(s_xh, t + 1)
                    pool.sem_inc(s_go, 1)
                    pool.tensor_tensor(xl[:, :, :], x[:, :, bass.ts(t, TT)], xh[:, :, :].bitcast(F32),
                                       ALU.subtract).then_inc(s_xl, 1)
                    butterflies(2 * t)
                    butterflies(2 * t + 1)

            @block.vector
            def _(dve):
                dve.sem_inc(s_dt, CREDITS)
                dve.memset(st[:, :, :], 0.0).then_inc(s_zero, 1)
                dve.memset(live[:, :], -1).then_inc(s_zero, 1)
                dve.wait_ge(s_zero, 2)
                for b in range(BATCH):
                    dve.memset(live[:, b * TILES_PER_SEQ:b * TILES_PER_SEQ + 1], 0).then_inc(s_zero, 1)
                for i in range(4):
                    dve.wait_ge(s_wh, i + 1)
                    dve.tensor_tensor(aw_lo[:, i], raws[i % 2], aw_hi[:, i].bitcast(F32), ALU.subtract).then_inc(s_wl, 1)
                dve.wait_ge(s_dexp, HPT * KD + KD + 2)
                dve.tensor_tensor(dmask[:, :, :, :].rearrange("p a b c -> p (a b) c"),
                                  dmask[:, :, :, :].rearrange("p a b c -> p (a b) c"),
                                  const[:, C_MASK:C_MASK + P].unsqueeze(1).to_broadcast([P, NH, CH]),
                                  ALU.mult).then_inc(s_dm, 1)
                dve.wait_ge(s_dm, 1)
                dve.wait_ge(s_wl, 4)
                dve.wait_ge(s_zero, 2 + BATCH)

                def body(rd):
                    t, items = rd.t, rd.items
                    if items is not FIRST:
                        dve.wait_ge(s_og, CPT * t)
                        for m in range(KD):
                            dve.wait_ge(s_sd, KD * rd.prev + m + 1)
                            dve.scalar_tensor_tensor(out=on[:, m, :], in0=og[:, m, :], scalar=nw[:, m:m + 1],
                                                     in1=sd[:, m % 2], op0=ALU.mult, op1=ALU.mult).then_inc(s_on, 1)
                        dve.wait_ge(s_oh, t)
                        dve.tensor_tensor(onl[:, :, :], on[:, :, :], onh[:, :, :].bitcast(F32),
                                          ALU.subtract).then_inc(s_ol, 1)
                        for m in range(KD):
                            dve.wait_ge(s_pj, rd.done("wo", m))
                            xt = x[:, m, bass.ts(rd.prev, TT)]
                            dve.tensor_tensor(xt, xt, proj[:, (rd.at("wo") + m) % 2], ALU.add).then_inc(s_dt, 1)
                    if items is TAIL:
                        return
                    dve.wait_ge(*rd.out("q", KD - 1))
                    dve.tensor_tensor(qd[:, :, :].rearrange("p m (c i) -> p m c i", c=CPT),
                                      qT[:, :, :].rearrange("p m (c i) -> p m c i", c=CPT),
                                      qdec[:, :, :].unsqueeze(2).to_broadcast([P, KD, CPT, CH]),
                                      ALU.mult).then_inc(s_qd, 1)
                    dve.wait_ge(s_st, (CPT + 1) * t)
                    dve.tensor_tensor(st[:, :, :].rearrange("p m c -> p (m c)").bitcast(I32),
                                      st[:, :, :].rearrange("p m c -> p (m c)").bitcast(I32),
                                      live[:, bass.ds(t, 1)].to_broadcast([P, KD * CH]),
                                      ALU.bitwise_and).then_inc(s_st, 1)
                    for c in range(CPT):
                        dve.wait_ge(s_pj, rd.done("kT", c))
                        dve.tensor_tensor(kd[:, c, :], proj[:, (rd.at("kT") + c) % 2], kdec[:, :], ALU.mult)\
                           .then_inc(s_dt, 1)
                    dve.wait_ge(s_st, (CPT + 1) * t + 1)
                    for c in range(CPT):
                        n = CPT * t + c
                        for j in range(HPT):
                            dve.wait_ge(s_sc, HPT * n + j + 1)
                            dve.tensor_tensor(pr[:, j], scores[:, j], dmask[:, j], ALU.mult).then_inc(s_pr, 1)
                        dve.wait_ge(s_u, n + 1)
                        dve.tensor_tensor(um[:, :, :], u_ps[:, :, :],
                                          const[:, C_BD:C_BD + P].unsqueeze(1).to_broadcast([P, KD, CH]),
                                          ALU.mult).then_inc(s_um, 1)
                        dve.tensor_tensor(st[:, :, :], st[:, :, :],
                                          cdec[:, :].unsqueeze(2).to_broadcast([P, KD, CH]),
                                          ALU.mult).then_inc(s_us, 1)
                        dve.wait_ge(s_um, n + 1)
                        dve.wait_ge(s_us, n + 1)
                        dve.tensor_tensor(st[:, :, :], st[:, :, :], um[:, :, :], ALU.add).then_inc(s_st, 1)
                        dve.wait_ge(s_o, n + 1)
                        dve.wait_ge(*rd.out("gate", KD - 1))
                        dve.tensor_tensor(og[:, :, c * CH:(c + 1) * CH], o_ps[:, :, :],
                                          sig[:, :, c * CH:(c + 1) * CH], ALU.mult).then_inc(s_og, 1)
                        dve.wait_ge(s_st, n + t + 2)

                rounds(dve, body)


def ffn_phase(nc, const, tag, x, w13_d, w2_d, out=None):
    with ExitStack() as ctx:
        p = Prog(nc, ctx)
        xh = p.sb(f"{tag}_x_hi", [P, KD, TOK], F32R)
        xl = p.sb(f"{tag}_x_lo", [P, KD, TOK], F32R)
        raw13 = p.sb(f"{tag}_w13_raw", [P, 2, KD, GW])
        raw2 = p.sb(f"{tag}_w2_raw", [P, HC, D])
        w13h = p.sb(f"{tag}_w13_hi", [P, 2, 2, KD, GW], F32R)
        w13l = p.sb(f"{tag}_w13_lo", [P, 2, 2, KD, GW], F32R)
        w2h = p.sb(f"{tag}_w2_hi", [P, 2, HC, D], F32R)
        w2l = p.sb(f"{tag}_w2_lo", [P, 2, HC, D], F32R)
        sg = p.sb(f"{tag}_silu", [P, HC, TT])
        h = p.sb(f"{tag}_h", [P, HC, TT])
        hh = p.sb(f"{tag}_h_hi", [P, HC, TT], F32R)
        hl = p.sb(f"{tag}_h_lo", [P, HC, TT], F32R)
        sq = p.sb(f"{tag}_squares", [P, KD, TT])
        sd = p.sb(f"{tag}_rstd", [P, TT])
        gate = p.ps(f"{tag}_gate", [P, TT])
        up = p.ps(f"{tag}_up", [P, TT])
        y = p.ps(f"{tag}_y", [P, KD, TT])
        mean = p.ps(f"{tag}_mean", [P, TT])
        var = p.ps(f"{tag}_var", [P, TT])
        s_r13, s_r2, s_wh, s_w13l, s_w2l = (p.sem(f"{tag}_{n}") for n in (
            "w13_in", "w2_in", "w_hi", "w13_lo", "w2_lo"))
        s_gu, s_s, s_h, s_hh, s_hl, s_y, s_add = (p.sem(f"{tag}_{n}") for n in (
            "gate_up_done", "silu_done", "h_done", "h_hi", "h_lo", "y_done", "y_added"))
        s_m, s_c, s_q, s_v, s_ln, s_r, s_x, s_xh, s_xl, s_o = (p.sem(f"{tag}_{n}") for n in (
            "mean", "centred", "squares", "var", "ln_var", "rstd", "x_normed", "x_hi", "x_lo", "stored"))
        NQ = NT * HC
        BEFORE, AFTER = 0, NT

        def tok(t):
            return bass.ts(t, TT)

        with nc.Block() as block:
            @block.sync
            def _(sp):
                with sp.Fori(0, NG) as g:
                    sp.wait_ge(s_w13l, g)
                    sp.dma_start(raw13[:, :, :, :].rearrange("p a k n -> p (a k n)"), w13_d[:, g, :]).then_inc(s_r13, 16)
                    sp.wait_ge(s_w2l, g)
                    sp.dma_start(raw2[:, :, :].rearrange("p c d -> p (c d)"), w2_d[:, g, :]).then_inc(s_r2, 16)
                if out is not None:
                    for t in range(NT):
                        sp.wait_ge(s_x, AFTER + t + 1)
                        sp.dma_start(out[:, :, t * TT:(t + 1) * TT], x[:, :, t * TT:(t + 1) * TT]).then_inc(s_o, 16)
                    sp.wait_ge(s_o, 16 * NT)

            @block.gpsimd
            def _(pool):
                with pool.Fori(0, NG // 2) as gp:
                    for slot in range(2):
                        g = gp * 2 + slot
                        pool.wait_ge(s_wh, 2 * g + 1)
                        pool.tensor_tensor(w13l[:, slot], raw13[:, :, :, :], w13h[:, slot].bitcast(F32),
                                           ALU.subtract).then_inc(s_w13l, 1)
                        pool.wait_ge(s_wh, 2 * g + 2)
                        pool.tensor_tensor(w2l[:, slot], raw2[:, :, :], w2h[:, slot].bitcast(F32),
                                           ALU.subtract).then_inc(s_w2l, 1)

            @block.tensor
            def _(pe):
                def average(bank, src):
                    for k in range(KD):
                        mm = pe.matmul(bank[:, :], const[:, C_MEAN:C_MEAN + P], src(k),
                                       start=(k == 0), stop=(k == KD - 1))
                    return mm

                def means(i, t):
                    if i >= AFTER:
                        pe.wait_ge(s_add, (NG - 1) * NT + t + 1)
                    if i:
                        pe.wait_ge(s_c, i)
                    average(mean, lambda k: x[:, k, tok(t)]).then_inc(s_m, 1)

                def variances(i):
                    pe.wait_ge(s_q, i + 1)
                    if i:
                        pe.wait_ge(s_ln, i)
                    average(var, lambda k: sq[:, k, :]).then_inc(s_v, 1)

                def gate_up(g, t, c, slot):
                    q = (g * NT + t) * HC + c
                    pe.wait_ge(s_h, q + HC)
                    for a, bank in ((0, gate), (1, up)):
                        for k in range(KD):
                            cs = slice(c * P, (c + 1) * P)
                            mm = three_passes(pe, bank[:, :], w13h[:, slot, a, k, cs], w13l[:, slot, a, k, cs],
                                              xh[:, k, tok(t)], xl[:, k, tok(t)], k == 0, k == KD - 1)
                    mm.then_inc(s_gu, 1)

                def down(g, t, c, slot):
                    q = (g * NT + t) * HC + c
                    pe.wait_ge(s_hl, q + 1)
                    if c == 0:
                        pe.wait_ge(s_add, g * NT + t)
                    for m in range(KD):
                        ms = slice(m * P, (m + 1) * P)
                        mm = three_passes(pe, y[:, m], w2h[:, slot, c, ms], w2l[:, slot, c, ms],
                                          hh[:, c], hl[:, c], c == 0, c == HC - 1)
                    mm.then_inc(s_y, 1)

                def tile(g, t, slot, before):
                    gate_up(g, t, 0, slot)
                    down(*before)
                    gate_up(g, t, 1, slot)
                    down(g, t, 0, slot)

                def group(g, slot):
                    pe.wait_ge(s_w13l, g + 1)
                    pe.wait_ge(s_w2l, g + 1)
                    tile(g, 0, slot, (g - 1, NT - 1, HC - 1, 1 - slot))
                    with pe.Fori(1, NT) as t:
                        tile(g, t, slot, (g, t - 1, HC - 1, slot))

                def first_group():
                    means(BEFORE, 0)
                    variances(BEFORE)
                    pe.wait_ge(s_w13l, 1)
                    for t in range(NT):
                        if t < NT - 1:
                            means(BEFORE + t + 1, t + 1)
                        pe.wait_ge(s_xl, t + 1)
                        gate_up(0, t, 0, 0)
                        if t < NT - 1:
                            variances(BEFORE + t + 1)
                        if t:
                            down(0, t - 1, 1, 0)
                        else:
                            pe.wait_ge(s_w2l, 1)
                        gate_up(0, t, 1, 0)
                        down(0, t, 0, 0)

                def last_group():
                    g = NG - 1
                    pe.wait_ge(s_w13l, g + 1)
                    pe.wait_ge(s_w2l, g + 1)
                    for t in range(NT):
                        gate_up(g, t, 0, 1)
                        if t >= 2:
                            variances(AFTER + t - 2)
                        down(*((g, t - 1, 1, 1) if t else (g - 1, NT - 1, 1, 0)))
                        gate_up(g, t, 1, 1)
                        if t:
                            means(AFTER + t - 1, t - 1)
                        down(g, t, 0, 1)
                    down(g, NT - 1, 1, 1)
                    variances(AFTER + NT - 2)
                    means(AFTER + NT - 1, NT - 1)
                    variances(AFTER + NT - 1)

                first_group()
                group(1, 1)
                with pe.Fori(1, NG // 2 - 1) as gp:
                    group(2 * gp, 0)
                    group(2 * gp + 1, 1)
                group(NG - 2, 0)
                last_group()

            @block.scalar
            def _(act):
                def split(g, slot):
                    act.wait_ge(s_r13, 16 * g + 16)
                    act.wait_ge(s_y, HC + NQ * (g - 1) if not isinstance(g, int) or g else 0)
                    act.copy(w13h[:, slot], raw13[:, :, :, :]).then_inc(s_wh, 1)
                    act.wait_ge(s_r2, 16 * g + 16)
                    act.copy(w2h[:, slot], raw2[:, :, :]).then_inc(s_wh, 1)

                def square(i, t):
                    act.wait_ge(s_c, i + 1)
                    act.wait_ge(s_v, i)
                    act.activation(sq[:, :, :], x[:, :, tok(t)], ACT.Square).then_inc(s_q, 1)

                def rstd(i):
                    act.wait_ge(s_v, i + 1)
                    act.wait_ge(s_x, i)
                    act.activation(sd[:, :], var[:, :], ACT.Ln, bias=const[:, C_EPS:C_EPS + 1]).then_inc(s_ln, 1)
                    act.wait_ge(s_ln, i + 1)
                    act.activation(sd[:, :], sd[:, :], ACT.Exp, scale=-0.5).then_inc(s_r, 1)

                def high(t):
                    act.wait_ge(s_x, BEFORE + t + 1)
                    act.copy(xh[:, :, tok(t)], x[:, :, tok(t)]).then_inc(s_xh, 1)

                def silu(g, t, c):
                    q = (g * NT + t) * HC + c
                    act.wait_ge(s_gu, q + 1)
                    act.wait_ge(s_h, q + 1)
                    act.activation(sg[:, c], gate[:, :], ACT.Silu).then_inc(s_s, 1)

                def h_high(g, t, c):
                    q = (g * NT + t) * HC + c
                    act.wait_ge(s_h, q + HC + 1)
                    act.wait_ge(s_y, q + 1)
                    act.copy(hh[:, c], h[:, c]).then_inc(s_hh, 1)

                def tile(g, t):
                    for c in range(HC):
                        silu(g, t, c)
                        h_high(g, t, c)

                def group(g, slot):
                    tile(g, 0)
                    split(g + 1, 1 - slot)
                    with act.Fori(1, NT) as t:
                        tile(g, t)

                square(BEFORE, 0)
                split(0, 0)
                rstd(BEFORE)
                high(0)
                for t in range(NT):
                    if t < NT - 1:
                        square(BEFORE + t + 1, t + 1)
                    silu(0, t, 0)
                    h_high(0, t, 0)
                    if t < NT - 1:
                        rstd(BEFORE + t + 1)
                        high(t + 1)
                    silu(0, t, 1)
                    h_high(0, t, 1)
                    if t == 0:
                        split(1, 1)
                group(1, 1)
                with act.Fori(1, NG // 2 - 1) as gp:
                    group(2 * gp, 0)
                    group(2 * gp + 1, 1)
                group(NG - 2, 0)
                for t in range(NT):
                    silu(NG - 1, t, 0)
                    h_high(NG - 1, t, 0)
                    if t >= 2:
                        rstd(AFTER + t - 2)
                    silu(NG - 1, t, 1)
                    h_high(NG - 1, t, 1)
                    if t:
                        square(AFTER + t - 1, t - 1)
                rstd(AFTER + NT - 2)
                square(AFTER + NT - 1, NT - 1)
                rstd(AFTER + NT - 1)

            @block.vector
            def _(dve):
                dve.sem_inc(s_h, HC)
                dve.sem_inc(s_y, HC)

                def centre(i, t):
                    dve.wait_ge(s_m, i + 1)
                    dve.tensor_tensor(x[:, :, tok(t)], x[:, :, tok(t)],
                                      mean[:, :].unsqueeze(1).to_broadcast([P, KD, TT]),
                                      ALU.subtract).then_inc(s_c, 1)

                def scale(i, t):
                    dve.wait_ge(s_r, i + 1)
                    dve.tensor_tensor(x[:, :, tok(t)], x[:, :, tok(t)],
                                      sd[:, :].unsqueeze(1).to_broadcast([P, KD, TT]), ALU.mult).then_inc(s_x, 1)

                def low(t):
                    dve.wait_ge(s_xh, t + 1)
                    dve.tensor_tensor(xl[:, :, tok(t)], x[:, :, tok(t)], xh[:, :, tok(t)].bitcast(F32),
                                      ALU.subtract).then_inc(s_xl, 1)

                def hidden(g, t, c):
                    q = (g * NT + t) * HC + c
                    dve.wait_ge(s_s, q + 1)
                    dve.tensor_tensor(h[:, c], sg[:, c], up[:, :], ALU.mult).then_inc(s_h, 1)
                    dve.wait_ge(s_h, q + HC + 1)
                    dve.wait_ge(s_hh, q + 1)
                    dve.wait_ge(s_y, q + 1)
                    dve.tensor_tensor(hl[:, c], h[:, c], hh[:, c].bitcast(F32), ALU.subtract).then_inc(s_hl, 1)

                def add(g, t):
                    dve.wait_ge(s_y, HC + (g * NT + t + 1) * HC)
                    dve.tensor_tensor(x[:, :, tok(t)], x[:, :, tok(t)], y[:, :, :], ALU.add).then_inc(s_add, 1)

                def tile(g, t, before):
                    hidden(g, t, 0)
                    add(*before)
                    hidden(g, t, 1)

                def group(g):
                    dve.wait_ge(s_add, (g - 1) * NT + NT - 1)
                    tile(g, 0, (g - 1, NT - 1))
                    with dve.Fori(1, NT) as t:
                        tile(g, t, (g, t - 1))

                centre(BEFORE, 0)
                scale(BEFORE, 0)
                low(0)
                for t in range(NT):
                    if t < NT - 1:
                        centre(BEFORE + t + 1, t + 1)
                    hidden(0, t, 0)
                    if t < NT - 1:
                        scale(BEFORE + t + 1, t + 1)
                    if t:
                        add(0, t - 1)
                    if t < NT - 1:
                        low(t + 1)
                    hidden(0, t, 1)
                group(1)
                with dve.Fori(1, NG // 2 - 1) as gp:
                    group(2 * gp)
                    group(2 * gp + 1)
                group(NG - 2)
                g = NG - 1
                for t in range(NT):
                    hidden(g, t, 0)
                    if t >= 2:
                        scale(AFTER + t - 2, t - 2)
                    add(*((g, t - 1) if t else (g - 1, NT - 1)))
                    hidden(g, t, 1)
                    if t:
                        centre(AFTER + t - 1, t - 1)
                add(g, NT - 1)
                scale(AFTER + NT - 2, NT - 2)
                centre(AFTER + NT - 1, NT - 1)
                scale(AFTER + NT - 1, NT - 1)


def scan_prepare_phase(nc, const, x, sel, feat, a, delta, du, parts, sel_d, wbc_d, wdt_d, fp_d):
    with ExitStack() as ctx:
        p = Prog(nc, ctx)
        bdt = feat[:, 0:KD]
        wbc = p.sb("w_bc", [P, KD, 2, P])
        wdt = p.sb("w_dt", [RK, D])
        rank = p.sb("rank", [RK, 2, TT])
        soft = p.sb("soft", [P, 2, KD, TT])
        bc_hi = p.sb("bc_hi", [3 * NS, 2, 2, TT], BF16)
        bc_r = p.sb("bc_rest", [3 * NS, 2, 2, TT])
        bc = p.ps("bc_rank", [P, 2, 2, TT])
        dt = p.ps("dt", [P, KD, TT])
        s_in, s_a, s_bc, s_r, s_dt, s_ab, s_re, s_so, s_de, s_du, s_sp, s_pt = (p.sem(f"prep_{n}") for n in (
            "in", "a", "bc_mm", "rank", "dt_mm", "abs", "relu", "soft", "delta", "du", "split", "parts"))
        RH = RK // 2

        def tiles(eng, stages):
            with eng.Fori(0, NT // 2) as i:
                for stage in stages:
                    for s in range(2):
                        stage(2 * i + s, s, 2 * i)

        with nc.Block() as block:
            @block.sync
            def _(sp):
                sp.dma_start(wbc[:, :, :, :], wbc_d).then_inc(s_in, 16)
                sp.dma_start(wdt[:, :], wdt_d).then_inc(s_in, 16)
                sp.dma_start(feat[:, :], fp_d[:, 0:2 * KD]).then_inc(s_in, 16)
                sp.dma_start(a[:, :, :], fp_d[:, 2 * KD:].rearrange("p (k n) -> p k n", k=KD)).then_inc(s_in, 16)
                sp.dma_start(sel[:, :, :], sel_d).then_inc(s_in, 16)
                sp.wait_ge(s_in, 80)

            @block.tensor
            def _(pe):
                pe.wait_ge(s_in, 80)

                def project(t, s, done):
                    pe.wait_ge(s_r, 2 * done)
                    pe.wait_ge(s_sp, 2 * done)
                    for i in range(2):
                        for k in range(KD):
                            mm = pe.matmul(bc[:, s, i], wbc[:, k, i, :], x[:, k, bass.ts(t, TT)],
                                           start=(k == 0), stop=(k == KD - 1))
                        mm.then_inc(s_bc, 1)

                def step_size(t, s, done):
                    pe.wait_ge(s_r, 2 * t + 2)
                    for m in range(KD):
                        pe.wait_ge(s_re, KD * done + (m + 1 if s else 0))
                        pe.matmul(dt[:, m], wdt[:, m * P:(m + 1) * P], rank[:, s]).then_inc(s_dt, 1)
                tiles(pe, [project, step_size])

            @block.scalar
            def _(act):
                act.wait_ge(s_in, 80)
                act.activation(a[:, :, :], a[:, :, :], ACT.Exp).then_inc(s_a, 1)
                act.wait_ge(s_a, 1)
                act.mul(a[:, :, :], a[:, :, :], -1.0).then_inc(s_a, 1)

                def ranks(t, s, done):
                    act.wait_ge(s_bc, 2 * t + 2)
                    act.wait_ge(s_dt, KD * done)
                    for i in range(2):
                        act.copy(rank[i * RH:(i + 1) * RH, s], bc[P - RH:P, s, i]).then_inc(s_r, 1)

                def magnitude(t, s, done):
                    act.wait_ge(s_de, done)
                    for m in range(KD):
                        act.wait_ge(s_dt, KD * t + m + 1)
                        act.activation(soft[:, s, m, :], dt[:, m], ACT.Abs, bias=bdt[:, m:m + 1]).then_inc(s_ab, 1)

                def exponent(t, s, done):
                    act.wait_ge(s_ab, KD * t + KD)
                    act.activation(soft[:, s], soft[:, s], ACT.Exp, scale=-1.0).then_inc(s_so, 1)

                def logarithm(t, s, done):
                    act.wait_ge(s_so, 2 * done + s + 1)
                    act.activation(soft[:, s], soft[:, s], ACT.Ln, bias=1.0).then_inc(s_so, 1)
                tiles(act, [ranks, magnitude, exponent, logarithm])
                act.wait_ge(s_a, 2)

            @block.vector
            def _(dve):
                dve.memset(parts[:, :, NT * TT:], 0.0).then_inc(s_pt, 1)

                def first(t, s, done):
                    dve.wait_ge(s_r, 2 * t + 2)
                    dve.wait_ge(s_pt, done + 1)
                    dve.tensor_copy(bc_hi[:, s], bc[0:3 * NS, s]).then_inc(s_sp, 1)

                def first_rest(t, s, done):
                    dve.wait_ge(s_sp, 2 * done + s + 1)
                    dve.scalar_tensor_tensor(out=bc_r[:, s], in0=bc_hi[:, s], scalar=const[0:3 * NS, C_M1:C_M1 + 1],
                                             in1=bc[0:3 * NS, s], op0=ALU.mult, op1=ALU.add).then_inc(s_sp, 1)

                def second(t, s, done):
                    dve.wait_ge(s_sp, 2 * done + s + 3)
                    dve.tensor_copy(bc_hi[:, s], bc_r[:, s]).then_inc(s_mid, 1)

                def second_rest(t, s, done):
                    dve.wait_ge(s_mid, t + 1)
                    dve.scalar_tensor_tensor(out=bc_r[:, s], in0=bc_hi[:, s], scalar=const[0:3 * NS, C_M2:C_M2 + 1],
                                             in1=bc_r[:, s], op0=ALU.mult, op1=ALU.add).then_inc(s_rest, 1)

                def third(t, s, done):
                    dve.wait_ge(s_rest, t + 1)
                    dve.tensor_copy(parts[:, :, bass.ts(t, TT)], bc_r[:, s]).then_inc(s_pt, 1)

                def positive(t, s, done):
                    for m in range(KD):
                        dve.wait_ge(s_ab, KD * t + m + 1)
                        dve.tensor_scalar(delta[:, m, bass.ts(t, TT)], dt[:, m], bdt[:, m:m + 1], 0.0,
                                          ALU.add, ALU.max).then_inc(s_re, 1)

                def softplus(t, s, done):
                    dve.wait_ge(s_re, KD * t + KD)
                    dve.wait_ge(s_so, 2 * done + s + 3)
                    dve.tensor_tensor(delta[:, :, bass.ts(t, TT)], delta[:, :, bass.ts(t, TT)], soft[:, s],
                                      ALU.add).then_inc(s_de, 1)
                s_mid, s_rest = p.sem("prep_mid"), p.sem("prep_rest")
                tiles(dve, [first, first_rest, second, second_rest, positive, third, softplus])

            @block.gpsimd
            def _(pool):
                with pool.Fori(0, NT) as t:
                    pool.wait_ge(s_de, t + 1)
                    pool.tensor_tensor(du[:, :, bass.ts(t, TT)], delta[:, :, bass.ts(t, TT)],
                                       x[:, :, bass.ts(t, TT)], ALU.mult).then_inc(s_du, 1)


def scan_phase(nc, const, x, sel, feat, a, delta, du, parts):
    HF = KD // 2
    SEGS = TILES_PER_SEQ * 2
    Q = 4
    with ExitStack() as ctx:
        p = Prog(nc, ctx)
        dpar = feat[:, KD:2 * KD]
        bs = p.sb("b_spread", [P, Q, TT])
        db = p.sb("d_b", [P, Q, HF, TT])
        hs = p.sb("h_states", [P, 2, HF, TT])
        hc = p.sb("h_times_c", [P, 2, HF, TT])
        hlast = p.sb("h_last", [P, KD, NS])
        tmp = p.sb("y_tmp", [P, HF, TT])
        b_ps = p.ps("b_ps", [P, 2, TT])
        c_ps = p.ps("c_ps", [P, 2, TT])
        da = p.ps("decay", [P, HF, TT])
        y = p.ps("scan_y", [P, HF, TT])
        names = ("b_mm", "c_mm", "b_spread", "decay", "db", "h", "hlast", "hc", "ysum", "ytmp", "yout", "zero",
                 "go_act", "go_pool")
        s_b, s_c, s_bs, s_da, s_db, s_h, s_hl, s_hc, s_y, s_yt, s_yo, s_z, s_ga, s_gp = (p.sem(f"scan_{n}") for n in names)
        C_BS, C_DB, C_H, C_HL, C_HC = 2, Q, Q * HF, 2, 2

        class Step:

            def __init__(self, b, seg, n, known):
                self.b, self.seg, self.n, self.known = b, seg, n, known
                self.s = SEGS * NS * b + NS * seg + n
                self.half = seg % 2
                self.t = TILES_PER_SEQ * b + seg // 2

            def after(self, k):
                if self.known and self.n + k >= NS:
                    return Step(self.b, self.seg + 1, self.n + k - NS, True)
                return Step(self.b, self.seg, self.n + k, self.known)

        def steps(eng, b, seg, body):
            def some(i, known):
                for u in range(Q):
                    body(Step(b, seg, Q * i + u, known), u)
            some(0, True)
            with eng.Fori(1, NS // Q - 1) as i:
                some(i, False)
            some(NS // Q - 1, True)

        with nc.Block() as block:
            @block.tensor
            def _(pe):
                def spread_b(st, u):
                    pe.wait_ge(s_bs, st.s - 2 + 1 + C_BS)
                    pe.matmul(b_ps[:, u % 2], sel[:, st.n, :], parts[:, 0, bass.ts(st.t, TT)]).then_inc(s_b, 1)

                def spread_c(st, u):
                    pe.wait_ge(s_hc, st.s - 2 + 1 + C_HC)
                    pe.matmul(c_ps[:, u % 2], sel[:, st.n, :], parts[:, 1, bass.ts(st.t, TT)]).then_inc(s_c, 1)

                def sum_states(s, u, start):
                    pe.wait_ge(s_hc, s + 1 + C_HC)
                    for f in range(HF):
                        mm = pe.matmul(y[:, f], const[:, C_ID:C_ID + P], hc[:, u % 2, f, :],
                                       start=start, stop=True, skip_group_check=True)
                    mm.then_inc(s_y, 1)

                def body(st, u):
                    if not (st.known and st.n == 0):
                        start = st.known and st.n == 1
                        if start:
                            pe.wait_ge(s_yo, HF * (SEGS * st.b + st.seg))
                        sum_states(st.s - 1, u - 1, start)
                    spread_c(st.after(1), u + 1)
                    spread_b(st.after(Q), u)

                zero = Step(0, 0, 0, True)
                spread_c(zero, 0)
                for k in range(Q):
                    spread_b(zero.after(k), k)
                with pe.Fori(0, BATCH) as b:
                    for seg in range(SEGS):
                        steps(pe, b, seg, body)
                        sum_states(SEGS * NS * b + NS * (seg + 1) - 1, 1, False)

            @block.scalar
            def _(act):
                def take_b(st, u):
                    act.wait_ge(s_b, st.s + 1)
                    act.wait_ge(s_db, st.s - Q + 1 + C_DB)
                    act.copy(bs[:, u % Q], b_ps[:, u % 2]).then_inc(s_bs, 1)

                def decays(st, f):
                    m = HF * st.half + f
                    act.wait_ge(s_h, HF * (st.s - 1) + f + 1 + C_H)
                    if st.known:
                        act.sem_inc(s_ga, 1)
                    act.activation(da[:, f], delta[:, m, bass.ts(st.t, TT)], ACT.Exp,
                                   scale=a[:, m, bass.ds(st.n, 1)]).then_inc(s_da, 1)

                def keep(s, u, half, n):
                    act.wait_ge(s_h, HF * s + HF + C_H)
                    act.copy(hlast[:, HF * half:HF * (half + 1), bass.ds(n, 1)],
                             hs[:, u % 2, :, TT - 1:TT]).then_inc(s_hl, 1)

                def body(st, u):
                    decays(st, 0)
                    take_b(st.after(2), u + 2)
                    decays(st, 1)
                    if not (st.known and st.n == 0):
                        keep(st.s - 1, u - 1, st.half, st.n - 1)

                zero = Step(0, 0, 0, True)
                for k in range(2):
                    take_b(zero.after(k), k)
                with act.Fori(0, BATCH) as b:
                    for seg in range(SEGS):
                        steps(act, b, seg, body)
                        keep(SEGS * NS * b + NS * (seg + 1) - 1, 1, seg % 2, NS - 1)

            @block.gpsimd
            def _(pool):
                pool.sem_inc(s_bs, C_BS)
                pool.sem_inc(s_db, C_DB)

                def body(st, u):
                    pool.wait_ge(s_bs, st.s + 1 + C_BS)
                    pool.wait_ge(s_h, HF * (st.s - Q + 1) + C_H)
                    pool.sem_inc(s_gp, 1)
                    pool.tensor_tensor(db[:, u], du[:, HF * st.half:HF * (st.half + 1), bass.ts(st.t, TT)],
                                       bs[:, u].unsqueeze(1).to_broadcast([P, HF, TT]),
                                       ALU.mult).then_inc(s_db, 1)

                with pool.Fori(0, BATCH) as b:
                    for seg in range(SEGS):
                        steps(pool, b, seg, body)

            @block.vector
            def _(dve):
                dve.sem_inc(s_hl, C_HL)
                dve.sem_inc(s_hc, C_HC)
                dve.sem_inc(s_h, C_H)

                def scan(st, u, f):
                    m = HF * st.half + f
                    dve.wait_ge(s_da, HF * st.s + f + 1)
                    dve.tensor_tensor_scan(hs[:, u % 2, f, :], da[:, f], db[:, u, f, :],
                                           hlast[:, m, bass.ds(st.n, 1)], ALU.mult, ALU.add).then_inc(s_h, 1)

                def times_c(s, u):
                    dve.wait_ge(s_h, HF * s + HF + C_H)
                    dve.wait_ge(s_c, s + 1)
                    dve.tensor_tensor(hc[:, u % 2], hs[:, u % 2],
                                      c_ps[:, u % 2].unsqueeze(1).to_broadcast([P, HF, TT]),
                                      ALU.mult).then_inc(s_hc, 1)

                def leave(b, seg):
                    done = SEGS * b + seg
                    dve.wait_ge(s_y, NS * (done + 1))
                    for f in range(HF):
                        m = HF * (seg % 2) + f
                        xt = x[:, m, bass.ts(TILES_PER_SEQ * b + seg // 2, TT)]
                        dve.wait_ge(s_yo, HF * done)
                        dve.scalar_tensor_tensor(out=tmp[:, f], in0=xt, scalar=dpar[:, m:m + 1], in1=y[:, f],
                                                 op0=ALU.mult, op1=ALU.add).then_inc(s_yt, 1)
                    for f in range(HF):
                        m = HF * (seg % 2) + f
                        xt = x[:, m, bass.ts(TILES_PER_SEQ * b + seg // 2, TT)]
                        dve.wait_ge(s_yt, HF * done + f + 1)
                        dve.tensor_tensor(xt, xt, tmp[:, f], ALU.add).then_inc(s_yo, 1)

                def body(st, u):
                    dve.wait_ge(s_db, st.s + 1 + C_DB)
                    dve.wait_ge(s_hl, st.s - 1 + C_HL)
                    dve.wait_ge(s_hc, st.s - 1 + C_HC)
                    scan(st, u, 0)
                    if not (st.known and st.n == 0):
                        if not (st.known and st.n == 1 and st.seg == 0):
                            dve.wait_ge(s_y, st.s - 2)
                        else:
                            dve.wait_ge(s_y, SEGS * NS * st.b)
                        times_c(st.s - 1, u - 1)
                    scan(st, u, 1)
                    if st.known and st.n == 1 and st.seg > 0:
                        leave(st.b, st.seg - 1)

                with dve.Fori(0, BATCH) as b:
                    dve.wait_ge(s_hl, SEGS * NS * b + C_HL)
                    dve.memset(hlast[:, :, :], 0.0).then_inc(s_z, 1)
                    dve.wait_ge(s_z, b + 1)
                    for seg in range(SEGS):
                        if seg >= 2:
                            dve.wait_ge(s_hl, SEGS * NS * b + NS * (seg - 1) + C_HL)
                        steps(dve, b, seg, body)
                        last = SEGS * NS * b + NS * (seg + 1) - 1
                        dve.wait_ge(s_y, last - 1)
                        times_c(last, 1)
                    leave(b, SEGS - 1)


def program(nc, x_d, cn, w2n, aw, ld_tok, ld_feat, ld_cols, wg1_d, wg2_d, nw_d, w13a, sel_d, wbc_d, wdt_d,
            fp_d, w13b, w2b, out):
    w2h = nc.dram_tensor("w2_hadamard", (P, HID // P, D), F32, kind="Internal").ap()
    with ExitStack() as ctx:
        p = Prog(nc, ctx)
        const = p.sb("const", [P, CW])
        x = p.sb("x", [P, KD, TOK])
        attention_phase(nc, const, x, cn, x_d, aw, ld_tok, ld_feat, ld_cols, wg1_d, wg2_d, nw_d, w2n, w2h)
        ffn_phase(nc, const, "ffn0", x, w13a, w2h.rearrange("p (g c) d -> p g (c d)", g=NG))
        with ExitStack() as scan:
            q = Prog(nc, scan)
            sel = q.sb("selectors", [3 * NS, NS, P], BF16)
            feat = q.sb("scan_feat", [P, 2 * KD])
            a = q.sb("a_neg", [P, KD, NS])
            delta, du = q.sb("delta", [P, KD, TOK]), q.sb("delta_x", [P, KD, TOK])
            bc_parts = q.sb("bc_parts", [3 * NS, 2, TOK + TT], BF16)
            scan_prepare_phase(nc, const, x, sel, feat, a, delta, du, bc_parts, sel_d, wbc_d, wdt_d, fp_d)
            scan_phase(nc, const, x, sel, feat, a, delta, du, bc_parts)
        ffn_phase(nc, const, "ffn1", x, w13b, w2b, out)


def kernel(**inputs):
    import ml_dtypes
    import numpy as np

    import concourse.bacc as bacc
    from concourse.bass_utils import run_bass_kernel_spmd

    def rows(w):
        return np.ascontiguousarray(w.reshape(w.shape[0] // P, P, w.shape[1]).transpose(1, 0, 2))

    def grouped(w1t, w3t):
        both = np.stack([rows(w1t), rows(w3t)], axis=1).reshape(P, 2, KD, NG, GW)
        return np.ascontiguousarray(both.transpose(0, 3, 1, 2, 4)).reshape(P, NG, 2 * KD * GW)

    n = {k: np.asarray(v) for k, v in inputs.items()}
    f = np.float32
    i = np.arange(P)
    const = np.zeros((P, CW), f)
    const[:, C_ID:C_ID + P] = np.eye(P)
    const[:, C_MEAN:C_MEAN + P] = 1.0 / D
    const[:, C_HEAD:C_HEAD + P] = (i[:, None] // HD == i[None] // HD) / HD
    had = np.ones((1, 1))
    while len(had) < P:
        had = np.block([[had, had], [had, -had]])
    const[:, C_HAD:C_HAD + P] = had
    const[:, C_DIFF:C_DIFF + P] = np.maximum(i[None] - i[:, None], 0)
    const[:, C_MASK:C_MASK + P] = i[None] >= i[:, None]
    const[:, C_POS:C_POS + P] = i[None] + 1
    const[:, C_BD:C_BD + P] = i[:, None] // HD == i[None] // HD
    const[:, C_REV] = CH - 1 - i
    const[:, C_M1] = -(i >= NS).astype(f)
    const[:, C_M2] = -(i >= 2 * NS).astype(f)
    const[:, C_EPS] = EPS
    sel = np.zeros((3 * NS, NS, P), ml_dtypes.bfloat16)
    for s in range(NS):
        sel[s::NS, s] = 1
    ld = n["L0_attn_log_decay"]
    wbc = n["L1_attn_W_bc"].T
    wb, wc = wbc[:, RK:RK + NS], wbc[:, RK + NS:]
    arrays = {
        "x_t": rows(n["L0_attn_x"].reshape(TOK, D).T),
        "const": const,
        "w2a_t": np.ascontiguousarray(rows(n["L0_ffn_W2"].T).reshape(P, NC, NSL, SW).transpose(0, 2, 1, 3))
        .reshape(P, NSL, NC * SW),
        "attn_w": np.stack([rows(n[f"L0_attn_{w}"]) for w in ("Wq", "Wk", "Wv", "Wo")]),
        "ld_tok": np.ascontiguousarray(np.broadcast_to(ld, (P, NH))),
        "ld_feat": np.ascontiguousarray(np.repeat(ld, HD).reshape(KD, P).T),
        "ld_cols": np.ascontiguousarray(np.broadcast_to(np.repeat(ld, HD), (P, D))),
        "wg1": rows(n["L0_attn_Wg1"]),
        "wg2": np.ascontiguousarray(n["L0_attn_Wg2"]),
        "norm_w": np.ascontiguousarray(n["L0_attn_norm_w"].reshape(KD, P).T),
        "w13a": grouped(n["L0_ffn_W1"].T, n["L0_ffn_W3"].T),
        "selectors": sel,
        "wbc": rows(np.concatenate([wb, wb, wb, wbc[:, :RK // 2], wc, wc, wc, wbc[:, RK // 2:RK]], axis=1))
        .reshape(P, KD, 2, P),
        "wdt": np.ascontiguousarray(n["L1_attn_W_dt"].T),
        "scan_feat": np.concatenate([n["L1_attn_b_dt"].reshape(KD, P).T, n["L1_attn_D_param"].reshape(KD, P).T,
                                     rows(n["L1_attn_A_log"]).reshape(P, KD * NS)], axis=1),
        "w13b": grouped(n["L1_ffn_w_gate_up"][:HID].T, n["L1_ffn_w_gate_up"][HID:].T),
        "w2b": rows(n["L1_ffn_w_down"].T).reshape(P, NG, HC * D),
    }
    nc = bacc.Bacc("TRN2", target_bir_lowering=False, num_devices=1)
    args = [nc.dram_tensor(f"in_{k}", a.shape, mybir.dt.from_np(a.dtype), kind="ExternalInput").ap()
            for k, a in arrays.items()]
    out = nc.dram_tensor("out_t", (P, KD, TOK), F32, kind="ExternalOutput").ap()
    program(nc, *args, out)
    r = run_bass_kernel_spmd(nc, [{f"in_{k}": a for k, a in arrays.items()}], core_ids=[0])
    got = r.results[0]["out_t"]
    return np.ascontiguousarray(got.transpose(2, 1, 0)).reshape(BATCH, SEQ, D)
```

```python
from contextlib import ExitStack

import concourse.bass as bass
from concourse import mybir

F32 = mybir.dt.float32
F32R = mybir.dt.float32r
BF16 = mybir.dt.bfloat16
I32 = mybir.dt.int32
ALU = mybir.AluOpType
ACT = mybir.ActivationFunctionType

P = 128
D = 512
KD = D // P
BATCH, SEQ = 2, 1024
TOK = BATCH * SEQ
TT = 512
NT = TOK // TT
TILES_PER_SEQ = SEQ // TT
HID = 2048
NH, HD = 16, 32
HPT = P // HD
CH = 128
CPT = TT // CH
NS = 32
RK = 64
EPS = 1e-5
LOG_EXP = "natural_log_exp_and_others"
GW = 256
NG = HID // GW
HC = GW // P
NC = HID // P
SW = 64
NSL = D // SW

C_ID, C_MEAN, C_HEAD, C_HAD, C_DIFF, C_MASK, C_POS, C_BD = (i * P for i in range(8))
C_REV = 8 * P
C_M1, C_M2, C_EPS = C_REV + 1, C_REV + 2, C_REV + 3
CW = C_EPS + 1


class Prog:

    def __init__(self, nc, ctx):
        self.nc, self.ctx = nc, ctx

    def sb(self, name, shape, dt=F32):
        return self.ctx.enter_context(self.nc.sbuf_tensor(name, shape, dt))

    def ps(self, name, shape, dt=F32):
        return self.ctx.enter_context(self.nc.psum_tensor(name, shape, dt))

    def sem(self, name):
        return self.nc.alloc_semaphore(name)


def three_passes(pe, out, w_hi, w_lo, x_hi, x_lo, first, last):
    pe.matmul(out, w_hi, x_hi, start=first, stop=False)
    pe.matmul(out, w_hi, x_lo, start=False, stop=False)
    return pe.matmul(out, w_lo, x_hi, start=False, stop=last)


def attention_phase(nc, const, x, cn, x_dram, aw_d, ld_tok, ld_feat, ld_cols, wg1_d, wg2_d, nw_d, w2n, w2h):
    with ExitStack() as ctx:
        p = Prog(nc, ctx)
        aw_hi = p.sb("attn_w_hi", [P, 4, KD, D], F32R)
        aw_lo = p.sb("attn_w_lo", [P, 4, KD, D], F32R)
        had = [p.sb("had_a", [P, NC, SW]), p.sb("had_b", [P, NC, SW])]
        small = p.sb("attn_small", [P, NH + KD + KD + 1])
        ldt, ldf, nw = small[:, 0:NH], small[:, NH:NH + KD], small[:, NH + KD:NH + 2 * KD]
        wg1 = p.sb("wg1", [P, KD, HD])
        wg2 = p.sb("wg2", [HD, D])
        dmask = p.sb("decay_st", [P, HPT, KD, CH])
        qdec = p.sb("q_decay", [P, KD, CH])
        kdec = p.sb("k_decay", [P, D])
        cdec = p.sb("chunk_decay", [P, KD])
        xh = p.sb("attn_x_hi", [P, KD, TT], F32R)
        xl = p.sb("attn_x_lo", [P, KD, TT], F32R)
        qT = p.sb("qT", [P, KD, TT])
        kT = p.sb("kT", [P, KD, TT])
        v = p.sb("v", [P, CPT, D])
        kd = p.sb("k_decayed", [P, CPT, D])
        qd = p.sb("q_decayed", [P, KD, TT])
        live = p.sb("state_live", [P, NT], I32)
        sig = p.sb("gate_sigmoid_or_og", [P, KD, TT])
        pr = p.sb("probs", [P, HPT, KD, CH])
        g1 = p.sb("g1", [HD, TT])
        st = p.sb("state", [P, KD, CH])
        um = p.sb("state_update", [P, KD, CH])
        sd = p.sb("head_rstd", [P, 2, TT])
        sq = pr[:, :, :, :].rearrange("p a b c -> p a (b c)")
        on = og = sig
        raws = [kd, pr[:, :, :, :].rearrange("p a b c -> p a (b c)")]
        onh, onl = xh, xl

        scores = p.ps("scores", [P, HPT, KD, CH])
        o_ps = p.ps("o_ps", [P, KD, CH])
        u_ps = p.ps("u_ps", [P, KD, CH])
        proj = p.ps("proj", [P, 2, TT])
        g1_ps = o_ps[0:HD, :, :].rearrange("p m c -> p (m c)")

        s_sm, s_const, s_aw = p.sem("attn_small_in"), p.sem("const_in"), [p.sem(f"attn_w{i}_in") for i in range(4)]
        s_x = [p.sem(f"x_in{t}") for t in range(NT)]
        s_wh, s_wl = p.sem("attn_w_hi_ready"), p.sem("attn_w_lo_ready")
        s_w2, s_bf, s_had, s_w2h = (p.sem(n) for n in ("w2_in", "butterflies", "w2_transformed", "w2h_stored"))
        s_dexp, s_dm = p.sem("decay_exp"), p.sem("decay_masked")
        s_xh, s_xl = p.sem("attn_xh"), p.sem("attn_xl")
        s_pj = p.sem("proj_done")
        s_at, s_dt = p.sem("proj_taken_by_act"), p.sem("proj_taken_by_dve")
        s_g1p, s_g1 = p.sem("g1_product"), p.sem("g1_ready")
        s_qd = p.sem("qd_ready")
        s_sc, s_pr = p.sem("scores_done"), p.sem("probs_ready")
        s_o, s_og = p.sem("o_done"), p.sem("og_ready")
        s_u, s_um, s_us, s_st = (p.sem(n) for n in ("update_done", "update_masked", "state_scaled", "state_ready"))
        s_sq, s_sd, s_on = (p.sem(n) for n in ("squares", "head_rstd_ready", "on_ready"))
        s_zero, s_go = p.sem("attn_cleared"), p.sem("attn_go_pool")
        s_oh, s_ol = p.sem("on_hi"), p.sem("on_lo")

        s_x0 = [p.sem(f"x_in0_piece{k}") for k in range(KD)]
        s_w0 = [p.sem(f"attn_w0_in_piece{k}") for k in range(KD)]
        p_xh, p_xl, p_wh, p_wl, p_sq, p_oh, p_ol = (p.sem(f"attn_{n}_piece") for n in (
            "xh", "xl", "w_hi", "w_lo", "squares", "on_hi", "on_lo"))

        def by_piece(k, whole, count, piece):
            return (whole, count) if k == KD - 1 else (piece, k + 1)

        FIRST = (["q"] * KD + ["k"] * KD + ["had0"] * 2 + ["v"] * CPT + ["gate"] * KD + ["had1"] * 2
                 + ["kT"] * CPT)
        NEXT = (["q"] * KD + ["norm"] * KD + ["k"] * KD + ["had0"] * 2 + ["v"] * CPT + ["gate"] * KD
                + ["wo"] * KD + ["had1"] * 2 + ["kT"] * CPT)
        TAIL = ["norm"] * KD + ["wo"] * KD
        STAGES = NC.bit_length() - 1
        BF = 2 * STAGES
        assert STAGES % 2 == 0 and NSL == 2 * NT

        def by_dve(items):
            return sum(n in ("kT", "wo") for n in items)
        CREDITS = 2

        class Round:

            def __init__(self, prev, items):
                self.prev, self.t, self.items = prev, prev + 1, items
                first = items is FIRST
                self.base = 0 if first else len(NEXT) * prev + len(FIRST)
                self.base_d = 0 if first else by_dve(NEXT) * prev + by_dve(FIRST)
                self.base_a = 0 if first else (len(NEXT) - by_dve(NEXT)) * prev + len(FIRST) - by_dve(FIRST)

            def at(self, name):
                return self.items.index(name)

            def done(self, name, m):
                return self.base + self.at(name) + m + 1

            def taken(self, i):
                n = by_dve(self.items[:i + 1])
                if by_dve(self.items[i:i + 1]):
                    return s_dt, self.base_d + n + CREDITS
                return s_at, self.base_a + i + 1 - n

            def out(self, name, m):
                return self.taken(self.at(name) + m)

        def rounds(eng, body):
            body(Round(-1, FIRST))
            with eng.Fori(0, NT - 1) as prev:
                body(Round(prev, NEXT))
            body(Round(NT - 1, TAIL))

        with nc.Block() as block:
            @block.sync
            def _(sp):
                def load_x(t):
                    sp.dma_start(x[:, :, t * TT:(t + 1) * TT], x_dram[:, :, t * TT:(t + 1) * TT]).then_inc(s_x[t], 16)

                def load_slice(j):
                    sp.dma_start(had[0][:, :, :].rearrange("p c d -> p (c d)"), w2n[:, j, :]).then_inc(s_w2, 16)

                def load_w(i):
                    if i >= 2:
                        sp.wait_ge(s_wl, i - 1)
                    sp.dma_start(raws[i % 2][:, :, :], aw_d[i]).then_inc(s_aw[i], 16)

                for k in range(KD):
                    sp.dma_start(x[:, k, 0:TT], x_dram[:, k, 0:TT]).then_inc(s_x0[k], 16)
                    sp.dma_start(raws[0][:, k, :], aw_d[0][:, k, :]).then_inc(s_w0[k], 16)
                load_w(1)
                load_slice(0)
                sp.dma_start(const[:, :], cn).then_inc(s_const, 16)
                load_w(2)
                sp.dma_start(ldt, ld_tok).then_inc(s_sm, 16)
                sp.dma_start(ldf, ld_feat).then_inc(s_sm, 16)
                sp.dma_start(nw, nw_d).then_inc(s_sm, 16)
                sp.dma_start(kdec[:, :], ld_cols).then_inc(s_sm, 16)
                sp.dma_start(wg1[:, :, :], wg1_d).then_inc(s_sm, 16)
                sp.dma_start(wg2[:, :], wg2_d).then_inc(s_sm, 16)
                load_w(3)
                for t in range(1, NT):
                    load_x(t)

                def body(rd):
                    if rd.items is TAIL:
                        return
                    for i in range(2):
                        j = 2 * rd.t + i
                        if i:
                            sp.wait_ge(s_pj, rd.done("had0", 1))
                        elif rd.items is NEXT:
                            sp.wait_ge(s_pj, rd.base - CPT)
                        if i or rd.items is NEXT:
                            load_slice(j)
                        sp.wait_ge(s_had, 2 * j + 2)
                        sp.dma_start(w2h[:, :, bass.ts(j, SW)], had[1][:, :, :]).then_inc(s_w2h, 16)
                rounds(sp, body)
                sp.wait_ge(s_w2h, 16 * NSL)

            @block.tensor
            def _(pe):
                def body(rd):
                    t, items = rd.t, rd.items

                    def bank(i):
                        if i < 2:
                            pe.wait_ge(s_dt, rd.base_d + i - 1 + CREDITS)
                        else:
                            pe.wait_ge(*rd.taken(i - 2))
                        return proj[:, i % 2]

                    def project(name, w, m, hi, lo, ready=None):
                        out = bank(rd.at(name) + m)
                        for k in range(KD):
                            if ready is not None:
                                for sem, value in ready(k):
                                    pe.wait_ge(sem, value)
                            mm = three_passes(pe, out, aw_hi[:, w, k, m * P:(m + 1) * P],
                                              aw_lo[:, w, k, m * P:(m + 1) * P],
                                              hi[:, k, :], lo[:, k, :], k == 0, k == KD - 1)
                        mm.then_inc(s_pj, 1)

                    def norms():
                        if items is not TAIL:
                            pe.wait_ge(s_sq, t)
                        for m in range(KD):
                            if items is TAIL:
                                pe.wait_ge(*by_piece(m, s_sq, NT, p_sq))
                            out = bank(rd.at("norm") + m)
                            pe.matmul(out, const[:, C_HEAD:C_HEAD + P], sq[:, m, :]).then_inc(s_pj, 1)

                    def outputs():
                        if items is not TAIL:
                            pe.wait_ge(s_ol, t)
                        for m in range(KD):
                            project("wo", 3, m, onh, onl,
                                    (lambda k: [by_piece(k, s_ol, NT, p_ol)]) if items is TAIL and m == 0 else None)

                    def transform(i):
                        pe.wait_ge(s_bf, BF * (2 * t + i) + BF)
                        for half in range(2):
                            out = bank(rd.at(f"had{i}") + half)
                            for c in range(NC // 2):
                                mm = pe.matmul(out[:, c * SW:(c + 1) * SW], const[:, C_HAD:C_HAD + P],
                                               had[0][:, half * (NC // 2) + c, :])
                            mm.then_inc(s_pj, 1)

                    if items is TAIL:
                        norms()
                        outputs()
                        return
                    if items is NEXT:
                        pe.wait_ge(s_xl, t + 1)
                    for m in range(KD):
                        project("q", 0, m, xh, xl,
                                (lambda k: [by_piece(k, s_xl, 1, p_xl), by_piece(k, s_wl, 1, p_wl)])
                                if items is FIRST and m == 0 else None)
                    if items is NEXT:
                        norms()
                    if items is FIRST:
                        pe.wait_ge(s_wl, 2)
                    for m in range(KD):
                        project("k", 1, m, xh, xl)
                    if items is FIRST:
                        pe.wait_ge(s_const, 16)
                    transform(0)
                    if items is FIRST:
                        pe.wait_ge(s_wl, 3)
                    for c in range(CPT):
                        out = bank(rd.at("v") + c)
                        cs = slice(c * CH, (c + 1) * CH)
                        for k in range(KD):
                            mm = three_passes(pe, out, xh[:, k, cs], xl[:, k, cs],
                                              aw_hi[:, 2, k, :], aw_lo[:, 2, k, :], k == 0, k == KD - 1)
                        mm.then_inc(s_pj, 1)
                    if items is NEXT:
                        pe.wait_ge(s_og, CPT * t)
                    else:
                        pe.wait_ge(s_sm, 96)
                    for k in range(KD):
                        mm = pe.matmul(g1_ps, wg1[:, k, :], x[:, k, bass.ts(t, TT)],
                                       start=(k == 0), stop=(k == KD - 1))
                    mm.then_inc(s_g1p, 1)
                    pe.wait_ge(s_g1, t + 1)
                    for m in range(KD):
                        out = bank(rd.at("gate") + m)
                        pe.matmul(out, wg2[:, m * P:(m + 1) * P], g1[:, :]).then_inc(s_pj, 1)
                    if items is NEXT:
                        outputs()
                    transform(1)
                    pe.wait_ge(*rd.out("v", CPT - 1))
                    for c in range(CPT):
                        out = bank(rd.at("kT") + c)
                        for m in range(KD):
                            mm = pe.transpose(out[:, m * P:(m + 1) * P], kT[:, m, c * CH:(c + 1) * CH],
                                              const[:, C_ID:C_ID + P])
                        mm.then_inc(s_pj, 1)
                    for c in range(CPT):
                        n = CPT * t + c
                        cs = slice(c * CH, (c + 1) * CH)
                        if not (items is FIRST and c == 0):
                            pe.wait_ge(s_pr, HPT * n)
                        for m in range(KD):
                            for j in range(HPT):
                                r = slice(j * HD, (j + 1) * HD)
                                mm = pe.matmul(scores[:, j, m, :], kT[r, m, cs], qT[r, m, cs])
                                if m == KD - 1:
                                    mm.then_inc(s_sc, 1)
                        pe.wait_ge(s_st, n + t + 1)
                        pe.wait_ge(s_qd, t + 1)
                        if not (items is FIRST and c == 0):
                            pe.wait_ge(s_og, n)
                        for m in range(KD):
                            pe.matmul(o_ps[:, m, :], st[:, m, :], qd[:, m, cs],
                                      start=(m == 0), stop=(m == KD - 1), skip_group_check=True)
                        pe.wait_ge(*rd.out("kT", c))
                        if not (items is FIRST and c == 0):
                            pe.wait_ge(s_um, n)
                        for m in range(KD):
                            mm = pe.matmul(u_ps[:, m, :], kd[:, c, m * P:(m + 1) * P], v[:, c, m * P:(m + 1) * P])
                        mm.then_inc(s_u, 1)
                        for j in range(HPT):
                            pe.wait_ge(s_pr, HPT * n + j + 1)
                            for m in range(KD):
                                h = m * HPT + j
                                mm = pe.matmul(o_ps[j * HD:(j + 1) * HD, m, :], v[:, c, h * HD:(h + 1) * HD],
                                               pr[:, j, m, :], start=False, stop=True, skip_group_check=True,
                                               tile_position=(0, j * HD))
                        mm.then_inc(s_o, 1)

                rounds(pe, body)

            @block.scalar
            def _(act):
                def weight_high(i):
                    act.wait_ge(s_aw[i], 16)
                    act.copy(aw_hi[:, i], raws[i % 2][:, :, :]).then_inc(s_wh, 1)

                def decays():
                    act.wait_ge(s_sm, 96)
                    act.wait_ge(s_const, 16)
                    for j in range(HPT):
                        for m in range(KD):
                            h = m * HPT + j
                            act.activation(dmask[:, j, m, :], const[:, C_DIFF:C_DIFF + P], ACT.Exp,
                                           scale=ldt[:, h:h + 1]).then_inc(s_dexp, 1)
                    for m in range(KD):
                        act.activation(qdec[:, m, :], const[:, C_POS:C_POS + P], ACT.Exp,
                                       scale=ldf[:, m:m + 1]).then_inc(s_dexp, 1)
                    act.activation(kdec[:, :], kdec[:, :], ACT.Exp,
                                   scale=const[:, C_REV:C_REV + 1]).then_inc(s_dexp, 1)
                    act.activation(cdec[:, :], ldf, ACT.Exp, scale=float(CH)).then_inc(s_dexp, 1)

                def body(rd):
                    t, items = rd.t, rd.items

                    def take(name, out, f):
                        for m in range(KD):
                            act.wait_ge(s_pj, rd.done(name, m))
                            act.activation(out[:, m, :], proj[:, (rd.at(name) + m) % 2], f).then_inc(s_at, 1)

                    def head_rstd():
                        act.preload_act_table_set(LOG_EXP)
                        if items is TAIL:
                            for m in range(KD):
                                act.wait_ge(s_pj, rd.done("norm", m))
                                act.activation(qT[:, m], proj[:, (rd.at("norm") + m) % 2], ACT.Ln,
                                               bias=const[:, C_EPS:C_EPS + 1]).then_inc(s_at, 1)
                            for m in range(KD):
                                act.wait_ge(*rd.out("norm", m))
                                act.activation(qT[:, m], qT[:, m], ACT.Exp, scale=-0.5).then_inc(s_sd, 1)
                            return
                        for pair in range(0, KD, 2):
                            for m in range(pair, pair + 2):
                                act.wait_ge(s_pj, rd.done("norm", m))
                                act.wait_ge(s_on, KD * rd.prev + max(m - 1, 0) + 1)
                                act.activation(sd[:, m % 2], proj[:, (rd.at("norm") + m) % 2], ACT.Ln,
                                               bias=const[:, C_EPS:C_EPS + 1]).then_inc(s_at, 1)
                            for m in range(pair, pair + 2):
                                act.wait_ge(*rd.out("norm", m))
                                act.activation(sd[:, m % 2], sd[:, m % 2], ACT.Exp, scale=-0.5).then_inc(s_sd, 1)

                    def high_of_normed():
                        if items is TAIL:
                            act.wait_ge(s_pj, rd.base)
                            for k in range(KD):
                                act.wait_ge(s_on, KD * rd.prev + k + 2)
                                act.copy(onh[:, k], on[:, k]).then_inc(by_piece(k, s_oh, NT, p_oh)[0], 1)
                            return
                        act.wait_ge(s_on, KD * t + 1)
                        act.wait_ge(s_pj, rd.done("v", CPT - 1))
                        act.copy(onh[:, :, :], on[:, :, :]).then_inc(s_oh, 1)

                    def take_transformed(i):
                        for half in range(2):
                            act.wait_ge(s_pj, rd.done(f"had{i}", half))
                            act.mul(had[1][:, half * (NC // 2):(half + 1) * (NC // 2), :],
                                    proj[:, (rd.at(f"had{i}") + half) % 2].rearrange("p (c d) -> p c d", c=NC // 2),
                                    float(HID) ** -0.5).then_inc(s_at, 1)
                            act.wait_ge(*rd.out(f"had{i}", half))
                            act.sem_inc(s_had, 1)

                    if items is FIRST:
                        for k in range(KD):
                            act.wait_ge(s_x0[k], 16)
                            act.copy(xh[:, k], x[:, k, 0:TT]).then_inc(by_piece(k, s_xh, 1, p_xh)[0], 1)
                            act.wait_ge(s_w0[k], 16)
                            act.copy(aw_hi[:, 0, k], raws[0][:, k]).then_inc(by_piece(k, s_wh, 1, p_wh)[0], 1)
                    if items is NEXT:
                        act.wait_ge(s_pj, rd.base - CPT)
                        act.copy(xh[:, :, :], x[:, :, bass.ts(t, TT)]).then_inc(s_xh, 1)
                    if items is not FIRST:
                        act.wait_ge(s_og, CPT * t)
                    if items is NEXT:
                        act.activation(sq[:, :, :], og[:, :, :], ACT.Square).then_inc(s_sq, 1)
                    if items is TAIL:
                        for k in range(KD):
                            act.activation(sq[:, k], og[:, k], ACT.Square).then_inc(by_piece(k, s_sq, NT, p_sq)[0], 1)
                    if items is TAIL:
                        head_rstd()
                        high_of_normed()
                        return
                    if items is FIRST:
                        weight_high(1)
                    take("q", qT, ACT.Silu)
                    if items is FIRST:
                        weight_high(2)
                    if items is NEXT:
                        head_rstd()
                    take("k", kT, ACT.Silu)
                    if items is FIRST:
                        weight_high(3)
                    take_transformed(0)
                    take("v", v, ACT.Silu)
                    if items is NEXT:
                        high_of_normed()
                    act.wait_ge(s_g1p, t + 1)
                    act.copy(g1[:, :], g1_ps).then_inc(s_g1, 1)
                    if items is NEXT:
                        act.wait_ge(s_ol, t)
                    take("gate", sig, ACT.Sigmoid)
                    if items is FIRST:
                        decays()
                        for i in range(1, NT):
                            act.wait_ge(s_x[i], 16)
                    take_transformed(1)

                rounds(act, body)

            @block.gpsimd
            def _(pool):
                def butterflies(j):
                    pool.wait_ge(s_w2, 16 * j + 16)
                    if not isinstance(j, int) or j:
                        pool.wait_ge(s_w2h, 16 * j)
                    for s in range(STAGES):
                        h = 1 << s
                        src = had[s % 2][:, :, :].rearrange("p (g two h) d -> p g two (h d)", two=2, h=h)
                        dst = had[(s + 1) % 2][:, :, :].rearrange("p (g two h) d -> p g two (h d)", two=2, h=h)
                        if s:
                            pool.wait_ge(s_bf, BF * j + 2 * s)
                        pool.tensor_tensor(dst[:, :, 0], src[:, :, 0], src[:, :, 1], ALU.add).then_inc(s_bf, 1)
                        pool.tensor_tensor(dst[:, :, 1], src[:, :, 0], src[:, :, 1], ALU.subtract).then_inc(s_bf, 1)

                butterflies(0)
                butterflies(1)
                with pool.Fori(0, NT - 1) as prev:
                    t = prev + 1
                    pool.wait_ge(s_xh, t + 1)
                    pool.sem_inc(s_go, 1)
                    pool.tensor_tensor(xl[:, :, :], x[:, :, bass.ts(t, TT)], xh[:, :, :].bitcast(F32),
                                       ALU.subtract).then_inc(s_xl, 1)
                    butterflies(2 * t)
                    butterflies(2 * t + 1)

            @block.vector
            def _(dve):
                dve.sem_inc(s_dt, CREDITS)
                dve.sem_inc(s_on, 1)
                dve.memset(st[:, :, :], 0.0).then_inc(s_zero, 1)
                dve.memset(live[:, :], -1).then_inc(s_zero, 1)
                dve.wait_ge(s_zero, 2)
                for b in range(BATCH):
                    dve.memset(live[:, b * TILES_PER_SEQ:b * TILES_PER_SEQ + 1], 0).then_inc(s_zero, 1)
                for k in range(KD):
                    dve.wait_ge(*by_piece(k, s_xh, 1, p_xh))
                    dve.tensor_tensor(xl[:, k], x[:, k, 0:TT], xh[:, k].bitcast(F32), ALU.subtract)\
                       .then_inc(by_piece(k, s_xl, 1, p_xl)[0], 1)
                    dve.wait_ge(*by_piece(k, s_wh, 1, p_wh))
                    dve.tensor_tensor(aw_lo[:, 0, k], raws[0][:, k], aw_hi[:, 0, k].bitcast(F32), ALU.subtract)\
                       .then_inc(by_piece(k, s_wl, 1, p_wl)[0], 1)
                for i in range(1, 4):
                    dve.wait_ge(s_wh, i + 1)
                    dve.tensor_tensor(aw_lo[:, i], raws[i % 2][:, :, :], aw_hi[:, i].bitcast(F32), ALU.subtract).then_inc(s_wl, 1)
                dve.wait_ge(s_dexp, HPT * KD + KD + 2)
                dve.tensor_tensor(dmask[:, :, :, :].rearrange("p a b c -> p (a b) c"),
                                  dmask[:, :, :, :].rearrange("p a b c -> p (a b) c"),
                                  const[:, C_MASK:C_MASK + P].unsqueeze(1).to_broadcast([P, NH, CH]),
                                  ALU.mult).then_inc(s_dm, 1)
                dve.wait_ge(s_dm, 1)
                dve.wait_ge(s_wl, 4)
                dve.wait_ge(s_zero, 2 + BATCH)

                def body(rd):
                    t, items = rd.t, rd.items
                    if items is not FIRST:
                        dve.wait_ge(s_og, CPT * t)
                        for m in range(KD):
                            dve.wait_ge(s_sd, KD * rd.prev + m + 1)
                            rstd = qT[:, m] if items is TAIL else sd[:, m % 2]
                            dve.scalar_tensor_tensor(out=on[:, m, :], in0=og[:, m, :], scalar=nw[:, m:m + 1],
                                                     in1=rstd, op0=ALU.mult, op1=ALU.mult).then_inc(s_on, 1)
                        if items is TAIL:
                            for k in range(KD):
                                dve.wait_ge(*by_piece(k, s_oh, NT, p_oh))
                                dve.tensor_tensor(onl[:, k], on[:, k], onh[:, k].bitcast(F32), ALU.subtract)\
                                   .then_inc(by_piece(k, s_ol, NT, p_ol)[0], 1)
                        else:
                            dve.wait_ge(s_oh, t)
                            dve.tensor_tensor(onl[:, :, :], on[:, :, :], onh[:, :, :].bitcast(F32),
                                              ALU.subtract).then_inc(s_ol, 1)
                        for m in range(KD):
                            dve.wait_ge(s_pj, rd.done("wo", m))
                            xt = x[:, m, bass.ts(rd.prev, TT)]
                            dve.tensor_tensor(xt, xt, proj[:, (rd.at("wo") + m) % 2], ALU.add).then_inc(s_dt, 1)
                    if items is TAIL:
                        return
                    dve.wait_ge(*rd.out("q", KD - 1))
                    dve.tensor_tensor(qd[:, :, :].rearrange("p m (c i) -> p m c i", c=CPT),
                                      qT[:, :, :].rearrange("p m (c i) -> p m c i", c=CPT),
                                      qdec[:, :, :].unsqueeze(2).to_broadcast([P, KD, CPT, CH]),
                                      ALU.mult).then_inc(s_qd, 1)
                    if items is NEXT:
                        dve.wait_ge(s_st, (CPT + 1) * t)
                    dve.tensor_tensor(st[:, :, :].rearrange("p m c -> p (m c)").bitcast(I32),
                                      st[:, :, :].rearrange("p m c -> p (m c)").bitcast(I32),
                                      live[:, bass.ds(t, 1)].to_broadcast([P, KD * CH]),
                                      ALU.bitwise_and).then_inc(s_st, 1)
                    for c in range(CPT):
                        dve.wait_ge(s_pj, rd.done("kT", c))
                        dve.tensor_tensor(kd[:, c, :], proj[:, (rd.at("kT") + c) % 2], kdec[:, :], ALU.mult)\
                           .then_inc(s_dt, 1)
                    dve.wait_ge(s_st, (CPT + 1) * t + 1)
                    for c in range(CPT):
                        n = CPT * t + c
                        for j in range(HPT):
                            dve.wait_ge(s_sc, HPT * n + j + 1)
                            dve.tensor_tensor(pr[:, j], scores[:, j], dmask[:, j], ALU.mult).then_inc(s_pr, 1)
                        dve.wait_ge(s_u, n + 1)
                        dve.tensor_tensor(um[:, :, :], u_ps[:, :, :],
                                          const[:, C_BD:C_BD + P].unsqueeze(1).to_broadcast([P, KD, CH]),
                                          ALU.mult).then_inc(s_um, 1)
                        dve.tensor_tensor(st[:, :, :], st[:, :, :],
                                          cdec[:, :].unsqueeze(2).to_broadcast([P, KD, CH]),
                                          ALU.mult).then_inc(s_us, 1)
                        dve.wait_ge(s_um, n + 1)
                        dve.wait_ge(s_us, n + 1)
                        dve.tensor_tensor(st[:, :, :], st[:, :, :], um[:, :, :], ALU.add).then_inc(s_st, 1)
                        dve.wait_ge(s_o, n + 1)
                        dve.wait_ge(*rd.out("gate", KD - 1))
                        dve.tensor_tensor(og[:, :, c * CH:(c + 1) * CH], o_ps[:, :, :],
                                          sig[:, :, c * CH:(c + 1) * CH], ALU.mult).then_inc(s_og, 1)
                        dve.wait_ge(s_st, n + t + 2)

                rounds(dve, body)


def ffn_phase(nc, const, tag, x, w13_d, w2_d, out=None, early=()):
    with ExitStack() as ctx:
        p = Prog(nc, ctx)
        xh = p.sb(f"{tag}_x_hi", [P, KD, TOK], F32R)
        xl = p.sb(f"{tag}_x_lo", [P, KD, TOK], F32R)
        raw13 = p.sb(f"{tag}_w13_raw", [P, 2, KD, GW])
        raw2 = p.sb(f"{tag}_w2_raw", [P, HC, D])
        w13h = p.sb(f"{tag}_w13_hi", [P, 2, 2, KD, GW], F32R)
        w13l = p.sb(f"{tag}_w13_lo", [P, 2, 2, KD, GW], F32R)
        w2h = p.sb(f"{tag}_w2_hi", [P, 2, HC, D], F32R)
        w2l = p.sb(f"{tag}_w2_lo", [P, 2, HC, D], F32R)
        sg = p.sb(f"{tag}_silu", [P, HC, TT])
        h = p.sb(f"{tag}_h", [P, HC, TT])
        hh = p.sb(f"{tag}_h_hi", [P, HC, TT], F32R)
        hl = p.sb(f"{tag}_h_lo", [P, HC, TT], F32R)
        sq = p.sb(f"{tag}_squares", [P, KD, TT])
        xs = p.sb(f"{tag}_x_sums", [P, 2, TT])
        sd = p.sb(f"{tag}_rstd", [P, TT])
        gate = p.ps(f"{tag}_gate", [P, TT])
        up = p.ps(f"{tag}_up", [P, TT])
        y = p.ps(f"{tag}_y", [P, KD, TT])
        mean = p.ps(f"{tag}_mean", [P, TT])
        var = p.ps(f"{tag}_var", [P, TT])
        s_r13, s_r2, s_wh, s_w13l, s_w2l = (p.sem(f"{tag}_{n}") for n in (
            "w13_in", "w2_in", "w_hi", "w13_lo", "w2_lo"))
        s_gu, s_s, s_h, s_hh, s_hl, s_y, s_add = (p.sem(f"{tag}_{n}") for n in (
            "gate_up_done", "silu_done", "h_done", "h_hi", "h_lo", "y_done", "y_added"))
        s_m, s_c, s_q, s_v, s_ln, s_r, s_x, s_xh, s_xl, s_o = (p.sem(f"{tag}_{n}") for n in (
            "mean", "centred", "squares", "var", "ln_var", "rstd", "x_normed", "x_hi", "x_lo", "stored"))
        s_xp, s_xs, s_qp, s_qs = (p.sem(f"{tag}_{n}") for n in (
            "x_pair_sums", "x_sums", "square_pair_sums", "square_sums"))
        p_c, p_q, p_x, p_xh, p_xl, p_add = (p.sem(f"{tag}_{n}_piece") for n in (
            "centred", "squares", "x_normed", "x_hi", "x_lo", "y_added"))
        NQ = NT * HC
        BEFORE, AFTER = 0, NT

        def alone(i):
            return i in (BEFORE, AFTER + NT - 1)

        def by_piece(i, k, whole, piece):
            if k == KD - 1:
                return whole, i + 1
            return piece, (KD - 1) * (i > BEFORE) + k + 1

        def sums(i):
            return i - 1 if i > BEFORE else 0

        def last_added(k):
            return (s_add, NG * NT) if k == KD - 1 else (p_add, k + 1)

        def tok(t):
            return bass.ts(t, TT)

        with nc.Block() as block:
            @block.sync
            def _(sp):
                def load13(g):
                    sp.dma_start(raw13[:, :, :, :].rearrange("p a k n -> p (a k n)"), w13_d[:, g, :]).then_inc(s_r13, 16)

                def load2(g):
                    sp.dma_start(raw2[:, :, :].rearrange("p c d -> p (c d)"), w2_d[:, g, :]).then_inc(s_r2, 16)

                load13(0)
                load2(0)
                for place, source, sem in early:
                    sp.dma_start(place, source).then_inc(sem, 16)
                with sp.Fori(0, NG - 1) as before:
                    sp.wait_ge(s_w13l, before + 1)
                    load13(before + 1)
                    sp.wait_ge(s_w2l, before + 1)
                    load2(before + 1)
                if out is not None:
                    for t in range(NT - 1):
                        sp.wait_ge(s_x, AFTER + t + 1)
                        sp.dma_start(out[:, :, t * TT:(t + 1) * TT], x[:, :, t * TT:(t + 1) * TT]).then_inc(s_o, 16)
                    for k in range(KD):
                        sp.wait_ge(*by_piece(AFTER + NT - 1, k, s_x, p_x))
                        sp.dma_start(out[:, k, TOK - TT:], x[:, k, TOK - TT:]).then_inc(s_o, 16)
                    sp.wait_ge(s_o, 16 * (NT - 1 + KD))

            @block.gpsimd
            def _(pool):
                def split(g, slot):
                    pool.wait_ge(s_wh, 2 * g + 1)
                    pool.tensor_tensor(w13l[:, slot], raw13[:, :, :, :], w13h[:, slot].bitcast(F32),
                                       ALU.subtract).then_inc(s_w13l, 1)
                    pool.wait_ge(s_wh, 2 * g + 2)
                    pool.tensor_tensor(w2l[:, slot], raw2[:, :, :], w2h[:, slot].bitcast(F32),
                                       ALU.subtract).then_inc(s_w2l, 1)

                def sum_x(i, t):
                    if i >= AFTER:
                        pool.wait_ge(s_add, (NG - 1) * NT + t + 1)
                    pool.wait_ge(s_m, i)
                    pool.tensor_tensor(xs[:, :, :], x[:, 0:2, tok(t)], x[:, 2:4, tok(t)], ALU.add).then_inc(s_xp, 1)
                    pool.wait_ge(s_xp, sums(i) + 1)
                    pool.tensor_tensor(xs[:, 0], xs[:, 0], xs[:, 1], ALU.add).then_inc(s_xs, 1)

                sum_x(BEFORE + 1, 1)
                split(0, 0)
                for t in range(2, NT):
                    sum_x(BEFORE + t, t)
                split(1, 1)
                with pool.Fori(1, NG // 2) as gp:
                    split(2 * gp, 0)
                    split(2 * gp + 1, 1)
                for t in range(NT - 1):
                    sum_x(AFTER + t, t)

            @block.tensor
            def _(pe):
                def average(bank, src, tiles, ready=None):
                    for k in range(tiles):
                        if ready is not None:
                            pe.wait_ge(*ready(k))
                        mm = pe.matmul(bank[:, :], const[:, C_MEAN:C_MEAN + P], src(k),
                                       start=(k == 0), stop=(k == tiles - 1))
                    return mm

                def means(i, t):
                    if i:
                        pe.wait_ge(s_c, i)
                    if alone(i):
                        average(mean, lambda k: x[:, k, tok(t)], KD,
                                last_added if i >= AFTER else None).then_inc(s_m, 1)
                    else:
                        pe.wait_ge(s_xs, sums(i) + 1)
                        average(mean, lambda k: xs[:, k], 1).then_inc(s_m, 1)

                def variances(i):
                    if i:
                        pe.wait_ge(s_ln, i)
                    if not alone(i):
                        pe.wait_ge(s_qs, sums(i) + 1)
                    average(var, lambda k: sq[:, k, :], KD if alone(i) else 1,
                            (lambda k: by_piece(i, k, s_q, p_q)) if alone(i) else None).then_inc(s_v, 1)

                def gate_up(g, t, c, slot, pieces=False):
                    q = (g * NT + t) * HC + c
                    pe.wait_ge(s_h, q + HC)
                    for a, bank in ((0, gate), (1, up)):
                        for k in range(KD):
                            if pieces and a == 0:
                                pe.wait_ge(*by_piece(BEFORE, k, s_xl, p_xl))
                            cs = slice(c * P, (c + 1) * P)
                            mm = three_passes(pe, bank[:, :], w13h[:, slot, a, k, cs], w13l[:, slot, a, k, cs],
                                              xh[:, k, tok(t)], xl[:, k, tok(t)], k == 0, k == KD - 1)
                    mm.then_inc(s_gu, 1)

                def down(g, t, c, slot):
                    q = (g * NT + t) * HC + c
                    pe.wait_ge(s_hl, q + 1)
                    if c == 0:
                        pe.wait_ge(s_add, g * NT + t)
                    for m in range(KD):
                        ms = slice(m * P, (m + 1) * P)
                        mm = three_passes(pe, y[:, m], w2h[:, slot, c, ms], w2l[:, slot, c, ms],
                                          hh[:, c], hl[:, c], c == 0, c == HC - 1)
                    mm.then_inc(s_y, 1)

                def tile(g, t, slot, before):
                    gate_up(g, t, 0, slot)
                    down(*before)
                    gate_up(g, t, 1, slot)
                    down(g, t, 0, slot)

                def group(g, slot):
                    pe.wait_ge(s_w13l, g + 1)
                    pe.wait_ge(s_w2l, g + 1)
                    tile(g, 0, slot, (g - 1, NT - 1, HC - 1, 1 - slot))
                    with pe.Fori(1, NT) as t:
                        tile(g, t, slot, (g, t - 1, HC - 1, slot))

                def first_group():
                    means(BEFORE, 0)
                    variances(BEFORE)
                    means(BEFORE + 1, 1)
                    pe.wait_ge(s_w13l, 1)
                    for t in range(NT):
                        if t:
                            pe.wait_ge(s_xl, t + 1)
                        gate_up(0, t, 0, 0, pieces=t == 0)
                        if t < NT - 1:
                            variances(BEFORE + t + 1)
                        if t:
                            down(0, t - 1, 1, 0)
                        else:
                            pe.wait_ge(s_w2l, 1)
                        gate_up(0, t, 1, 0)
                        if t < NT - 2:
                            means(BEFORE + t + 2, t + 2)
                        down(0, t, 0, 0)

                def last_group():
                    g = NG - 1
                    pe.wait_ge(s_w13l, g + 1)
                    pe.wait_ge(s_w2l, g + 1)
                    for t in range(NT):
                        gate_up(g, t, 0, 1)
                        down(*((g, t - 1, 1, 1) if t else (g - 1, NT - 1, 1, 0)))
                        if t >= 2:
                            variances(AFTER + t - 2)
                        gate_up(g, t, 1, 1)
                        down(g, t, 0, 1)
                        if t:
                            means(AFTER + t - 1, t - 1)
                    down(g, NT - 1, 1, 1)
                    means(AFTER + NT - 1, NT - 1)
                    variances(AFTER + NT - 2)
                    variances(AFTER + NT - 1)

                first_group()
                group(1, 1)
                with pe.Fori(1, NG // 2 - 1) as gp:
                    group(2 * gp, 0)
                    group(2 * gp + 1, 1)
                group(NG - 2, 0)
                last_group()

            @block.scalar
            def _(act):
                def split(g, slot):
                    act.wait_ge(s_r13, 16 * g + 16)
                    if not isinstance(g, int) or g:
                        act.wait_ge(s_y, HC + NQ * (g - 1))
                    act.copy(w13h[:, slot], raw13[:, :, :, :]).then_inc(s_wh, 1)
                    act.wait_ge(s_r2, 16 * g + 16)
                    act.copy(w2h[:, slot], raw2[:, :, :]).then_inc(s_wh, 1)

                def square(i, t):
                    if i:
                        act.wait_ge(s_v, i)
                    if alone(i):
                        for k in range(KD):
                            act.wait_ge(*by_piece(i, k, s_c, p_c))
                            act.activation(sq[:, k], x[:, k, tok(t)], ACT.Square)\
                               .then_inc(by_piece(i, k, s_q, p_q)[0], 1)
                        return
                    act.wait_ge(s_c, i + 1)
                    act.activation(sq[:, :, :], x[:, :, tok(t)], ACT.Square).then_inc(s_q, 1)

                def rstd(i):
                    act.preload_act_table_set(LOG_EXP)
                    act.wait_ge(s_v, i + 1)
                    if i:
                        act.wait_ge(s_x, i)
                    act.activation(sd[:, :], var[:, :], ACT.Ln, bias=const[:, C_EPS:C_EPS + 1]).then_inc(s_ln, 1)
                    act.wait_ge(s_ln, i + 1)
                    act.activation(sd[:, :], sd[:, :], ACT.Exp, scale=-0.5).then_inc(s_r, 1)

                def high(t):
                    if t == 0:
                        for k in range(KD):
                            act.wait_ge(*by_piece(BEFORE, k, s_x, p_x))
                            act.copy(xh[:, k, tok(t)], x[:, k, tok(t)]).then_inc(by_piece(BEFORE, k, s_xh, p_xh)[0], 1)
                        return
                    act.wait_ge(s_x, BEFORE + t + 1)
                    act.copy(xh[:, :, tok(t)], x[:, :, tok(t)]).then_inc(s_xh, 1)

                def silu(g, t, c):
                    q = (g * NT + t) * HC + c
                    act.wait_ge(s_gu, q + 1)
                    act.wait_ge(s_h, q + 1)
                    act.activation(sg[:, c], gate[:, :], ACT.Silu).then_inc(s_s, 1)

                def h_high(g, t, c):
                    q = (g * NT + t) * HC + c
                    act.wait_ge(s_h, q + HC + 1)
                    act.wait_ge(s_y, q + 1)
                    act.copy(hh[:, c], h[:, c]).then_inc(s_hh, 1)

                def tile(g, t):
                    for c in range(HC):
                        silu(g, t, c)
                        h_high(g, t, c)

                def group(g, slot):
                    tile(g, 0)
                    split(g + 1, 1 - slot)
                    with act.Fori(1, NT) as t:
                        tile(g, t)

                square(BEFORE, 0)
                split(0, 0)
                rstd(BEFORE)
                high(0)
                square(BEFORE + 1, 1)
                for t in range(NT):
                    silu(0, t, 0)
                    h_high(0, t, 0)
                    if t < NT - 1:
                        rstd(BEFORE + t + 1)
                        high(t + 1)
                    silu(0, t, 1)
                    h_high(0, t, 1)
                    if t < NT - 2:
                        square(BEFORE + t + 2, t + 2)
                    if t == 0:
                        split(1, 1)
                group(1, 1)
                with act.Fori(1, NG // 2 - 1) as gp:
                    group(2 * gp, 0)
                    group(2 * gp + 1, 1)
                group(NG - 2, 0)
                for t in range(NT):
                    silu(NG - 1, t, 0)
                    h_high(NG - 1, t, 0)
                    if t >= 2:
                        rstd(AFTER + t - 2)
                    silu(NG - 1, t, 1)
                    h_high(NG - 1, t, 1)
                    if t:
                        square(AFTER + t - 1, t - 1)
                rstd(AFTER + NT - 2)
                square(AFTER + NT - 1, NT - 1)
                rstd(AFTER + NT - 1)

            @block.vector
            def _(dve):
                dve.sem_inc(s_h, HC)
                dve.sem_inc(s_y, HC)

                def centre(i, t):
                    dve.wait_ge(s_m, i + 1)
                    if alone(i):
                        for k in range(KD):
                            dve.tensor_tensor(x[:, k, tok(t)], x[:, k, tok(t)], mean[:, :], ALU.subtract)\
                               .then_inc(by_piece(i, k, s_c, p_c)[0], 1)
                        return
                    dve.tensor_tensor(x[:, :, tok(t)], x[:, :, tok(t)],
                                      mean[:, :].unsqueeze(1).to_broadcast([P, KD, TT]),
                                      ALU.subtract).then_inc(s_c, 1)

                def pair_sums(i):
                    dve.wait_ge(s_q, i + 1)
                    dve.tensor_tensor(sq[:, 0:2], sq[:, 0:2], sq[:, 2:4], ALU.add).then_inc(s_qp, 1)
                    dve.wait_ge(s_qp, sums(i) + 1)
                    dve.tensor_tensor(sq[:, 0], sq[:, 0], sq[:, 1], ALU.add).then_inc(s_qs, 1)

                def scale(i, t):
                    dve.wait_ge(s_r, i + 1)
                    if alone(i):
                        for k in range(KD):
                            dve.tensor_tensor(x[:, k, tok(t)], x[:, k, tok(t)], sd[:, :], ALU.mult)\
                               .then_inc(by_piece(i, k, s_x, p_x)[0], 1)
                        return
                    dve.tensor_tensor(x[:, :, tok(t)], x[:, :, tok(t)],
                                      sd[:, :].unsqueeze(1).to_broadcast([P, KD, TT]), ALU.mult).then_inc(s_x, 1)

                def low(t):
                    if t == 0:
                        for k in range(KD):
                            dve.wait_ge(*by_piece(BEFORE, k, s_xh, p_xh))
                            dve.tensor_tensor(xl[:, k, tok(t)], x[:, k, tok(t)], xh[:, k, tok(t)].bitcast(F32),
                                              ALU.subtract).then_inc(by_piece(BEFORE, k, s_xl, p_xl)[0], 1)
                        return
                    dve.wait_ge(s_xh, t + 1)
                    dve.tensor_tensor(xl[:, :, tok(t)], x[:, :, tok(t)], xh[:, :, tok(t)].bitcast(F32),
                                      ALU.subtract).then_inc(s_xl, 1)

                def hidden(g, t, c):
                    q = (g * NT + t) * HC + c
                    dve.wait_ge(s_s, q + 1)
                    dve.tensor_tensor(h[:, c], sg[:, c], up[:, :], ALU.mult).then_inc(s_h, 1)
                    dve.wait_ge(s_h, q + HC + 1)
                    dve.wait_ge(s_hh, q + 1)
                    dve.wait_ge(s_y, q + 1)
                    dve.tensor_tensor(hl[:, c], h[:, c], hh[:, c].bitcast(F32), ALU.subtract).then_inc(s_hl, 1)

                def add(g, t):
                    dve.wait_ge(s_y, HC + (g * NT + t + 1) * HC)
                    if isinstance(g, int) and g == NG - 1 and t == NT - 1:
                        for k in range(KD):
                            dve.tensor_tensor(x[:, k, tok(t)], x[:, k, tok(t)], y[:, k], ALU.add)\
                               .then_inc(last_added(k)[0], 1)
                        return
                    dve.tensor_tensor(x[:, :, tok(t)], x[:, :, tok(t)], y[:, :, :], ALU.add).then_inc(s_add, 1)

                def tile(g, t, before):
                    hidden(g, t, 0)
                    add(*before)
                    hidden(g, t, 1)

                def group(g):
                    dve.wait_ge(s_add, (g - 1) * NT + NT - 1)
                    tile(g, 0, (g - 1, NT - 1))
                    with dve.Fori(1, NT) as t:
                        tile(g, t, (g, t - 1))

                centre(BEFORE, 0)
                scale(BEFORE, 0)
                low(0)
                centre(BEFORE + 1, 1)
                pair_sums(BEFORE + 1)
                for t in range(NT):
                    hidden(0, t, 0)
                    if t < NT - 1:
                        scale(BEFORE + t + 1, t + 1)
                    if t:
                        add(0, t - 1)
                    if t < NT - 1:
                        low(t + 1)
                    hidden(0, t, 1)
                    if t < NT - 2:
                        centre(BEFORE + t + 2, t + 2)
                        pair_sums(BEFORE + t + 2)
                group(1)
                with dve.Fori(1, NG // 2 - 1) as gp:
                    group(2 * gp)
                    group(2 * gp + 1)
                group(NG - 2)
                g = NG - 1
                for t in range(NT):
                    hidden(g, t, 0)
                    add(*((g, t - 1) if t else (g - 1, NT - 1)))
                    if t >= 2:
                        scale(AFTER + t - 2, t - 2)
                    hidden(g, t, 1)
                    if t:
                        centre(AFTER + t - 1, t - 1)
                        if t == NT - 1:
                            add(g, t)
                        pair_sums(AFTER + t - 1)
                scale(AFTER + NT - 2, NT - 2)
                centre(AFTER + NT - 1, NT - 1)
                scale(AFTER + NT - 1, NT - 1)


def scan_prepare_phase(nc, const, x, s_in, wbc, wdt, feat, a, delta, du, parts):
    with ExitStack() as ctx:
        p = Prog(nc, ctx)
        bdt = feat[:, 0:KD]
        rank = p.sb("rank", [RK, 2, TT])
        soft = p.sb("soft", [P, 2, KD, TT])
        bc_hi = p.sb("bc_hi", [3 * NS, 2, 2, TT], BF16)
        bc_r = p.sb("bc_rest", [3 * NS, 2, 2, TT])
        bc = p.ps("bc_rank", [P, 2, 2, TT])
        dt = p.ps("dt", [P, KD, TT])
        s_a, s_bc, s_r, s_dt, s_ab, s_re, s_so, s_de, s_du, s_sp, s_pt = (p.sem(f"prep_{n}") for n in (
            "a", "bc_mm", "rank", "dt_mm", "abs", "relu", "soft", "delta", "du", "split", "parts"))
        s_mid, s_rest, s_dx = p.sem("prep_mid"), p.sem("prep_rest"), p.sem("prep_du_by_dve")
        RH = RK // 2

        def tiles(eng, stages):
            for i in range(NT // 2):
                for stage in stages:
                    for s in range(2):
                        stage(2 * i + s, s, 2 * i)

        with nc.Block() as block:
            @block.tensor
            def _(pe):
                pe.wait_ge(s_in, 80)

                def project(t, s, done):
                    if done:
                        pe.wait_ge(s_r, 2 * done)
                        pe.wait_ge(s_sp, 2 * done)
                    for i in range(2):
                        for k in range(KD):
                            mm = pe.matmul(bc[:, s, i], wbc[:, k, i, :], x[:, k, bass.ts(t, TT)],
                                           start=(k == 0), stop=(k == KD - 1))
                        mm.then_inc(s_bc, 1)

                def step_size(t, s, done):
                    pe.wait_ge(s_r, 2 * t + 2)
                    for m in range(KD):
                        if t:
                            pe.wait_ge(s_re, KD * (t - 1) + m + 1)
                        pe.matmul(dt[:, m], wdt[:, m * P:(m + 1) * P], rank[:, s]).then_inc(s_dt, 1)
                tiles(pe, [project, step_size])

            @block.scalar
            def _(act):
                act.preload_act_table_set(LOG_EXP)
                act.wait_ge(s_in, 80)
                act.activation(a[:, :, :], a[:, :, :], ACT.Exp).then_inc(s_a, 1)
                act.wait_ge(s_a, 1)
                act.mul(a[:, :, :], a[:, :, :], -1.0).then_inc(s_a, 1)

                def ranks(t, s, done):
                    act.wait_ge(s_bc, 2 * t + 2)
                    if done:
                        act.wait_ge(s_dt, KD * done)
                    for i in range(2):
                        act.copy(rank[i * RH:(i + 1) * RH, s], bc[P - RH:P, s, i]).then_inc(s_r, 1)

                def magnitude(t, s, done):
                    if done:
                        act.wait_ge(s_de, done)
                    for m in range(KD):
                        act.wait_ge(s_dt, KD * t + m + 1)
                        act.activation(soft[:, s, m, :], dt[:, m], ACT.Abs, bias=bdt[:, m:m + 1]).then_inc(s_ab, 1)

                def exponent(t, s, done):
                    act.wait_ge(s_ab, KD * t + KD)
                    act.activation(soft[:, s], soft[:, s], ACT.Exp, scale=-1.0).then_inc(s_so, 1)

                def logarithm(t, s, done):
                    act.wait_ge(s_so, 2 * t + 1)
                    act.activation(soft[:, s], soft[:, s], ACT.Ln, bias=1.0).then_inc(s_so, 1)
                def soft_part(t, s, done):
                    for stage in (magnitude, exponent, logarithm):
                        stage(t, s, done)
                tiles(act, [ranks, soft_part])
                act.wait_ge(s_a, 2)

            @block.vector
            def _(dve):
                def first(t, s, done):
                    dve.wait_ge(s_r, 2 * t + 2)
                    if done:
                        dve.wait_ge(s_pt, done)
                    dve.tensor_copy(bc_hi[:, s], bc[0:3 * NS, s]).then_inc(s_sp, 1)

                def first_rest(t, s, done):
                    dve.wait_ge(s_sp, 2 * done + s + 1)
                    dve.scalar_tensor_tensor(out=bc_r[:, s], in0=bc_hi[:, s], scalar=const[0:3 * NS, C_M1:C_M1 + 1],
                                             in1=bc[0:3 * NS, s], op0=ALU.mult, op1=ALU.add).then_inc(s_sp, 1)

                def second(t, s, done):
                    dve.wait_ge(s_sp, 2 * done + s + 3)
                    dve.tensor_copy(bc_hi[:, s], bc_r[:, s]).then_inc(s_mid, 1)

                def second_rest(t, s, done):
                    dve.wait_ge(s_mid, t + 1)
                    dve.scalar_tensor_tensor(out=bc_r[:, s], in0=bc_hi[:, s], scalar=const[0:3 * NS, C_M2:C_M2 + 1],
                                             in1=bc_r[:, s], op0=ALU.mult, op1=ALU.add).then_inc(s_rest, 1)

                def third(t, s, done):
                    dve.wait_ge(s_rest, t + 1)
                    dve.tensor_copy(parts[:, :, bass.ts(t, TT)], bc_r[:, s]).then_inc(s_pt, 1)

                def positive_first(t, s, done):
                    if s == 0:
                        positive(t)

                def positive_second(t, s, done):
                    if s == 1:
                        positive(t)

                def positive(t):
                    for m in range(KD):
                        dve.wait_ge(s_ab, KD * t + m + 1)
                        dve.tensor_scalar(delta[:, m, bass.ts(t, TT)], dt[:, m], bdt[:, m:m + 1], 0.0,
                                          ALU.add, ALU.max).then_inc(s_re, 1)

                def softplus_first(t, s, done):
                    if s == 0:
                        softplus(t)

                def softplus_second(t, s, done):
                    if s == 1:
                        softplus(t)

                def softplus(t):
                    dve.wait_ge(s_re, KD * t + KD)
                    dve.wait_ge(s_so, 2 * t + 2)
                    dve.tensor_tensor(delta[:, :, bass.ts(t, TT)], delta[:, :, bass.ts(t, TT)], soft[:, t % 2],
                                      ALU.add).then_inc(s_de, 1)

                def times_x(t, s, done):
                    if s == 1:
                        dve.wait_ge(s_de, t + 1)
                        dve.tensor_tensor(du[:, :, bass.ts(t, TT)], delta[:, :, bass.ts(t, TT)],
                                          x[:, :, bass.ts(t, TT)], ALU.mult).then_inc(s_dx, 1)
                tiles(dve, [first, first_rest, positive_first, second, second_rest, third,
                            softplus_first, positive_second, softplus_second, times_x])

            @block.gpsimd
            def _(pool):
                for t in range(0, NT, 2):
                    pool.wait_ge(s_de, t + 1)
                    pool.tensor_tensor(du[:, :, bass.ts(t, TT)], delta[:, :, bass.ts(t, TT)],
                                       x[:, :, bass.ts(t, TT)], ALU.mult).then_inc(s_du, 1)


def scan_phase(nc, const, x, sel, feat, a, delta, du, parts):
    HF = KD // 2
    HALVES = 2
    SEGS = BATCH * HALVES
    TPS = TILES_PER_SEQ
    Q = 4
    with ExitStack() as ctx:
        p = Prog(nc, ctx)
        dpar = feat[:, KD:2 * KD]
        bs = p.sb("b_spread", [P, 2, SEQ])
        db = p.sb("d_b", [P, Q, HF, SEQ])
        hs = p.sb("h_states", [P, 2, HF, SEQ])
        hc = p.sb("h_times_c", [P, 2, HF, SEQ])
        da = p.sb("decay", [P, HF, SEQ])
        b_ps = p.ps("b_ps", [P, SEQ])
        c_ps = p.ps("c_ps", [P, SEQ])
        y = p.ps("scan_y", [P, HF, SEQ])
        names = ("b_mm", "c_mm", "b_spread", "decay", "db", "h", "hc", "ysum", "ytmp", "yout")
        s_b, s_c, s_bs, s_da, s_db, s_h, s_hc, s_y, s_yt, s_yo = (p.sem(f"scan_{n}") for n in names)
        C_BS, C_DB, C_H, C_HC, C_Y = 1, 2, Q * HF, 2, 2

        class Step:

            def __init__(self, seg, n, known):
                self.seg, self.n, self.known = seg, n, known
                self.b, self.half = divmod(seg, HALVES)
                self.s = NS * seg + n

            def after(self, k):
                if self.known and self.n + k >= NS:
                    return Step(self.seg + 1, self.n + k - NS, True) if self.seg < SEGS - 1 else None
                return Step(self.seg, self.n + k, self.known)

        def steps(eng, seg, body):
            def some(i, known):
                for u in range(Q):
                    body(Step(seg, Q * i + u, known), u)
            some(0, True)
            with eng.Fori(1, NS // Q - 1) as i:
                some(i, False)
            some(NS // Q - 1, True)

        with nc.Block() as block:
            @block.tensor
            def _(pe):
                def spread(out, which, st):
                    for i in range(TPS):
                        mm = pe.matmul(out[:, i * TT:(i + 1) * TT], sel[:, st.n, :],
                                       parts[:, which, (TPS * st.b + i) * TT:(TPS * st.b + i + 1) * TT])
                    return mm

                def spread_b(st):
                    pe.wait_ge(s_bs, st.s + C_BS)
                    spread(b_ps, 0, st).then_inc(s_b, 1)

                def spread_c(st):
                    pe.wait_ge(s_hc, st.s + C_HC)
                    spread(c_ps, 1, st).then_inc(s_c, 1)

                def sum_states(s, u, start):
                    pe.wait_ge(s_hc, s + 1 + C_HC)
                    for f in range(HF):
                        for i in range(TPS):
                            ts = slice(i * TT, (i + 1) * TT)
                            mm = pe.matmul(y[:, f, ts], const[:, C_ID:C_ID + P], hc[:, u % 2, f, ts],
                                           start=start, stop=True, skip_group_check=True)
                    mm.then_inc(s_y, 1)

                def body(st, u):
                    spread_c(st)
                    if st.after(3):
                        spread_b(st.after(3))
                    if not (st.known and st.n == 0):
                        start = st.known and st.n == 1
                        if start:
                            pe.wait_ge(s_yo, HF * st.seg)
                        sum_states(st.s - 1, u - 1, start)

                for k in range(3):
                    spread_b(Step(0, k, True))
                for seg in range(SEGS):
                    steps(pe, seg, body)
                    sum_states(NS * (seg + 1) - 1, 1, False)

            @block.scalar
            def _(act):
                def take_b(st, u):
                    act.wait_ge(s_b, st.s + 1)
                    act.wait_ge(s_db, st.s - 1 + C_DB)
                    act.copy(bs[:, u % 2], b_ps[:, :]).then_inc(s_bs, 1)

                def decays(st, f):
                    m = HF * st.half + f
                    act.wait_ge(s_h, HF * (st.s - 1) + f + 1 + C_H)
                    act.activation(da[:, f], delta[:, m, st.b * SEQ:(st.b + 1) * SEQ], ACT.Exp,
                                   scale=a[:, m, bass.ds(st.n, 1)]).then_inc(s_da, 1)

                def body(st, u):
                    decays(st, 0)
                    if st.after(2):
                        take_b(st.after(2), u)
                    decays(st, 1)

                act.preload_act_table_set("exp_and_others")
                for k in range(2):
                    take_b(Step(0, k, True), k)
                for seg in range(SEGS):
                    steps(act, seg, body)

            @block.gpsimd
            def _(pool):
                pool.sem_inc(s_bs, C_BS)
                pool.sem_inc(s_db, C_DB)

                def body(st, u):
                    pool.wait_ge(s_bs, st.s + 1 + C_BS)
                    pool.wait_ge(s_h, HF * (st.s - Q + 1) + C_H)
                    pool.tensor_tensor(db[:, u], du[:, HF * st.half:HF * (st.half + 1), st.b * SEQ:(st.b + 1) * SEQ],
                                       bs[:, u % 2].unsqueeze(1).to_broadcast([P, HF, SEQ]),
                                       ALU.mult).then_inc(s_db, 1)

                for seg in range(SEGS):
                    steps(pool, seg, body)

            @block.vector
            def _(dve):
                dve.sem_inc(s_hc, C_HC)
                dve.sem_inc(s_h, C_H)
                dve.sem_inc(s_y, C_Y)

                def scan(st, u, f):
                    dve.wait_ge(s_da, HF * st.s + f + 1)
                    dve.tensor_tensor_scan(hs[:, u % 2, f, :], da[:, f], db[:, u, f, :], 0.0,
                                           ALU.mult, ALU.add).then_inc(s_h, 1)

                def times_c(s, u):
                    dve.wait_ge(s_h, HF * s + HF + C_H)
                    dve.wait_ge(s_c, s + 1)
                    dve.wait_ge(s_y, s - 1 + C_Y)
                    dve.tensor_tensor(hc[:, u % 2], hs[:, u % 2],
                                      c_ps[:, :].unsqueeze(1).to_broadcast([P, HF, SEQ]),
                                      ALU.mult).then_inc(s_hc, 1)

                def leave(seg):
                    b, half = divmod(seg, HALVES)
                    dve.wait_ge(s_y, NS * (seg + 1) + C_Y)
                    for f in range(HF):
                        m = HF * half + f
                        dve.scalar_tensor_tensor(out=y[:, f], in0=x[:, m, b * SEQ:(b + 1) * SEQ],
                                                 scalar=dpar[:, m:m + 1], in1=y[:, f],
                                                 op0=ALU.mult, op1=ALU.add).then_inc(s_yt, 1)
                    for f in range(HF):
                        xt = x[:, HF * half + f, b * SEQ:(b + 1) * SEQ]
                        dve.wait_ge(s_yt, HF * seg + f + 1)
                        dve.tensor_tensor(xt, xt, y[:, f], ALU.add).then_inc(s_yo, 1)

                def body(st, u):
                    dve.wait_ge(s_db, st.s + 1 + C_DB)
                    dve.wait_ge(s_hc, st.s - 1 + C_HC)
                    scan(st, u, 0)
                    if not (st.known and st.n == 0):
                        times_c(st.s - 1, u - 1)
                    scan(st, u, 1)
                    if st.known and st.n == 1 and st.seg > 0:
                        leave(st.seg - 1)

                for seg in range(SEGS):
                    steps(dve, seg, body)
                    times_c(NS * (seg + 1) - 1, 1)
                leave(SEGS - 1)


def program(nc, x_d, cn, w2n, aw, ld_tok, ld_feat, ld_cols, wg1_d, wg2_d, nw_d, w13a, sel_d, wbc_d, wdt_d,
            fp_d, w13b, w2b, out):
    w2h = nc.dram_tensor("w2_hadamard", (P, HID // P, D), F32, kind="Internal").ap()
    with ExitStack() as ctx:
        p = Prog(nc, ctx)
        const = p.sb("const", [P, CW])
        x = p.sb("x", [P, KD, TOK])
        attention_phase(nc, const, x, cn, x_d, aw, ld_tok, ld_feat, ld_cols, wg1_d, wg2_d, nw_d, w2n, w2h)
        with ExitStack() as scan:
            q = Prog(nc, scan)
            s_in = q.sem("scan_in")
            sel = q.sb("selectors", [3 * NS, NS, P], BF16)
            feat = q.sb("scan_feat", [P, 2 * KD])
            a = q.sb("a_neg", [P, KD, NS])
            wbc = q.sb("w_bc", [P, KD, 2, P])
            wdt = q.sb("w_dt", [RK, D])
            early = ((sel[:, :, :], sel_d, s_in), (wbc[:, :, :, :], wbc_d, s_in), (wdt[:, :], wdt_d, s_in),
                     (feat[:, :], fp_d[:, 0:2 * KD], s_in),
                     (a[:, :, :], fp_d[:, 2 * KD:].rearrange("p (k n) -> p k n", k=KD), s_in))
            ffn_phase(nc, const, "ffn0", x, w13a, w2h.rearrange("p (g c) d -> p g (c d)", g=NG), early=early)
            delta, du = q.sb("delta", [P, KD, TOK]), q.sb("delta_x", [P, KD, TOK])
            bc_parts = q.sb("bc_parts", [3 * NS, 2, TOK], BF16)
            scan_prepare_phase(nc, const, x, s_in, wbc, wdt, feat, a, delta, du, bc_parts)
            scan_phase(nc, const, x, sel, feat, a, delta, du, bc_parts)
        ffn_phase(nc, const, "ffn1", x, w13b, w2b, out)


def kernel(**inputs):
    import ml_dtypes
    import numpy as np

    import concourse.bacc as bacc
    from concourse.bass_utils import run_bass_kernel_spmd

    def rows(w):
        return np.ascontiguousarray(w.reshape(w.shape[0] // P, P, w.shape[1]).transpose(1, 0, 2))

    def grouped(w1t, w3t):
        both = np.stack([rows(w1t), rows(w3t)], axis=1).reshape(P, 2, KD, NG, GW)
        return np.ascontiguousarray(both.transpose(0, 3, 1, 2, 4)).reshape(P, NG, 2 * KD * GW)

    n = {k: np.asarray(v) for k, v in inputs.items()}
    f = np.float32
    i = np.arange(P)
    const = np.zeros((P, CW), f)
    const[:, C_ID:C_ID + P] = np.eye(P)
    const[:, C_MEAN:C_MEAN + P] = 1.0 / D
    const[:, C_HEAD:C_HEAD + P] = (i[:, None] // HD == i[None] // HD) / HD
    had = np.ones((1, 1))
    while len(had) < P:
        had = np.block([[had, had], [had, -had]])
    const[:, C_HAD:C_HAD + P] = had
    const[:, C_DIFF:C_DIFF + P] = np.maximum(i[None] - i[:, None], 0)
    const[:, C_MASK:C_MASK + P] = i[None] >= i[:, None]
    const[:, C_POS:C_POS + P] = i[None] + 1
    const[:, C_BD:C_BD + P] = i[:, None] // HD == i[None] // HD
    const[:, C_REV] = CH - 1 - i
    const[:, C_M1] = -(i >= NS).astype(f)
    const[:, C_M2] = -(i >= 2 * NS).astype(f)
    const[:, C_EPS] = EPS
    sel = np.zeros((3 * NS, NS, P), ml_dtypes.bfloat16)
    for s in range(NS):
        sel[s::NS, s] = 1
    ld = n["L0_attn_log_decay"]
    wbc = n["L1_attn_W_bc"].T
    wb, wc = wbc[:, RK:RK + NS], wbc[:, RK + NS:]
    arrays = {
        "x_t": rows(n["L0_attn_x"].reshape(TOK, D).T),
        "const": const,
        "w2a_t": np.ascontiguousarray(rows(n["L0_ffn_W2"].T).reshape(P, NC, NSL, SW).transpose(0, 2, 1, 3))
        .reshape(P, NSL, NC * SW),
        "attn_w": np.stack([rows(n[f"L0_attn_{w}"]) for w in ("Wq", "Wk", "Wv", "Wo")]),
        "ld_tok": np.ascontiguousarray(np.broadcast_to(ld, (P, NH))),
        "ld_feat": np.ascontiguousarray(np.repeat(ld, HD).reshape(KD, P).T),
        "ld_cols": np.ascontiguousarray(np.broadcast_to(np.repeat(ld, HD), (P, D))),
        "wg1": rows(n["L0_attn_Wg1"]),
        "wg2": np.ascontiguousarray(n["L0_attn_Wg2"]),
        "norm_w": np.ascontiguousarray(n["L0_attn_norm_w"].reshape(KD, P).T),
        "w13a": grouped(n["L0_ffn_W1"].T, n["L0_ffn_W3"].T),
        "selectors": sel,
        "wbc": rows(np.concatenate([wb, wb, wb, wbc[:, :RK // 2], wc, wc, wc, wbc[:, RK // 2:RK]], axis=1))
        .reshape(P, KD, 2, P),
        "wdt": np.ascontiguousarray(n["L1_attn_W_dt"].T),
        "scan_feat": np.concatenate([n["L1_attn_b_dt"].reshape(KD, P).T, n["L1_attn_D_param"].reshape(KD, P).T,
                                     rows(n["L1_attn_A_log"]).reshape(P, KD * NS)], axis=1),
        "w13b": grouped(n["L1_ffn_w_gate_up"][:HID].T, n["L1_ffn_w_gate_up"][HID:].T),
        "w2b": rows(n["L1_ffn_w_down"].T).reshape(P, NG, HC * D),
    }
    nc = bacc.Bacc("TRN2", target_bir_lowering=False, num_devices=1)
    args = [nc.dram_tensor(f"in_{k}", a.shape, mybir.dt.from_np(a.dtype), kind="ExternalInput").ap()
            for k, a in arrays.items()]
    out = nc.dram_tensor("out_t", (P, KD, TOK), F32, kind="ExternalOutput").ap()
    program(nc, *args, out)
    r = run_bass_kernel_spmd(nc, [{f"in_{k}": a for k, a in arrays.items()}], core_ids=[0])
    got = r.results[0]["out_t"]
    return np.ascontiguousarray(got.transpose(2, 1, 0)).reshape(BATCH, SEQ, D)
```
